# Optimizing a Trainium2 kernel written in Bass

```python
import numpy as np
import jax
import jax.numpy as jnp

def _softmax(x, axis=-1):
    return jax.nn.softmax(x, axis=axis)

def _gelu(x):
    return jax.nn.gelu(x, approximate=True)

def _silu(x):
    return jax.nn.silu(x)

def _sigmoid(x):
    return jax.nn.sigmoid(x)

def _layernorm(x, axis=-1, eps=1e-05):
    m = jnp.mean(x, axis=axis, keepdims=True)
    v = jnp.var(x, axis=axis, keepdims=True)
    return (x - m) / jnp.sqrt(v + eps)

def _scatter_add(tgt, idx, src, axis=0):
    return tgt.at[idx].add(src)

def _segment_sum(src, seg, n):
    return jax.ops.segment_sum(src, seg, n)
kernel_name = 'mk_prb_d1_jaxref_r4_7fddaa'

def setup_inputs(seed: int=0):
    np.random.seed(seed)
    _w = jnp.asarray

    def _L0_attn_setup():
        import jax, jax.numpy as jnp
        import numpy as np
        from jax import lax
        B, L, D = (2, 1024, 256)
        ORDER = 2
        EMB = 3
        FO = 64
        K = 3

        def _implicit_filter(seq_len, freqs_i, w1, b1, w2, b2, w3, b3, decay_i):
            t = jnp.linspace(0.0, 1.0, seq_len)
            ang = 2.0 * jnp.pi * freqs_i[None, :] * t[:, None]
            enc = jnp.concatenate([jnp.sin(ang), jnp.cos(ang), t[:, None]], axis=-1)
            h = jax.nn.gelu(enc @ w1 + b1, approximate=False)
            h = jax.nn.gelu(h @ w2 + b2, approximate=False)
            h = h @ w3 + b3
            window = jnp.exp(-jnp.abs(decay_i)[None, :] * t[:, None] * seq_len)
            return h * window

        def _fft_conv(v, h):
            seq_len = v.shape[1]
            fft_len = 1 << (2 * seq_len - 1).bit_length()
            v_f = jnp.fft.rfft(v, n=fft_len, axis=1)
            h_f = jnp.fft.rfft(h, n=fft_len, axis=0)[None]
            y = jnp.fft.irfft(v_f * h_f, n=fft_len, axis=1)
            return y[:, :seq_len, :]

        def _gated_control(u, kw, kb, gw, gb):
            xc = lax.conv_general_dilated(u, kw, window_strides=(1,), padding=[(K // 2, K // 2)], dimension_numbers=('NWC', 'WIO', 'NWC'), feature_group_count=u.shape[-1]) + kb
            gate = jax.nn.sigmoid(xc @ gw + gb)
            return xc * gate
        key = jax.random.key(seed)
        ks = jax.random.split(key, 10)
        f32 = jnp.float32
        rn = lambda k, shape, s=0.02: jax.random.normal(k, shape, dtype=f32) * s
        return {'x': jax.random.normal(ks[0], (B, L, D), dtype=f32), 'in_proj_w': rn(ks[1], (D, (ORDER + 1) * D)), 'in_proj_b': jnp.zeros(((ORDER + 1) * D,), f32), 'out_proj_w': rn(ks[2], (D, D)), 'out_proj_b': jnp.zeros((D,), f32), 'freqs': rn(ks[3], (ORDER, EMB), 0.01), 'mlp_w1': rn(ks[4], (ORDER, 2 * EMB + 1, FO), 0.1), 'mlp_b1': jnp.zeros((ORDER, FO), f32), 'mlp_w2': rn(ks[5], (ORDER, FO, FO), 0.1), 'mlp_b2': jnp.zeros((ORDER, FO), f32), 'mlp_w3': rn(ks[6], (ORDER, FO, D), 0.1), 'mlp_b3': jnp.zeros((ORDER, D), f32), 'decay': jnp.full((ORDER, D), 0.5, f32), 'conv_w': rn(ks[7], (ORDER, K, 1, D), 0.1), 'conv_b': jnp.zeros((ORDER, D), f32), 'gate_w': rn(ks[8], (ORDER, D, D)), 'gate_b': jnp.zeros((ORDER, D), f32)}
    _L0_attn_in = _L0_attn_setup()

    def _L0_ffn_setup():
        import jax, jax.numpy as jnp
        import numpy as np

        def _bitlinear(x, w_latent):
            scale = jax.lax.stop_gradient(jnp.clip(jnp.mean(jnp.abs(w_latent), axis=1, keepdims=True), 1e-05, None))
            tern = jnp.clip(jnp.round(w_latent / scale), -1.0, 1.0)
            w = w_latent + jax.lax.stop_gradient(tern - w_latent)
            return x @ (w * scale).T
        key = jax.random.key(seed)
        ks = jax.random.split(key, 6)
        dim, hidden, rank = (256, 1024, 16)
        B, S = (4, 1024)
        x = jax.random.normal(ks[0], (B, S, dim), dtype=jnp.float32)
        w_fc = 0.02 * jax.random.normal(ks[1], (hidden, dim), dtype=jnp.float32)
        w_proj = 0.02 * jax.random.normal(ks[2], (dim, hidden), dtype=jnp.float32)
        u = 0.02 * jax.random.normal(ks[3], (hidden, rank), dtype=jnp.float32)
        v = 0.02 * jax.random.normal(ks[4], (rank, dim), dtype=jnp.float32)
        fast_b = jax.random.normal(ks[5], (rank, rank), dtype=jnp.float32)
        gate = jnp.float32(0.05)
        return {'x': x, 'fast_b': fast_b, 'w_fc': w_fc, 'w_proj': w_proj, 'u': u, 'v': v, 'gate': gate}
    _L0_ffn_in = _L0_ffn_setup()
    _d = {'L0_attn_x': _L0_attn_in['x'], 'L0_attn_in_proj_w': _L0_attn_in['in_proj_w'], 'L0_attn_in_proj_b': _L0_attn_in['in_proj_b'], 'L0_attn_out_proj_w': _L0_attn_in['out_proj_w'], 'L0_attn_out_proj_b': _L0_attn_in['out_proj_b'], 'L0_attn_freqs': _L0_attn_in['freqs'], 'L0_attn_mlp_w1': _L0_attn_in['mlp_w1'], 'L0_attn_mlp_b1': _L0_attn_in['mlp_b1'], 'L0_attn_mlp_w2': _L0_attn_in['mlp_w2'], 'L0_attn_mlp_b2': _L0_attn_in['mlp_b2'], 'L0_attn_mlp_w3': _L0_attn_in['mlp_w3'], 'L0_attn_mlp_b3': _L0_attn_in['mlp_b3'], 'L0_attn_decay': _L0_attn_in['decay'], 'L0_attn_conv_w': _L0_attn_in['conv_w'], 'L0_attn_conv_b': _L0_attn_in['conv_b'], 'L0_attn_gate_w': _L0_attn_in['gate_w'], 'L0_attn_gate_b': _L0_attn_in['gate_b'], 'L0_ffn_fast_b': _L0_ffn_in['fast_b'], 'L0_ffn_w_fc': _L0_ffn_in['w_fc'], 'L0_ffn_w_proj': _L0_ffn_in['w_proj'], 'L0_ffn_u': _L0_ffn_in['u'], 'L0_ffn_v': _L0_ffn_in['v'], 'L0_ffn_gate': _L0_ffn_in['gate']}
    _x0 = _d['L0_attn_x']
    _d['L0_attn_x'] = jax.random.normal(jax.random.fold_in(jax.random.key(seed), 1), (4, 2048, 256), dtype=_x0.dtype)
    del _x0
    return _d

def reference(L0_attn_x, L0_attn_in_proj_w, L0_attn_in_proj_b, L0_attn_out_proj_w, L0_attn_out_proj_b, L0_attn_freqs, L0_attn_mlp_w1, L0_attn_mlp_b1, L0_attn_mlp_w2, L0_attn_mlp_b2, L0_attn_mlp_w3, L0_attn_mlp_b3, L0_attn_decay, L0_attn_conv_w, L0_attn_conv_b, L0_attn_gate_w, L0_attn_gate_b, L0_ffn_fast_b, L0_ffn_w_fc, L0_ffn_w_proj, L0_ffn_u, L0_ffn_v, L0_ffn_gate):

    def _L0_attn_ref(x, in_proj_w, in_proj_b, out_proj_w, out_proj_b, freqs, mlp_w1, mlp_b1, mlp_w2, mlp_b2, mlp_w3, mlp_b3, decay, conv_w, conv_b, gate_w, gate_b):
        import jax, jax.numpy as jnp
        import numpy as np
        from jax import lax
        B, L, D = (2, 1024, 256)
        ORDER = 2
        EMB = 3
        FO = 64
        K = 3

        def _implicit_filter(seq_len, freqs_i, w1, b1, w2, b2, w3, b3, decay_i):
            t = jnp.linspace(0.0, 1.0, seq_len)
            ang = 2.0 * jnp.pi * freqs_i[None, :] * t[:, None]
            enc = jnp.concatenate([jnp.sin(ang), jnp.cos(ang), t[:, None]], axis=-1)
            h = jax.nn.gelu(enc @ w1 + b1, approximate=False)
            h = jax.nn.gelu(h @ w2 + b2, approximate=False)
            h = h @ w3 + b3
            window = jnp.exp(-jnp.abs(decay_i)[None, :] * t[:, None] * seq_len)
            return h * window

        def _fft_conv(v, h):
            seq_len = v.shape[1]
            fft_len = 1 << (2 * seq_len - 1).bit_length()
            v_f = jnp.fft.rfft(v, n=fft_len, axis=1)
            h_f = jnp.fft.rfft(h, n=fft_len, axis=0)[None]
            y = jnp.fft.irfft(v_f * h_f, n=fft_len, axis=1)
            return y[:, :seq_len, :]

        def _gated_control(u, kw, kb, gw, gb):
            xc = lax.conv_general_dilated(u, kw, window_strides=(1,), padding=[(K // 2, K // 2)], dimension_numbers=('NWC', 'WIO', 'NWC'), feature_group_count=u.shape[-1]) + kb
            gate = jax.nn.sigmoid(xc @ gw + gb)
            return xc * gate
        _, seq_len, d = x.shape
        proj = x @ in_proj_w + in_proj_b
        v = proj[..., :d]
        for i in range(ORDER):
            ctrl = proj[..., (i + 1) * d:(i + 2) * d]
            h = _implicit_filter(seq_len, freqs[i], mlp_w1[i], mlp_b1[i], mlp_w2[i], mlp_b2[i], mlp_w3[i], mlp_b3[i], decay[i])
            v = _fft_conv(v, h)
            v = v * _gated_control(ctrl, conv_w[i], conv_b[i], gate_w[i], gate_b[i])
        return v @ out_proj_w + out_proj_b

    def _L0_ffn_ref(x, fast_b, w_fc, w_proj, u, v, gate):
        import jax, jax.numpy as jnp
        import numpy as np

        def _bitlinear(x, w_latent):
            scale = jax.lax.stop_gradient(jnp.clip(jnp.mean(jnp.abs(w_latent), axis=1, keepdims=True), 1e-05, None))
            tern = jnp.clip(jnp.round(w_latent / scale), -1.0, 1.0)
            w = w_latent + jax.lax.stop_gradient(tern - w_latent)
            return x @ (w * scale).T
        h = _bitlinear(x, w_fc) + gate * (x @ v.T @ fast_b.T @ u.T)
        r = jnp.maximum(h, 0.0)
        return _bitlinear(r * r, w_proj)
    x = L0_attn_x
    xn = _layernorm(x, axis=-1)
    x = x + _L0_attn_ref(xn, L0_attn_in_proj_w, L0_attn_in_proj_b, L0_attn_out_proj_w, L0_attn_out_proj_b, L0_attn_freqs, L0_attn_mlp_w1, L0_attn_mlp_b1, L0_attn_mlp_w2, L0_attn_mlp_b2, L0_attn_mlp_w3, L0_attn_mlp_b3, L0_attn_decay, L0_attn_conv_w, L0_attn_conv_b, L0_attn_gate_w, L0_attn_gate_b) + _L0_ffn_ref(xn, L0_ffn_fast_b, L0_ffn_w_fc, L0_ffn_w_proj, L0_ffn_u, L0_ffn_v, L0_ffn_gate)
    return x

_drawn_inputs = setup_inputs


def setup_inputs(seed=0):
    import zlib

    import numpy as np

    out = dict(_drawn_inputs(seed))
    spreads = {'L0_attn_in_proj_b': (0.0, 0.1),
     'L0_attn_out_proj_b': (0.0, 0.1),
     'L0_attn_mlp_b1': (0.0, 0.1),
     'L0_attn_mlp_b2': (0.0, 0.1),
     'L0_attn_mlp_b3': (0.0, 0.1),
     'L0_attn_decay': (0.5, 0.2),
     'L0_attn_conv_b': (0.0, 0.1),
     'L0_attn_gate_b': (0.0, 0.1)}
    factors = {}
    for name, (base, spread) in spreads.items():
        noise = np.random.default_rng([zlib.crc32(name.encode()), seed]).standard_normal(out[name].shape)
        drawn = base * np.exp(spread * noise) if base else spread * noise
        out[name] = jnp.asarray(drawn.astype(out[name].dtype))
    for name, factor in factors.items():
        out[name] = (out[name] * factor).astype(out[name].dtype)
    return out
```

```python
from contextlib import ExitStack

import concourse.bass as bass
from concourse import mybir

F32 = mybir.dt.float32
F32R = mybir.dt.float32r
I32 = mybir.dt.int32
ALU = mybir.AluOpType
ACT = mybir.ActivationFunctionType
AX = mybir.AxisListType

P = 128
B, L, D = 4, 2048, 256
KT = D // P
HID, RANK = 1024, 16
HT = HID // P
ORDERS, FO, EMB = 2, 64, 3
CH = 512
TT = CH // P
CPB = L // CH
NCH = B * CPB
NA = L // P
COLS = B * NA
PADDED = P - 1 + L
NEAR = 4
TAIL_FROM = (NEAR - 1) * P + 1
GC = 8
TC = 2
TILES = GC // TC
GPI = D // GC // (NCH // ORDERS)
ITERS = NCH // ORDERS
ROUND = 12582912.0
TWO_PI = 6.283185
LEAST_NORMAL = 1.17549435e-38


def setup_stage(nc, hbm, ident, bv_row, srow, flag, V, GC1, Win, Wgate, eps, half):
    (in_w, in_b, out_b, freqs, w1, b1, w2, b2, w3, b3, decay, gate_w, fast_b, w_fc, w_proj, u, v, gate,
     filters, fc_hi, fc_lo, proj_t) = hbm
    with ExitStack() as ctx:
        def sb(name, shape, dt=F32):
            return ctx.enter_context(nc.sbuf_tensor(name, shape, dt))

        def sem(name):
            return ctx.enter_context(nc.semaphore(name))

        Vf = V[:, :, :, :].rearrange("p c n a -> p (c n a)")
        Gf = GC1[:, :, :, :].rearrange("p c n a -> p (c n a)")
        hT = Vf[:, 0:4 * L].rearrange("p (w j) -> p w j", w=4)
        fc_nat = Vf[:, 8192:10240].rearrange("p (m d) -> p m d", m=HT)
        weff = Vf[:, 8192:10240].rearrange("p (k h) -> p k h", k=KT)
        fc_tern = Vf[:, 10240:12288].rearrange("p (m d) -> p m d", m=HT)
        pr_nat = Vf[:, 12288:14336].rearrange("p (k h) -> p k h", k=KT)
        pr_tern = Vf[:, 14336:16384].rearrange("p (k h) -> p k h", k=KT)
        t = Gf[:, 0:2 * L].rearrange("p (o j) -> p o j", o=ORDERS)
        enc = Gf[0:2 * EMB, 2 * L:4 * L].rearrange("p (o j) -> p o j", o=ORDERS)
        h1 = Gf[0:FO, 4 * L:6 * L].rearrange("p (o j) -> p o j", o=ORDERS)
        h2 = Gf[0:FO, 6 * L:8 * L].rearrange("p (o j) -> p o j", o=ORDERS)

        jint = Gf[:, 4 * L:6 * L].bitcast(I32).rearrange("p (o j) -> p o j", o=ORDERS)
        rnd = Gf[0:2 * EMB, 4 * L:5 * L]
        prow = sb("prow", [2 * EMB, 1], I32)
        prow_f = sb("prow_f", [2 * EMB, 1])
        phase = sb("phase", [2 * EMB, 1])
        f6 = sb("f6", [2 * EMB, ORDERS])
        w1sc = sb("w1sc", [2 * EMB, ORDERS, FO])
        w1t = sb("w1t", [1, ORDERS, FO])
        w2s = sb("w2s", [FO, ORDERS, FO])
        w3s = sb("w3s", [FO, ORDERS, D])
        b1s = sb("b1s", [FO, ORDERS])
        b2s = sb("b2s", [FO, ORDERS])
        b3s = sb("b3s", [P, ORDERS * KT])
        dec = sb("dec", [P, ORDERS * KT])
        ndec = sb("ndec", [P, ORDERS * KT])
        zpad = sb("zpad", [P, 4, P - 1])
        ones = sb("ones", [P, P])
        win_f = sb("win_f", [P, KT, 3 * D])
        gw_f = sb("gw_f", [P, ORDERS * KT, D])
        us = sb("us", [P, HT, RANK])
        vs = sb("vs", [RANK, D])
        fbT = sb("fbT", [RANK, RANK])
        gcol = sb("gcol", [P, 1])
        uT = sb("uT", [RANK, HID])
        m1 = sb("m1", [RANK, D])
        fsc = sb("fsc", [P, HT])
        fth = sb("fth", [P, 2 * HT])
        psc = sb("psc", [P, KT])
        pth = sb("pth", [P, 2 * KT])
        diag = sb("diag", [P, KT, P])
        weff_hi = sb("weff_hi", [P, KT, HID], F32R)
        weff_lo = sb("weff_lo", [P, KT, HID], F32R)
        projT = sb("projT", [P, HT, D], F32R)
        mx4 = sb("mx4", [P, 4])
        mx1 = sb("mx1", [P, 1])
        mxr = sb("mxr", [1, 2])
        ps = ctx.enter_context(nc.psum_tensor("ps_setup", [P, 8, 512], F32))

        filter_in, weights_in = sem("filter_in"), sem("weights_in")
        FILTER_LOADS, WEIGHT_LOADS = 22, 8
        ident_zero, ident_ready, iota_ready = sem("ident_zero"), sem("ident_ready"), sem("iota_ready")
        dve_step = sem("dve_step")
        angle_ready, enc_ready = sem("angle_ready"), sem("enc_ready")
        ndec_ready, win_ready, h_ready, pad_ready = sem("ndec_ready"), sem("win_ready"), sem("h_ready"), sem("pad_ready")
        l1_mm, l2_mm, l3_mm = sem("l1_mm"), sem("l2_mm"), sem("l3_mm")
        h1_ready, h2_ready = sem("h1_ready"), sem("h2_ready")
        uT_mm, m1_mm, rank_ready = sem("uT_mm"), sem("m1_mm"), sem("rank_ready")
        tern_ready, fcT_mm, lr_mm, fcT_read, lr_read = sem("tern_ready"), sem("fcT_mm"), sem("lr_mm"), sem("fcT_read"), sem("lr_read")
        weff_ready, weff_hi_ready, weff_lo_ready = sem("weff_ready"), sem("weff_hi_ready"), sem("weff_lo_ready")
        projT_mm, proj_ready, srow_mm, diag_ready = sem("projT_mm"), sem("proj_ready"), sem("srow_mm"), sem("diag_ready")
        peak_ready, peakT_mm = sem("peak_ready"), sem("peakT_mm")
        hi_ready = sem("hi_ready")
        stored = sem("stored")
        ctx.enter_context(nc.allow_non_contiguous_dma(reason="a few small vectors, one value a partition"))
        block = ctx.enter_context(nc.Block())

        @block.sync
        def _(sp):
            def load(dst, src, s):
                sp.dma_start(dst, src).then_inc(s, 16)

            for o in range(ORDERS):
                for half_ in range(2):
                    load(f6[half_ * EMB:(half_ + 1) * EMB, o:o + 1], freqs[o:o + 1, :].rearrange("o k -> k o"), filter_in)
                load(w1sc[:, o, :], w1[o, 0:2 * EMB, :], filter_in)
                load(w1t[:, o, :], w1[o, 2 * EMB:2 * EMB + 1, :], filter_in)
                load(w2s[:, o, :], w2[o], filter_in)
                load(w3s[:, o, :], w3[o], filter_in)
                load(b1s[:, o:o + 1], b1[o:o + 1, :].rearrange("o f -> f o"), filter_in)
                load(b2s[:, o:o + 1], b2[o:o + 1, :].rearrange("o f -> f o"), filter_in)
                load(b3s[:, KT * o:KT * o + KT], b3[o, :].rearrange("(c p) -> p c", p=P), filter_in)
                load(dec[:, KT * o:KT * o + KT], decay[o, :].rearrange("(c p) -> p c", p=P), filter_in)
                load(gw_f[:, KT * o:KT * o + KT, :], gate_w[o].rearrange("(k p) c -> p k c", p=P), filter_in)
            load(us[:, :, :], u.rearrange("(m p) r -> p m r", p=P), weights_in)
            load(vs[:, :], v, weights_in)
            load(fbT[:, :], fast_b.rearrange("i j -> j i"), weights_in)
            load(gcol[:, :], bass.AP(gate.tensor, 0, [[0, P], [1, 1]]), weights_in)
            load(fc_nat, w_fc.rearrange("(m p) d -> p m d", p=P), weights_in)
            load(pr_nat, w_proj.rearrange("(k p) h -> p k h", p=P), weights_in)
            load(win_f[:, :, :], in_w.rearrange("(k p) c -> p k c", p=P), weights_in)
            load(bv_row[:, :], bass.AP(in_b.tensor, 0, [[0, P], [1, D]]), weights_in)
            sp.wait_ge(pad_ready, 1)
            rows = filters.rearrange("(w p) j -> p w j", p=P)
            load(rows[:, 0:KT, L:PADDED], zpad[:, 0:KT, :], stored)
            load(rows[:, KT:2 * KT, 0:P - 1], zpad[:, KT:2 * KT, :], stored)
            for w in range(4):
                sp.wait_ge(h_ready, w + 1)
                at = 0 if w < KT else P - 1
                load(filters[w * P:(w + 1) * P, at:at + L], hT[:, w, :], stored)
            sp.wait_ge(weff_hi_ready, 1)
            load(fc_hi, weff_hi[:, :, :].bitcast(F32), stored)
            sp.wait_ge(weff_lo_ready, 1)
            load(fc_lo, weff_lo[:, :, :].bitcast(F32), stored)
            sp.wait_ge(proj_ready, 1)
            load(proj_t, projT[:, :, :].bitcast(F32), stored)
            sp.wait_ge(stored, 16 * 9)

        @block.gpsimd
        def _(pool):
            pool.memset(ident[:, :], 0.0).then_inc(ident_zero, 1)
            pool.wait_ge(ident_zero, 1)
            pool.affine_select(out=ident[:, :], in_=ident[:, :], compare_op=ALU.not_equal, fill=1.0, base=0,
                               pattern=[[-1, P]], channel_multiplier=1).then_inc(ident_ready, 1)
            pool.iota(jint[:, 0, :], [[-1, L]], base=L - 1, channel_multiplier=0).then_inc(iota_ready, 1)
            pool.iota(jint[:, 1, :], [[1, L]], base=0, channel_multiplier=0).then_inc(iota_ready, 1)
            pool.iota(prow[:, :], [[0, 1]], base=0, channel_multiplier=1).then_inc(iota_ready, 1)
            pool.memset(eps[:, :], 1e-5).then_inc(iota_ready, 1)
            pool.memset(half[:, :], -0.5).then_inc(iota_ready, 1)

        @block.vector
        def _(dve):
            steps = [0]

            def link(ins):
                steps[0] += 1
                ins.then_inc(dve_step, 1)
                dve.wait_ge(dve_step, steps[0])

            dve.memset(zpad[:, :, :], 0.0).then_inc(pad_ready, 1)
            dve.wait_ge(iota_ready, 5)
            link(dve.tensor_copy(t, jint))
            link(dve.tensor_scalar(t, t, 1.0 / (L - 1), None, ALU.mult))
            link(dve.tensor_copy(prow_f[:, :], prow[:, :]))
            link(dve.tensor_scalar(phase[:, :], prow_f[:, :], float(EMB), 0.25, ALU.is_ge, ALU.mult))
            dve.wait_ge(filter_in, 16 * FILTER_LOADS)
            for o in range(ORDERS):
                link(dve.tensor_scalar(enc[:, o, :], t[0:2 * EMB, o, :], f6[:, o:o + 1], phase[:, :], ALU.mult, ALU.add))
                link(dve.tensor_scalar(rnd, enc[:, o, :], ROUND, None, ALU.add))
                link(dve.tensor_scalar(rnd, rnd, ROUND, None, ALU.subtract))
                dve.tensor_tensor(enc[:, o, :], enc[:, o, :], rnd, ALU.subtract).then_inc(angle_ready, 1)
            link(dve.tensor_scalar(ndec[:, :], dec[:, :], -1.0, None, ALU.mult))
            link(dve.tensor_tensor(ndec[:, :], ndec[:, :], dec[:, :], ALU.min))
            link(dve.tensor_scalar(ndec[:, :], ndec[:, :], float(L), None, ALU.mult))
            dve.memset(ones[:, :], 1.0).then_inc(ndec_ready, 1)
            dve.wait_ge(weights_in, 16 * WEIGHT_LOADS)
            dve.wait_ge(uT_mm, 1)
            dve.tensor_copy(uT[:, :], ps[0:RANK, 0:2, :].rearrange("p a b -> p (a b)"))
            dve.wait_ge(m1_mm, 1)
            dve.tensor_scalar(m1[:, :], ps[0:RANK, 2, 0:D], gcol[0:RANK, :], None, ALU.mult).then_inc(rank_ready, 1)
            for nat, tern, sc, th, m, width in ((fc_nat, fc_tern, fsc, fth, HT, D), (pr_nat, pr_tern, psc, pth, KT, HID)):
                link(dve.tensor_reduce(sc[:, :], nat, AX.X, ALU.add, apply_absolute_value=True))
                link(dve.tensor_scalar(sc[:, :], sc[:, :], 1.0 / width, 1e-5, ALU.mult, ALU.max))
                dve.tensor_scalar(th[:, 0:m], sc[:, :], 0.5, None, ALU.mult)
                link(dve.tensor_scalar(th[:, m:2 * m], sc[:, :], -0.5, None, ALU.mult))
                for i in range(m):
                    last = dve.tensor_scalar(tern[:, i, :], nat[:, i, :], th[:, m + i:m + i + 1], None, ALU.is_lt)
                link(last)
                for i in range(m):
                    last = dve.scalar_tensor_tensor(out=tern[:, i, :], in0=nat[:, i, :], scalar=th[:, i:i + 1],
                                                    in1=tern[:, i, :], op0=ALU.is_gt, op1=ALU.subtract)
                link(last)
            for i in range(HT):
                last = dve.tensor_scalar(fc_tern[:, i, :], fc_tern[:, i, :], fsc[:, i:i + 1], None, ALU.mult)
            last.then_inc(tern_ready, 1)
            dve.wait_ge(ident_ready, 1)
            for k in range(KT):
                last = dve.tensor_scalar(diag[:, k, :], ident[:, :], psc[:, k:k + 1], None, ALU.mult)
            last.then_inc(diag_ready, 1)
            dve.wait_ge(hi_ready, 2)
            dve.tensor_tensor(Win[1][:, :, :], win_f[:, :, :], Win[0][:, :, :].bitcast(F32), ALU.subtract)
            dve.tensor_tensor(Wgate[1][:, :, :], gw_f[:, :, :], Wgate[0][:, :, :].bitcast(F32), ALU.subtract)
            for w in range(4):
                dve.wait_ge(win_ready, w + 1)
                dve.wait_ge(l3_mm, w + 1)
                b4 = 4 * (w % 2)
                dve.scalar_tensor_tensor(out=hT[:, w, :], in0=ps[:, b4:b4 + 4, :].rearrange("p a b -> p (a b)"),
                                         scalar=b3s[:, w:w + 1], in1=hT[:, w, :], op0=ALU.add, op1=ALU.mult).then_inc(h_ready, 1)
            dve.wait_ge(h_ready, 4)
            dve.tensor_reduce(mx4[:, 0:KT], hT[:, 0:KT, 0:L - TAIL_FROM], AX.X, ALU.max, apply_absolute_value=True)
            link(dve.tensor_reduce(mx4[:, KT:2 * KT], hT[:, KT:2 * KT, TAIL_FROM:L], AX.X, ALU.max, apply_absolute_value=True))
            dve.tensor_reduce(mx1[:, :], mx4[:, :], AX.X, ALU.max).then_inc(peak_ready, 1)
            dve.wait_ge(fcT_mm, 1)
            link(dve.tensor_copy(Vf[:, 8192:10240], ps[:, 0:4, :].rearrange("p a b -> p (a b)")))
            dve.wait_ge(lr_mm, 1)
            dve.tensor_tensor(Vf[:, 8192:10240], Vf[:, 8192:10240],
                              ps[:, 4:8, :].rearrange("p a b -> p (a b)"), ALU.add).then_inc(weff_ready, 1)
            dve.wait_ge(weff_hi_ready, 1)
            dve.tensor_tensor(weff_lo[:, :, :], weff, weff_hi[:, :, :].bitcast(F32), ALU.subtract).then_inc(weff_lo_ready, 1)
            dve.wait_ge(projT_mm, 1)
            dve.tensor_copy(projT[:, :, :].rearrange("p m d -> p (m d)"), ps[:, 0:4, :].rearrange("p a b -> p (a b)")).then_inc(proj_ready, 1)
            dve.wait_ge(srow_mm, 1)
            dve.tensor_copy(srow[:, :], ps[:, 4, 0:D])
            dve.wait_ge(peakT_mm, 1)
            link(dve.tensor_reduce(mxr[:, 0:1], ps[0:1, 5, 0:P], AX.X, ALU.max))
            link(dve.tensor_scalar(mxr[:, 1:2], mxr[:, 0:1], LEAST_NORMAL, None, ALU.is_ge))
            link(dve.tensor_copy(flag[:, :], mxr[:, 1:2]))

        @block.scalar
        def _(act):
            for o in range(ORDERS):
                act.wait_ge(angle_ready, o + 1)
                act.activation(enc[:, o, :], enc[:, o, :], ACT.Sin, scale=TWO_PI).then_inc(enc_ready, 1)
            act.wait_ge(filter_in, 16 * FILTER_LOADS)
            for o in range(ORDERS):
                act.wait_ge(l1_mm, o + 1)
                act.activation(h1[:, o, :], ps[0:FO, 4 * o:4 * o + 4, :].rearrange("p a b -> p (a b)"), ACT.Gelu,
                               bias=b1s[:, o:o + 1]).then_inc(h1_ready, 1)
            for o in range(ORDERS):
                act.wait_ge(l2_mm, o + 1)
                act.activation(h2[:, o, :], ps[0:FO, 4 * o:4 * o + 4, :].rearrange("p a b -> p (a b)"), ACT.Gelu,
                               bias=b2s[:, o:o + 1]).then_inc(h2_ready, 1)
            act.wait_ge(ndec_ready, 1)
            for w in range(4):
                act.activation(hT[:, w, :], t[:, w // KT, :], ACT.Exp, scale=ndec[:, w:w + 1]).then_inc(win_ready, 1)
            act.wait_ge(weights_in, 16 * WEIGHT_LOADS)
            act.activation(Win[0][:, :, :], win_f[:, :, :], ACT.Copy).then_inc(hi_ready, 1)
            act.activation(Wgate[0][:, :, :], gw_f[:, :, :], ACT.Copy).then_inc(hi_ready, 1)
            act.wait_ge(weff_ready, 1)
            act.activation(weff_hi[:, :, :], weff, ACT.Copy).then_inc(weff_hi_ready, 1)

        @block.tensor
        def _(pe):
            pe.wait_ge(weights_in, 16 * WEIGHT_LOADS)
            pe.wait_ge(ident_ready, 1)
            for m in range(HT):
                last = pe.transpose(ps[0:RANK, m // 4, (m % 4) * P:(m % 4 + 1) * P], us[:, m, :], ident[:, :])
            last.then_inc(uT_mm, 1)
            pe.matmul(ps[0:RANK, 2, 0:D], fbT[:, :], vs[:, :], start=True, stop=True).then_inc(m1_mm, 1)
            pe.wait_ge(rank_ready, 1)
            pe.wait_ge(filter_in, 16 * FILTER_LOADS)
            for o in range(ORDERS):
                pe.wait_ge(enc_ready, o + 1)
                for j in range(4):
                    js = slice(j * 512, j * 512 + 512)
                    pe.matmul(ps[0:FO, 4 * o + j, :], w1sc[:, o, :], enc[:, o, js], start=True, stop=False)
                    last = pe.matmul(ps[0:FO, 4 * o + j, :], w1t[:, o, :], t[0:1, o, js], start=False, stop=True)
                last.then_inc(l1_mm, 1)
            for o in range(ORDERS):
                pe.wait_ge(h1_ready, o + 1)
                for j in range(4):
                    last = pe.matmul(ps[0:FO, 4 * o + j, :], w2s[:, o, :], h1[:, o, j * 512:j * 512 + 512], start=True, stop=True)
                last.then_inc(l2_mm, 1)
            pe.wait_ge(h2_ready, 2)
            for w in range(4):
                if w >= 2:
                    pe.wait_ge(h_ready, w - 1)
                o, c = w // KT, w % KT
                for j in range(4):
                    last = pe.matmul(ps[:, 4 * (w % 2) + j, :], w3s[:, o, c * P:(c + 1) * P], h2[:, o, j * 512:j * 512 + 512],
                                     start=True, stop=True)
                last.then_inc(l3_mm, 1)
            pe.wait_ge(tern_ready, 1)
            pe.wait_ge(h_ready, 3)
            for k in range(KT):
                for m in range(HT):
                    last = pe.transpose(ps[:, 2 * k + m // 4, (m % 4) * P:(m % 4 + 1) * P], fc_tern[:, m, k * P:(k + 1) * P], ident[:, :])
            last.then_inc(fcT_mm, 1)
            pe.wait_ge(h_ready, 4)
            for k in range(KT):
                for j in range(2):
                    last = pe.matmul(ps[:, 4 + 2 * k + j, :], m1[:, k * P:(k + 1) * P], uT[:, j * 512:j * 512 + 512],
                                     start=True, stop=True)
            last.then_inc(lr_mm, 1)
            pe.wait_ge(weff_ready, 1)
            for m in range(HT):
                for k in range(KT):
                    last = pe.transpose(ps[:, m // 2, (m % 2) * D + k * P:(m % 2) * D + (k + 1) * P],
                                        pr_tern[:, k, m * P:(m + 1) * P], ident[:, :])
            last.then_inc(projT_mm, 1)
            pe.wait_ge(diag_ready, 1)
            pe.matmul(ps[:, 4, 0:D], ones[:, :], diag[:, :, :].rearrange("p k c -> p (k c)"), start=True, stop=True).then_inc(srow_mm, 1)
            pe.wait_ge(peak_ready, 1)
            pe.transpose(ps[0:1, 5, 0:P], mx1[:, :], ident[:, :]).then_inc(peakT_mm, 1)


def wait_alone(eng, sem, value, passed):
    eng.wait_ge(sem, value)
    eng.sem_inc(passed, 1)


def split_mm(pe, out, w, x, start, stop, **more):
    pe.matmul(out, w[0], x[0], start=start, stop=False, **more)
    pe.matmul(out, w[1], x[0], start=False, stop=False, **more)
    return pe.matmul(out, w[0], x[1], start=False, stop=stop, **more)


def project_stage(nc, x, xnT_hbm, gc2_hbm, in_b, conv_w, conv_b, gate_b, ident, bv_row, V, GC1, Win, Wgate, eps, half):
    with ExitStack() as ctx:
        def sb(name, shape, dt=F32):
            return ctx.enter_context(nc.sbuf_tensor(name, shape, dt))

        def sem(name):
            return ctx.enter_context(nc.semaphore(name))

        xt = sb("xt", [P, TT, D])
        norms = sb("norms", [P, TT, 11])
        stats, mv, ve, rs, nt = norms[:, :, 0:6], norms[:, :, 6:8], norms[:, :, 8], norms[:, :, 9], norms[:, :, 10]
        xn = [sb("xn_hi", [P, KT, CH], F32R), sb("xn_lo", [P, KT, CH], F32R)]
        xnF = sb("xnF", [P, KT, CH])
        ctrl = [sb(f"ctrl{i}", [P, 4, CH + 2]) for i in range(2)]
        xc = sb("xc", [P, 4, CH])
        xcs = [[sb(f"xc_{part}{o}", [P, KT, CH], F32R) for part in ("hi", "lo")] for o in range(ORDERS)]
        taps = sb("taps", [P, 4, 6])
        kw, cb, kb, gb = taps[:, :, 0:3], taps[:, :, 3], taps[:, :, 4], taps[:, :, 5]
        pT = ctx.enter_context(nc.psum_tensor("pT", [P, KT, CH], F32))
        pn = ctx.enter_context(nc.psum_tensor("pn", [P, TT, D], F32))
        pc = ctx.enter_context(nc.psum_tensor("pc", [P, 4, CH], F32))

        bias_in = sem("bias_in")
        sp_passed, pool_passed, dve_passed = sem("sp_passed"), sem("pool_passed"), sem("dve_passed")
        x_loaded = sem("x_loaded")
        stat_done, aggr_done = sem("stat_done"), sem("aggr_done")
        rstd_step = sem("rstd_step")
        xn_ready = sem("xn_ready")
        xT_mm = sem("xT_mm")
        xn_hi_done, xnF_copied, xn_split = sem("xn_hi_done"), sem("xnF_copied"), sem("xn_split")
        xnF_saved = sem("xnF_saved")
        ctrl_mm, ctrl_copied = sem("ctrl_mm"), sem("ctrl_copied")
        v_mm, v_stored = sem("v_mm"), sem("v_stored")
        halo_done = sem("halo_done")
        tap0_done, tap1_done = sem("tap0_done"), sem("tap1_done")
        xc_ready = sem("xc_ready")
        xc_hi_done = sem("xc_hi_done")
        xc_split_dve, xc_split_pool = sem("xc_split_dve"), sem("xc_split_pool")
        gate_mm = sem("gate_mm")
        gate_done = sem("gate_done")
        gc_done = sem("gc_done")
        gcT_mm = sem("gcT_mm")
        gc1_stored = sem("gc1_stored")
        gc2_saved = sem("gc2_saved")
        ctx.enter_context(nc.allow_non_contiguous_dma(reason="a few small vectors, one value a partition"))
        block = ctx.enter_context(nc.Block())

        def steps(eng, step):
            step(-1, -1)
            step(0, 0)
            with eng.Fori(0, (NCH - 4) // 4) as m:
                batch_of[eng.engine] = m
                for j in range(4):
                    step(m * 4 + (j + 1), 1 + j)
            for s in range(NCH - 3, NCH + 1):
                step(s, s)

        batch_of = {}

        def batch(eng, s, s0):
            return s // CPB if isinstance(s, int) else batch_of[eng.engine] + s0 // CPB

        def tapped(buffer, c, k):
            at = 2 - k if c < KT else k
            return buffer[:, c, at:at + CH]

        def has(s0):
            return 0 <= s0 < NCH, s0 + 1 < NCH, s0 >= 1

        @block.sync
        def _(sp):
            sp.dma_start(cb, in_b[D:3 * D].rearrange("(c p) -> p c", p=P)).then_inc(bias_in, 16)
            for o in range(ORDERS):
                cs = slice(KT * o, KT * o + KT)
                for k in range(3):
                    sp.dma_start(kw[:, cs, k], conv_w[o, k, 0, :].rearrange("(c p) -> p c", p=P)).then_inc(bias_in, 16)
                sp.dma_start(kb[:, cs], conv_b[o, :].rearrange("(c p) -> p c", p=P)).then_inc(bias_in, 16)
                sp.dma_start(gb[:, cs], gate_b[o, :].rearrange("(c p) -> p c", p=P)).then_inc(bias_in, 16)
            sp.sem_inc(gc2_saved, 16)
            x_tiles = x.rearrange("n (q i p) d -> (n q) p i d", i=TT, p=P)

            def load_x(c):
                sp.dma_start(xt[:, :, :], x_tiles[bass.ds(c, 1)].rearrange("c p i d -> (c p) i d")).then_inc(x_loaded, 16)

            load_x(0)

            def step(s, s0):
                front, ahead, back = has(s0)
                if ahead:
                    wait_alone(sp, xnF_copied, s + 2, sp_passed)
                    sp.dma_start(xnT_hbm[bass.ds(s + 1, 1)].rearrange("c p k t -> (c p) k t"), xnF[:, :, :]).then_inc(xnF_saved, 16)
                if s0 + 2 < NCH:
                    wait_alone(sp, xT_mm, s + 2, sp_passed)
                    load_x(s + 2)
                if back:
                    wait_alone(sp, gc_done, 4 * s + 4, sp_passed)
                    sp.dma_start(gc2_hbm[bass.ds(s - 1, 1)].rearrange("c p k t -> (c p) k t"), xc[:, KT:2 * KT, :]).then_inc(gc2_saved, 16)

            steps(sp, step)
            sp.wait_ge(xnF_saved, 16 * NCH)
            sp.wait_ge(gc2_saved, 16 * NCH + 16)

        @block.gpsimd
        def _(pool):
            def rstd(c, first=False):
                r = 6 * c
                pool.wait_ge(aggr_done, 4 * c + 4)
                if not first:
                    pool.wait_ge(xn_ready, c)
                pool.tensor_tensor(ve, mv[:, :, 1], eps[:, :], ALU.add).then_inc(rstd_step, 1)
                pool.wait_ge(rstd_step, r + 1)
                pool.tensor_tensor(rs, ve, half[:, :], ALU.pow).then_inc(rstd_step, 1)
                pool.wait_ge(rstd_step, r + 2)
                pool.tensor_tensor(nt, rs, rs, ALU.mult).then_inc(rstd_step, 1)
                pool.wait_ge(rstd_step, r + 3)
                pool.tensor_tensor(nt, nt, ve, ALU.mult).then_inc(rstd_step, 1)
                wait_alone(pool, rstd_step, r + 4, pool_passed)
                pool.tensor_scalar(nt, nt, -0.5, 1.5, ALU.mult, ALU.add).then_inc(rstd_step, 1)
                pool.wait_ge(rstd_step, r + 5)
                pool.tensor_tensor(rs, rs, nt, ALU.mult).then_inc(rstd_step, 1)

            def step(s, s0):
                front, ahead, back = has(s0)
                if back:
                    for c in (1, 3):
                        pool.wait_ge(xc_hi_done, 4 * s - 4 + c + 1)
                        pool.tensor_tensor(xcs[c // KT][1][:, c % KT, :], xc[:, c, :], xcs[c // KT][0][:, c % KT, :].bitcast(F32),
                                           ALU.subtract).then_inc(xc_split_pool, 1)
                if s0 + 2 < NCH:
                    rstd(s + 2)

            rstd(0, True)
            steps(pool, step)

        @block.vector
        def _(dve):
            dve.sem_inc(gc1_stored, 1)
            dve.sem_inc(gc_done, 4)
            dve.sem_inc(xc_ready, 4)

            def statistics(c):
                dve.wait_ge(x_loaded, 16 * c + 16)
                for i in range(TT):
                    dve.bn_stats(stats[:, i, :], xt[:, i, :]).then_inc(stat_done, 1)
                for i in range(TT):
                    wait_alone(dve, stat_done, 4 * c + i + 1, dve_passed)
                    dve.bn_aggr(mv[:, i, :], stats[:, i, :]).then_inc(aggr_done, 1)

            def step(s, s0):
                front, ahead, back = has(s0)
                par, k = s0 % 2, s0 % 4

                def halo(o):
                    cs = slice(KT * o, KT * o + KT)
                    near, far, inner_far, inner_near = (0, CH + 1, CH, 1) if o else (CH + 1, 0, 1, CH)
                    if front:
                        dve.wait_ge(ctrl_copied, 4 * s + KT * o + KT)
                    if front and k == 0:
                        last = dve.memset(ctrl[par][:, cs, near:near + 1], 0.0)
                    elif front:
                        last = dve.tensor_copy(ctrl[par][:, cs, near:near + 1], ctrl[1 - par][:, cs, inner_far:inner_far + 1])
                    if back and k == 0:
                        last = dve.memset(ctrl[1 - par][:, cs, far:far + 1], 0.0)
                    elif back:
                        last = dve.tensor_copy(ctrl[1 - par][:, cs, far:far + 1], ctrl[par][:, cs, inner_near:inner_near + 1])
                    last.then_inc(halo_done, 1)

                def tap(o, k_, before, done):
                    for c in range(KT * o, KT * o + KT):
                        dve.wait_ge(before, 4 * s - 4 + c + 1)
                        dve.scalar_tensor_tensor(out=xc[:, c, :], in0=tapped(ctrl[1 - par], c, k_), scalar=kw[:, c, k_:k_ + 1],
                                                 in1=xc[:, c, :], op0=ALU.mult, op1=ALU.add).then_inc(done, 1)

                def low(c):
                    dve.wait_ge(xc_hi_done, 4 * s - 4 + c + 1)
                    dve.tensor_tensor(xcs[c // KT][1][:, c % KT, :], xc[:, c, :], xcs[c // KT][0][:, c % KT, :].bitcast(F32),
                                      ALU.subtract).then_inc(xc_split_dve, 1)

                def gated(c):
                    dve.wait_ge(gate_done, 4 * s - 4 + c + 1)
                    dve.tensor_tensor(xc[:, c, :], pc[:, c, :], xc[:, c, :], ALU.mult).then_inc(gc_done, 1)

                if s0 >= 0:
                    halo(0)
                if back:
                    tap(0, 1, tap0_done, tap1_done)
                    tap(0, 2, tap1_done, xc_ready)
                if ahead:
                    dve.wait_ge(rstd_step, 6 * s + 12)
                    for i in range(TT):
                        last = dve.tensor_scalar(xt[:, i, :], xt[:, i, :], mv[:, i, 0:1], rs[:, i:i + 1], ALU.subtract, ALU.mult)
                    last.then_inc(xn_ready, 1)
                if s0 >= 0:
                    halo(1)
                if back:
                    tap(1, 1, tap0_done, tap1_done)
                    low(0)
                    tap(1, 2, tap1_done, xc_ready)
                    low(2)
                if front:
                    dve.wait_ge(v_mm, s + 1)
                    dve.tensor_tensor(V[:, :, bass.ds(batch(dve, s, s0), 1), TT * k:TT * k + TT].rearrange("p c n a -> p c (n a)"),
                                      pn[:, :, :].rearrange("p i c -> p c i"),
                                      bv_row[:, :].unsqueeze(2).broadcast_to([P, D, TT]), ALU.add).then_inc(v_stored, 1)
                if back:
                    gated(0)
                    gated(1)
                if ahead:
                    dve.wait_ge(xn_hi_done, s + 2)
                    dve.tensor_tensor(xn[1][:, :, :], xnF[:, :, :], xn[0][:, :, :].bitcast(F32), ALU.subtract).then_inc(xn_split, 1)
                if back:
                    gated(2)
                    gated(3)
                if s0 + 2 < NCH:
                    statistics(s + 2)

            statistics(0)
            steps(dve, step)

        @block.scalar
        def _(act):
            act.wait_ge(bias_in, 16 * 11)

            def step(s, s0):
                front, ahead, back = has(s0)
                par = s0 % 2

                def controls(o):
                    if s0 >= 1 and o == 0:
                        act.wait_ge(xc_ready, 4 * s)
                    for c in range(KT * o, KT * o + KT):
                        act.wait_ge(ctrl_mm, 4 * s + c + 1)
                        act.activation(ctrl[par][:, c, 1:CH + 1], pc[:, c, ::-1] if c < KT else pc[:, c, :], ACT.Identity, bias=cb[:, c:c + 1]).then_inc(ctrl_copied, 1)

                def first_tap(o):
                    act.wait_ge(halo_done, 2 * s + o + 1)
                    if o == 0:
                        act.wait_ge(gcT_mm, s)
                    else:
                        act.wait_ge(gc2_saved, 16 * s)
                    for c in range(KT * o, KT * o + KT):
                        act.activation(xc[:, c, :], tapped(ctrl[1 - par], c, 0), ACT.Identity, bias=kb[:, c:c + 1],
                                       scale=kw[:, c, 0:1]).then_inc(tap0_done, 1)

                def high(o):
                    act.wait_ge(gate_mm, 4 * s - 4 + KT * o + KT)
                    for c in range(KT * o, KT * o + KT):
                        act.wait_ge(xc_ready, 4 * s + c + 1)
                        act.activation(xcs[o][0][:, c % KT, :], xc[:, c, :], ACT.Copy).then_inc(xc_hi_done, 1)

                for o in range(ORDERS):
                    if front:
                        controls(o)
                    if back:
                        first_tap(o)
                if back:
                    high(0)
                if ahead:
                    act.wait_ge(xT_mm, s + 2)
                    if s0 >= 0:
                        act.wait_ge(xnF_saved, 16 * s + 16)
                    act.activation(xnF[:, :, :], pT[:, :, :], ACT.Copy).then_inc(xnF_copied, 1)
                if back:
                    high(1)
                if ahead:
                    act.wait_ge(xnF_copied, s + 2)
                    act.activation(xn[0][:, :, :], xnF[:, :, :], ACT.Copy).then_inc(xn_hi_done, 1)
                if back:
                    for c in range(4):
                        act.wait_ge(gate_mm, 4 * s + c + 1)
                        act.activation(pc[:, c, :], pc[:, c, :], ACT.Sigmoid, bias=gb[:, c:c + 1]).then_inc(gate_done, 1)
                    act.wait_ge(gcT_mm, s + 1)
                    pk = (s0 - 1) % 4
                    act.activation(GC1[:, :, bass.ds(batch(act, s - 1, s0 - 1), 1), TT * pk:TT * pk + TT].rearrange("p c n a -> p c (n a)"),
                                   pn[:, :, :].rearrange("p i c -> p c i"), ACT.Copy).then_inc(gc1_stored, 1)

            steps(act, step)

        @block.tensor
        def _(pe):
            pe.sem_inc(gate_mm, 4)
            pe.sem_inc(gcT_mm, 1)

            def step(s, s0):
                front, ahead, back = has(s0)
                if front:
                    pe.wait_ge(xn_split, s + 1)
                    for c in range(4):
                        if s0 >= 1:
                            pe.wait_ge(gc_done, 4 * s - 4 + c + 1)
                        for k in range(KT):
                            ws = slice(D + c * P, D + (c + 1) * P)
                            last = split_mm(pe, pc[:, c, :], (Win[0][:, k, ws], Win[1][:, k, ws]),
                                            (xn[0][:, k, :], xn[1][:, k, :]), k == 0, k == KT - 1)
                        last.then_inc(ctrl_mm, 1)
                    if s0 >= 1:
                        pe.wait_ge(gc1_stored, s)
                    for i in range(TT):
                        ts = slice(i * P, (i + 1) * P)
                        for k in range(KT):
                            last = split_mm(pe, pn[:, i, :], (xn[0][:, k, ts], xn[1][:, k, ts]),
                                            (Win[0][:, k, 0:D], Win[1][:, k, 0:D]), k == 0, k == KT - 1)
                    last.then_inc(v_mm, 1)
                if ahead:
                    pe.wait_ge(xn_ready, s + 2)
                    if s0 >= 0:
                        pe.wait_ge(xnF_copied, s + 1)
                    for k in range(KT):
                        for i in range(TT):
                            last = pe.transpose(pT[:, k, i * P:(i + 1) * P], xt[:, i, k * P:(k + 1) * P], ident[:, :])
                    last.then_inc(xT_mm, 1)
                if back:
                    for o in range(ORDERS):
                        pe.wait_ge(xc_split_dve, 2 * s - 2 + o + 1)
                        pe.wait_ge(xc_split_pool, 2 * s - 2 + o + 1)
                        for co in range(KT):
                            c = KT * o + co
                            if front:
                                pe.wait_ge(ctrl_copied, 4 * s + c + 1)
                            else:
                                pe.wait_ge(gc_done, 4 * s - 4 + c + 1)
                            for k in range(KT):
                                ws = slice(co * P, (co + 1) * P)
                                last = split_mm(pe, pc[:, c, :], (Wgate[0][:, KT * o + k, ws], Wgate[1][:, KT * o + k, ws]),
                                                (xcs[o][0][:, k, :], xcs[o][1][:, k, :]), k == 0, k == KT - 1)
                            last.then_inc(gate_mm, 1)
                    pe.wait_ge(gc_done, 4 * s + KT)
                    if front:
                        pe.wait_ge(v_stored, s + 1)
                    else:
                        pe.wait_ge(gc1_stored, s)
                    for i in range(TT):
                        for k in range(KT):
                            last = pe.transpose(pn[:, TT - 1 - i, k * P:(k + 1) * P], xc[:, k, i * P:(i + 1) * P], ident[:, :])
                    last.then_inc(gcT_mm, 1)

            steps(pe, step)


def mix_stage(nc, x, filters, fc_hi, fc_lo, proj_t, xnT_hbm, xf_hbm, out_b, srow, flag, V, GC1):
    with ExitStack() as ctx:
        def sb(name, shape, dt=F32):
            return ctx.enter_context(nc.sbuf_tensor(name, shape, dt))

        def sem(name):
            return ctx.enter_context(nc.semaphore(name))

        wfc = [sb("wfc_hi", [P, KT, HID], F32R), sb("wfc_lo", [P, KT, HID], F32R)]
        wproj = sb("wproj", [P, HT, D], F32R)
        T = sb("T", [P, TILES, TC, NEAR * P])
        xraw = sb("xraw", [P, KT, CH])
        xn = [sb("xm_hi", [P, KT, CH], F32R), sb("xm_lo", [P, KT, CH], F32R)]
        xb = sb("xb", [P, TT, D])
        bo_row = sb("bo_row", [P, D])
        r = [sb(f"r{i}", [P, CH]) for i in range(2)]
        r_hi = [sb(f"r_hi{i}", [P, CH], F32R) for i in range(2)]
        r_lo = [sb(f"r_lo{i}", [P, CH], F32R) for i in range(2)]
        py = [ctx.enter_context(nc.psum_tensor(f"py{i}", [P, GC, B, NA], F32)) for i in range(2)]
        pf = [ctx.enter_context(nc.psum_tensor(f"pf{i}", [P, CH], F32)) for i in range(2)]
        pp = ctx.enter_context(nc.psum_tensor("pp", [P, TT, D], F32))

        w_in, bo_in = sem("w_in"), sem("bo_in")
        sp_passed, pool_passed = sem("sp_passed"), sem("pool_passed")
        T_loaded = [sem(f"T_loaded{q}") for q in range(TILES)]
        tile_mm = sem("tile_mm")
        far_loaded, far_used = sem("far_loaded"), sem("far_used")
        y_out = sem("y_out")
        xraw_loaded, xn_hi_done, xn_split = sem("xraw_loaded"), sem("xn_hi_done"), sem("xn_split")
        xb_loaded, xb_biased = sem("xb_loaded"), sem("xb_biased")
        scaled, xf_saved = sem("scaled"), sem("xf_saved")
        xf_ready = sem("xf_ready")
        fc_mm = sem("fc_mm")
        relu_done = sem("relu_done")
        sq_done, r_hi_done = sem("sq_done"), sem("r_hi_done")
        r_split = sem("r_split")
        proj_mm = sem("proj_mm")
        ctx.enter_context(nc.allow_non_contiguous_dma(reason="a few small vectors, one value a partition"))
        block = ctx.enter_context(nc.Block())

        hankel = bass.AP(filters.tensor, 0, [[1, P], [PADDED, ORDERS * D], [1, L]])
        FAR = (NA // NEAR - 1) * TILES

        def groups(eng, order, body):
            with eng.Fori(0, ITERS) as m:
                body(m, m + ITERS * order)

        @block.sync
        def _(sp):
            for dst, src in ((wfc[0], fc_hi), (wfc[1], fc_lo), (wproj, proj_t)):
                sp.dma_start(dst[:, :, :].bitcast(F32), src).then_inc(w_in, 16)
            sp.sem_inc(tile_mm, TILES)
            tail = sp.value_load(flag[0:1, 0:1], min_val=0, max_val=1)
            for order in range(ORDERS):
                def body(m, it):
                    for g in range(GPI):
                        G = it * GPI + g
                        row = m * (GPI * GC) + (order * D + g * GC)

                        def load(slot, q, block_, s):
                            first = L - NEAR * P * (block_ + 1) if order == 0 else NEAR * P * block_
                            sp.dma_start(T[:, slot, :, :], hankel[:, bass.ds(row + q * TC, TC), first:first + NEAR * P]).then_inc(s, 16)

                        wait_alone(sp, tile_mm, G * TILES + 1, sp_passed)
                        load(0, 0, 0, T_loaded[0])
                        wait_alone(sp, tile_mm, G * TILES + 2, sp_passed)
                        with sp.If(tail > 0):
                            for j in range(FAR):
                                load(1, j % TILES, 1 + j // TILES, far_loaded)
                                wait_alone(sp, far_used, G * FAR + (j + 1), sp_passed)
                        for q in range(1, TILES):
                            wait_alone(sp, tile_mm, G * TILES + q + 1, sp_passed)
                            load(q, q, 0, T_loaded[q])
                groups(sp, order, body)

        @block.gpsimd
        def _(pool):
            x_tiles = x.rearrange("n (q i p) d -> (n q) p i d", i=TT, p=P)

            def load_raw(c):
                pool.dma_start(xraw[:, :, :], xnT_hbm[bass.ds(c, 1)].rearrange("c p k t -> (c p) k t")).then_inc(xraw_loaded, 16)

            def load_xb(it):
                pool.dma_start(xb[:, :, :], x_tiles[bass.ds(it, 1)].rearrange("c p i d -> (c p) i d")).then_inc(xb_loaded, 16)
                wait_alone(pool, xb_loaded, it * 16 + 16, pool_passed)
                pool.tensor_tensor(xb[:, :, :], xb[:, :, :], bo_row[:, :].unsqueeze(1).broadcast_to([P, TT, D]), ALU.add).then_inc(xb_biased, 1)

            def save_xf(it):
                wait_alone(pool, xf_ready, it + 2, pool_passed)
                pool.dma_start(xf_hbm[bass.ds(it, 1)].rearrange("c p i d -> (c p) i d"), xb[:, :, :]).then_inc(xf_saved, 16)
                wait_alone(pool, xf_saved, it * 16 + 16, pool_passed)

            pool.dma_start(bo_row[:, :], bass.AP(out_b.tensor, 0, [[0, P], [1, D]])).then_inc(bo_in, 16)
            pool.wait_ge(bo_in, 16)
            load_raw(0)
            load_xb(0)
            with pool.Fori(1, NCH) as i:
                wait_alone(pool, xn_split, i, pool_passed)
                load_raw(i)
                save_xf(i - 1)
                load_xb(i)
            save_xf(NCH - 1)

        @block.vector
        def _(dve):
            dve.sem_inc(y_out, 2)
            dve.sem_inc(r_split, 2)

            def split_x(it):
                dve.wait_ge(xn_hi_done, it + 1)
                dve.tensor_tensor(xn[1][:, :, :], xraw[:, :, :], xn[0][:, :, :].bitcast(F32), ALU.subtract).then_inc(xn_split, 1)

            def finish(it):
                dve.wait_ge(proj_mm, it * HT + HT + 2)
                dve.tensor_tensor(pp[:, :, :], pp[:, :, :], srow[:, :].unsqueeze(1).broadcast_to([P, TT, D]), ALU.mult).then_inc(scaled, 1)
                dve.wait_ge(scaled, it + 1)
                dve.wait_ge(xb_biased, it + 1)
                dve.tensor_tensor(xb[:, :, :], pp[:, :, :], xb[:, :, :], ALU.add).then_inc(xf_ready, 1)

            def body(m, it, order, prev):
                split_x(it)
                if prev is not None:
                    finish(prev)
                for g in range(GPI):
                    for j in range(2):
                        uu = it * HT + (2 * g + j)
                        dve.wait_ge(relu_done, uu + 3)
                        dve.tensor_tensor(r[j][:, :], r[j][:, :], r[j][:, :], ALU.mult).then_inc(sq_done, 1)
                        dve.wait_ge(r_hi_done, uu + 1)
                        dve.tensor_tensor(r_lo[j][:, :], r[j][:, :], r_hi[j][:, :].bitcast(F32), ALU.subtract).then_inc(r_split, 1)
                    G = it * GPI + g
                    c0 = m * (GPI * GC) + g * GC
                    out = V[:, bass.ds(c0, GC)].rearrange("p c n a -> p (c n a)")
                    y = py[g % 2][:, :, :, :].rearrange("p c n a -> p (c n a)")
                    dve.wait_ge(tile_mm, G * TILES + 2 * TILES)
                    if order == 0:
                        dve.tensor_tensor(out, y, GC1[:, bass.ds(c0, GC)].rearrange("p c n a -> p (c n a)"), ALU.mult).then_inc(y_out, 1)
                    else:
                        dve.tensor_copy(out, y).then_inc(y_out, 1)

            body(0, 0, 0, None)
            with dve.Fori(1, ITERS) as m:
                body(m, m, 0, m - 1)
            with dve.Fori(0, ITERS) as m:
                body(m, m + ITERS, 1, m + (ITERS - 1))
            finish(NCH - 1)

        @block.scalar
        def _(act):
            act.sem_inc(relu_done, 2)
            with act.Fori(0, NCH) as it:
                act.wait_ge(xraw_loaded, it * 16 + 16)
                act.wait_ge(fc_mm, it * HT + HT)
                act.activation(xn[0][:, :, :], xraw[:, :, :], ACT.Copy).then_inc(xn_hi_done, 1)
                for m in range(HT):
                    uu, j = it * HT + m, m % 2
                    act.wait_ge(fc_mm, uu + HT + 1)
                    act.wait_ge(r_split, uu + 1)
                    act.activation(r[j][:, :], pf[j][:, :], ACT.Relu).then_inc(relu_done, 1)
                    act.wait_ge(sq_done, uu + 1)
                    act.wait_ge(proj_mm, uu + 1)
                    act.activation(r_hi[j][:, :], r[j][:, :], ACT.Copy).then_inc(r_hi_done, 1)

        @block.tensor
        def _(pe):
            pe.sem_inc(fc_mm, HT)
            pe.sem_inc(proj_mm, 2)
            pe.sem_inc(xf_ready, 1)
            tail = pe.value_load(flag[0:1, 0:1], min_val=0, max_val=1)
            pe.wait_ge(w_in, 16 * 3)

            def fc(it, m):
                if m == 0:
                    pe.wait_ge(xn_split, it + 1)
                pe.wait_ge(relu_done, it * HT + (m + 1))
                ws = slice(m * P, (m + 1) * P)
                for k in range(KT):
                    last = split_mm(pe, pf[m % 2][:, :], (wfc[0][:, k, ws], wfc[1][:, k, ws]),
                                    (xn[0][:, k, :], xn[1][:, k, :]), k == 0, k == KT - 1)
                last.then_inc(fc_mm, 1)

            def proj(it, m):
                pe.wait_ge(r_split, it * HT + (m + 3))
                if m == 0:
                    pe.wait_ge(xf_ready, it + 1)
                for i in range(TT):
                    for n, part in enumerate((r_hi, r_lo)):
                        last = pe.matmul(pp[:, i, :], part[m % 2][:, i * P:(i + 1) * P], wproj[:, m, :],
                                         start=(m == 0 and n == 0 and i % 2 == 0), stop=(m == HT - 1 and n == 1),
                                         skip_group_check=True)
                last.then_inc(proj_mm, 1)

            for order in range(ORDERS):
                def body(m, it):
                    for g in range(GPI):
                        G = it * GPI + g
                        y = py[g % 2]

                        def conv(slot, q, block_):
                            for c in range(TC):
                                for A in range(NEAR * block_, NEAR * block_ + NEAR):
                                    j = A - NEAR * block_
                                    if order == 0:
                                        j = NEAR - 1 - j
                                    last = pe.matmul(y[:, q * TC + c, :, A:NA], T[:, slot, c, j * P:(j + 1) * P],
                                                     V[:, bass.ds(m * (GPI * GC) + (g * GC + q * TC + c), 1), :, 0:NA - A]
                                                     .rearrange("p c n a -> p (c n) a"),
                                                     start=(q == 0 and c == 0 and A == 0), stop=True, skip_group_check=True)
                            return last

                        def near(q):
                            pe.wait_ge(T_loaded[q], G * 16 + 16)
                            conv(q, q, 0).then_inc(tile_mm, 1)

                        pe.wait_ge(y_out, G + 1)
                        near(0)
                        with pe.If(tail > 0):
                            for j in range(FAR):
                                pe.wait_ge(far_loaded, G * (16 * FAR) + 16 * (j + 1))
                                conv(1, j % TILES, 1 + j // TILES).then_inc(far_used, 1)
                        fc(it, 2 * g)
                        near(1)
                        if g > 0:
                            proj(it, 2 * g - 1)
                        fc(it, 2 * g + 1)
                        near(2)
                        near(3)
                        proj(it, 2 * g)
                    proj(it, HT - 1)
                groups(pe, order, body)


def output_stage(nc, out, out_w, gc2_hbm, xf_hbm, ident, V):
    with ExitStack() as ctx:
        def sb(name, shape, dt=F32):
            return ctx.enter_context(nc.sbuf_tensor(name, shape, dt))

        def sem(name):
            return ctx.enter_context(nc.semaphore(name))

        wo = sb("wo", [P, KT, D])
        ys = [sb(f"ys{i}", [P, TT, D]) for i in range(2)]
        gc2 = [sb(f"gc2_{i}", [P, KT, CH]) for i in range(2)]
        yg = [sb(f"yg{i}", [P, KT, CH]) for i in range(2)]
        xf = [sb(f"xf{i}", [P, TT, D]) for i in range(2)]
        pT = [ctx.enter_context(nc.psum_tensor(f"pyT{i}", [P, KT, CH], F32)) for i in range(2)]
        po = [ctx.enter_context(nc.psum_tensor(f"po{i}", [P, TT, D], F32)) for i in range(2)]

        wo_in = sem("wo_in")
        sp_passed, pool_passed = sem("sp_passed"), sem("pool_passed")
        ys_ready = sem("ys_ready")
        yT_mm = sem("yT_mm")
        gc2_loaded = [sem(f"gc2_loaded{i}") for i in range(2)]
        xf_loaded = [sem(f"xf_loaded{i}") for i in range(2)]
        yg_ready = sem("yg_ready")
        out_mm = sem("out_mm")
        out_ready = sem("out_ready")
        out_saved = [sem(f"out_saved{i}") for i in range(2)]
        block = ctx.enter_context(nc.Block())
        out_tiles = out.rearrange("n (q i p) d -> (n q) p i d", i=TT, p=P)

        @block.sync
        def _(sp):
            sp.dma_start(wo[:, :, :], out_w.rearrange("(k p) c -> p k c", p=P)).then_inc(wo_in, 16)

            def load(m, first):
                for i in range(2):
                    c = m * 2 + i
                    if not first:
                        wait_alone(sp, yg_ready, c + 1, sp_passed)
                    sp.dma_start(gc2[i][:, :, :], gc2_hbm[bass.ds(c, 1)].rearrange("c p k t -> (c p) k t")).then_inc(gc2_loaded[i], 16)
                    if not first:
                        wait_alone(sp, out_saved[i], m * 16, sp_passed)
                    sp.dma_start(xf[i][:, :, :], xf_hbm[bass.ds(c, 1)].rearrange("c p i d -> (c p) i d")).then_inc(xf_loaded[i], 16)

            load(0, True)
            with sp.Fori(1, NCH // 2) as m:
                load(m, False)

        @block.gpsimd
        def _(pool):
            with pool.Fori(0, NCH // 2) as m:
                for i in range(2):
                    c = m * 2 + i
                    wait_alone(pool, out_ready, c + 3, pool_passed)
                    pool.dma_start(out_tiles[bass.ds(c, 1)].rearrange("c p i d -> (c p) i d"), xf[i][:, :, :]).then_inc(out_saved[i], 16)
            for i in range(2):
                pool.wait_ge(out_saved[i], 8 * NCH)

        @block.scalar
        def _(act):
            act.sem_inc(yT_mm, 2)
            with act.Fori(0, B) as n:
                for k in range(CPB):
                    c = n * CPB + k
                    act.wait_ge(yT_mm, c + 1)
                    act.activation(ys[k % 2][:, :, :].rearrange("p i c -> p c i"),
                                   V[:, :, bass.ds(n, 1), TT * k:TT * k + TT].rearrange("p c n a -> p c (n a)"),
                                   ACT.Copy).then_inc(ys_ready, 1)

        @block.vector
        def _(dve):
            dve.sem_inc(yg_ready, 2)
            dve.sem_inc(out_ready, 2)
            dve.sem_inc(out_mm, 2)
            with dve.Fori(0, NCH // 2) as m:
                for i in range(2):
                    c = m * 2 + i
                    dve.wait_ge(yT_mm, c + 3)
                    dve.wait_ge(gc2_loaded[i], m * 16 + 16)
                    dve.wait_ge(out_mm, c + 1)
                    dve.tensor_tensor(yg[i][:, :, :], pT[i][:, :, :], gc2[i][:, :, :], ALU.mult).then_inc(yg_ready, 1)
                    dve.wait_ge(out_mm, c + 3)
                    dve.wait_ge(xf_loaded[i], m * 16 + 16)
                    dve.tensor_tensor(xf[i][:, :, :], po[i][:, :, :], xf[i][:, :, :], ALU.add).then_inc(out_ready, 1)

        @block.tensor
        def _(pe):
            pe.wait_ge(wo_in, 16)
            with pe.Fori(0, NCH // 2) as m:
                for i in range(2):
                    c = m * 2 + i
                    pe.wait_ge(ys_ready, c + 1)
                    pe.wait_ge(yg_ready, c + 1)
                    for k in range(KT):
                        for t in range(TT):
                            last = pe.transpose(pT[i][:, k, t * P:(t + 1) * P], ys[i][:, t, k * P:(k + 1) * P], ident[:, :])
                    last.then_inc(yT_mm, 1)
                    pe.wait_ge(yg_ready, c + 3)
                    pe.wait_ge(out_ready, c + 1)
                    for t in range(TT):
                        for k in range(KT):
                            last = pe.matmul(po[i][:, t, :], yg[i][:, k, t * P:(t + 1) * P], wo[:, k, :], start=(k == 0), stop=(k == KT - 1))
                    last.then_inc(out_mm, 1)


def conv_ffn_kernel(nc, x, in_w, in_b, out_w, out_b, freqs, w1, b1, w2, b2, w3, b3, decay, conv_w, conv_b,
                    gate_w, gate_b, fast_b, w_fc, w_proj, u, v, gate, out):
    filters = nc.dram_tensor("filters", [ORDERS * D, PADDED], F32).ap()
    fc_hi = nc.dram_tensor("fc_hi", [P, KT, HID], F32).ap()
    fc_lo = nc.dram_tensor("fc_lo", [P, KT, HID], F32).ap()
    proj_t = nc.dram_tensor("proj_t", [P, HT, D], F32).ap()
    xnT_hbm = nc.dram_tensor("xnT_hbm", [NCH, P, KT, CH], F32).ap()
    gc2_hbm = nc.dram_tensor("gc2_hbm", [NCH, P, KT, CH], F32).ap()
    xf_hbm = nc.dram_tensor("xf_hbm", [NCH, P, TT, D], F32).ap()

    with ExitStack() as ctx:
        def sb(name, shape, dt=F32):
            return ctx.enter_context(nc.sbuf_tensor(name, shape, dt))

        ident = sb("ident", [P, P])
        bv_row, srow = sb("bv_row", [P, D]), sb("srow", [P, D])
        flag = sb("flag", [1, 1], I32)
        eps, half = sb("eps", [P, TT]), sb("half", [P, TT])
        V = sb("V", [P, D, B, NA])
        GC1 = sb("GC1", [P, D, B, NA])
        with ExitStack() as weights:
            Win = [weights.enter_context(nc.sbuf_tensor(f"win_{part}", [P, KT, 3 * D], F32R)) for part in ("hi", "lo")]
            Wgate = [weights.enter_context(nc.sbuf_tensor(f"wgate_{part}", [P, ORDERS * KT, D], F32R)) for part in ("hi", "lo")]
            hbm = (in_w, in_b, out_b, freqs, w1, b1, w2, b2, w3, b3, decay, gate_w, fast_b, w_fc, w_proj, u, v, gate,
                   filters, fc_hi, fc_lo, proj_t)
            setup_stage(nc, hbm, ident, bv_row, srow, flag, V, GC1, Win, Wgate, eps, half)
            project_stage(nc, x, xnT_hbm, gc2_hbm, in_b, conv_w, conv_b, gate_b, ident, bv_row, V, GC1, Win, Wgate, eps, half)
        mix_stage(nc, x, filters, fc_hi, fc_lo, proj_t, xnT_hbm, xf_hbm, out_b, srow, flag, V, GC1)
        output_stage(nc, out, out_w, gc2_hbm, xf_hbm, ident, V)


_INS = ["attn_x", "attn_in_proj_w", "attn_in_proj_b", "attn_out_proj_w", "attn_out_proj_b", "attn_freqs",
        "attn_mlp_w1", "attn_mlp_b1", "attn_mlp_w2", "attn_mlp_b2", "attn_mlp_w3", "attn_mlp_b3", "attn_decay",
        "attn_conv_w", "attn_conv_b", "attn_gate_w", "attn_gate_b", "ffn_fast_b", "ffn_w_fc", "ffn_w_proj",
        "ffn_u", "ffn_v", "ffn_gate"]


def kernel(**inputs):
    import numpy as _np
    import concourse.bacc as _bacc
    from concourse import mybir as _mybir
    from concourse.bass_utils import run_bass_kernel_spmd as _run

    nc = _bacc.Bacc("TRN2", target_bir_lowering=False, num_devices=1)
    arrays, args = {}, []
    for name in _INS:
        a = _np.ascontiguousarray(inputs["L0_" + name])
        arrays[f"in_{name}"] = a
        args.append(nc.dram_tensor(f"in_{name}", a.shape, _mybir.dt.from_np(a.dtype), kind="ExternalInput").ap())
    args.append(nc.dram_tensor("out_0", (B, L, D), F32, kind="ExternalOutput").ap())
    conv_ffn_kernel(nc, *args)
    r = _run(nc, [arrays], core_ids=[0])
    return r.results[0]["out_0"]
```

```python
from contextlib import ExitStack

import concourse.bass as bass
from concourse import mybir

F32 = mybir.dt.float32
F32R = mybir.dt.float32r
I32 = mybir.dt.int32
ALU = mybir.AluOpType
ACT = mybir.ActivationFunctionType
AX = mybir.AxisListType

P = 128
B, L, D = 4, 2048, 256
KT = D // P
HID, RANK = 1024, 16
HT = HID // P
ORDERS, FO, EMB = 2, 64, 3
CH = 512
TT = CH // P
CPB = L // CH
NCH = B * CPB
NA = L // P
COLS = B * NA
PADDED = P - 1 + L
NEAR = 3
MID_FROM = (NEAR - 1) * P + 1
FAR_FROM = NEAR * P + 1
FARS = (NA - NEAR - 1) // NEAR
GC = 8
TC = 2
TILES = GC // TC
GROUPS = ORDERS * D // GC
GPI = D // GC // (NCH // ORDERS)
ITERS = NCH // ORDERS
ROUND = 12582912.0
TWO_PI = 6.283185
LEAST_NORMAL = 1.17549435e-38


def setup_stage(nc, hbm, ident, bv_row, srow, flag, V, GC1, Win, Wgate, eps, half):
    (in_w, in_b, out_b, freqs, w1, b1, w2, b2, w3, b3, decay, gate_w, fast_b, w_fc, w_proj, u, v, gate,
     filters, fc_hi, fc_lo, proj_t) = hbm
    with ExitStack() as ctx:
        def sb(name, shape, dt=F32):
            return ctx.enter_context(nc.sbuf_tensor(name, shape, dt))

        def sem(name):
            return ctx.enter_context(nc.semaphore(name))

        Vf = V[:, :, :, :].rearrange("p c n a -> p (c n a)")
        Gf = GC1[:, :, :, :].rearrange("p c n a -> p (c n a)")
        hT = Vf[:, 0:4 * L].rearrange("p (w j) -> p w j", w=4)
        fc_nat = Vf[:, 8192:10240].rearrange("p (m d) -> p m d", m=HT)
        weff = Vf[:, 8192:10240].rearrange("p (k h) -> p k h", k=KT)
        fc_tern = Vf[:, 10240:12288].rearrange("p (m d) -> p m d", m=HT)
        pr_nat = Vf[:, 12288:14336].rearrange("p (k h) -> p k h", k=KT)
        pr_tern = Vf[:, 14336:16384].rearrange("p (k h) -> p k h", k=KT)
        t = Gf[:, 0:2 * L].rearrange("p (o j) -> p o j", o=ORDERS)
        enc = Gf[0:2 * EMB, 2 * L:4 * L].rearrange("p (o j) -> p o j", o=ORDERS)
        h1 = Gf[0:FO, 4 * L:6 * L].rearrange("p (o j) -> p o j", o=ORDERS)
        h2 = Gf[0:FO, 6 * L:8 * L].rearrange("p (o j) -> p o j", o=ORDERS)

        jint = Gf[:, 4 * L:6 * L].bitcast(I32).rearrange("p (o j) -> p o j", o=ORDERS)
        rnd = Gf[0:2 * EMB, 4 * L:5 * L]
        prow = sb("prow", [2 * EMB, 1], I32)
        prow_f = sb("prow_f", [2 * EMB, 1])
        phase = sb("phase", [2 * EMB, 1])
        f6 = sb("f6", [2 * EMB, ORDERS])
        w1sc = sb("w1sc", [2 * EMB, ORDERS, FO])
        w1t = sb("w1t", [1, ORDERS, FO])
        w2s = sb("w2s", [FO, ORDERS, FO])
        w3s = sb("w3s", [FO, ORDERS, D])
        b1s = sb("b1s", [FO, ORDERS])
        b2s = sb("b2s", [FO, ORDERS])
        b3s = sb("b3s", [P, ORDERS * KT])
        dec = sb("dec", [P, ORDERS * KT])
        ndec = sb("ndec", [P, ORDERS * KT])
        zpad = sb("zpad", [P, 4, P - 1])
        ones = sb("ones", [P, P])
        win_f = sb("win_f", [P, KT, 3 * D])
        gw_f = sb("gw_f", [P, ORDERS * KT, D])
        us = sb("us", [P, HT, RANK])
        vs = sb("vs", [RANK, D])
        fbT = sb("fbT", [RANK, RANK])
        gcol = sb("gcol", [P, 1])
        uT = sb("uT", [RANK, HID])
        m1 = sb("m1", [RANK, D])
        fsc = sb("fsc", [P, HT])
        fth = sb("fth", [P, 2 * HT])
        psc = sb("psc", [P, KT])
        pth = sb("pth", [P, 2 * KT])
        diag = sb("diag", [P, KT, P])
        weff_hi = sb("weff_hi", [P, KT, HID], F32R)
        weff_lo = sb("weff_lo", [P, KT, HID], F32R)
        projT = sb("projT", [P, HT, D], F32R)
        peaks = sb("peaks", [P, 2, 4])
        reach = sb("reach", [1, 1 + GROUPS])
        ps = ctx.enter_context(nc.psum_tensor("ps_setup", [P, 8, 512], F32))

        filter_in, weights_in = sem("filter_in"), sem("weights_in")
        FILTER_LOADS, WEIGHT_LOADS = 22, 8
        ident_zero, ident_ready, iota_ready = sem("ident_zero"), sem("ident_ready"), sem("iota_ready")
        dve_step = sem("dve_step")
        angle_ready, enc_ready = sem("angle_ready"), sem("enc_ready")
        ndec_ready, win_ready, h_ready, pad_ready = sem("ndec_ready"), sem("win_ready"), sem("h_ready"), sem("pad_ready")
        l1_mm, l2_mm, l3_mm = sem("l1_mm"), sem("l2_mm"), sem("l3_mm")
        h1_ready, h2_ready = sem("h1_ready"), sem("h2_ready")
        uT_mm, m1_mm, rank_ready = sem("uT_mm"), sem("m1_mm"), sem("rank_ready")
        tern_ready, fcT_mm, lr_mm, fcT_read, lr_read = sem("tern_ready"), sem("fcT_mm"), sem("lr_mm"), sem("fcT_read"), sem("lr_read")
        weff_ready, weff_hi_ready, weff_lo_ready = sem("weff_ready"), sem("weff_hi_ready"), sem("weff_lo_ready")
        projT_mm, proj_ready, srow_mm, diag_ready = sem("projT_mm"), sem("proj_ready"), sem("srow_mm"), sem("diag_ready")
        peak_ready, peakT_mm = sem("peak_ready"), sem("peakT_mm")
        hi_ready = sem("hi_ready")
        stored = sem("stored")
        ctx.enter_context(nc.allow_non_contiguous_dma(reason="a few small vectors, one value a partition"))
        block = ctx.enter_context(nc.Block())

        @block.sync
        def _(sp):
            def load(dst, src, s):
                sp.dma_start(dst, src).then_inc(s, 16)

            for o in range(ORDERS):
                for half_ in range(2):
                    load(f6[half_ * EMB:(half_ + 1) * EMB, o:o + 1], freqs[o:o + 1, :].rearrange("o k -> k o"), filter_in)
                load(w1sc[:, o, :], w1[o, 0:2 * EMB, :], filter_in)
                load(w1t[:, o, :], w1[o, 2 * EMB:2 * EMB + 1, :], filter_in)
                load(w2s[:, o, :], w2[o], filter_in)
                load(w3s[:, o, :], w3[o], filter_in)
                load(b1s[:, o:o + 1], b1[o:o + 1, :].rearrange("o f -> f o"), filter_in)
                load(b2s[:, o:o + 1], b2[o:o + 1, :].rearrange("o f -> f o"), filter_in)
                load(b3s[:, KT * o:KT * o + KT], b3[o, :].rearrange("(c p) -> p c", p=P), filter_in)
                load(dec[:, KT * o:KT * o + KT], decay[o, :].rearrange("(c p) -> p c", p=P), filter_in)
                load(gw_f[:, KT * o:KT * o + KT, :], gate_w[o].rearrange("(k p) c -> p k c", p=P), filter_in)
            load(us[:, :, :], u.rearrange("(m p) r -> p m r", p=P), weights_in)
            load(vs[:, :], v, weights_in)
            load(fbT[:, :], fast_b.rearrange("i j -> j i"), weights_in)
            load(gcol[:, :], bass.AP(gate.tensor, 0, [[0, P], [1, 1]]), weights_in)
            load(fc_nat, w_fc.rearrange("(m p) d -> p m d", p=P), weights_in)
            load(pr_nat, w_proj.rearrange("(k p) h -> p k h", p=P), weights_in)
            load(win_f[:, :, :], in_w.rearrange("(k p) c -> p k c", p=P), weights_in)
            load(bv_row[:, :], bass.AP(in_b.tensor, 0, [[0, P], [1, D]]), weights_in)
            sp.wait_ge(pad_ready, 1)
            rows = filters.rearrange("(w p) j -> p w j", p=P)
            load(rows[:, 0:KT, L:PADDED], zpad[:, 0:KT, :], stored)
            load(rows[:, KT:2 * KT, 0:P - 1], zpad[:, KT:2 * KT, :], stored)
            for w in range(4):
                sp.wait_ge(h_ready, w + 1)
                at = 0 if w < KT else P - 1
                load(filters[w * P:(w + 1) * P, at:at + L], hT[:, w, :], stored)
            sp.wait_ge(weff_hi_ready, 1)
            load(fc_hi, weff_hi[:, :, :].bitcast(F32), stored)
            sp.wait_ge(weff_lo_ready, 1)
            load(fc_lo, weff_lo[:, :, :].bitcast(F32), stored)
            sp.wait_ge(proj_ready, 1)
            load(proj_t, projT[:, :, :].bitcast(F32), stored)
            sp.wait_ge(stored, 16 * 9)

        @block.gpsimd
        def _(pool):
            pool.memset(ident[:, :], 0.0).then_inc(ident_zero, 1)
            pool.wait_ge(ident_zero, 1)
            pool.affine_select(out=ident[:, :], in_=ident[:, :], compare_op=ALU.not_equal, fill=1.0, base=0,
                               pattern=[[-1, P]], channel_multiplier=1).then_inc(ident_ready, 1)
            pool.iota(jint[:, 0, :], [[-1, L]], base=L - 1, channel_multiplier=0).then_inc(iota_ready, 1)
            pool.iota(jint[:, 1, :], [[1, L]], base=0, channel_multiplier=0).then_inc(iota_ready, 1)
            pool.iota(prow[:, :], [[0, 1]], base=0, channel_multiplier=1).then_inc(iota_ready, 1)
            pool.memset(eps[:, :], 1e-5).then_inc(iota_ready, 1)
            pool.memset(half[:, :], -0.5).then_inc(iota_ready, 1)

        @block.vector
        def _(dve):
            steps = [0]

            def link(ins):
                steps[0] += 1
                ins.then_inc(dve_step, 1)
                dve.wait_ge(dve_step, steps[0])

            dve.memset(zpad[:, :, :], 0.0).then_inc(pad_ready, 1)
            dve.wait_ge(iota_ready, 5)
            link(dve.tensor_copy(t, jint))
            link(dve.tensor_scalar(t, t, 1.0 / (L - 1), None, ALU.mult))
            link(dve.tensor_copy(prow_f[:, :], prow[:, :]))
            link(dve.tensor_scalar(phase[:, :], prow_f[:, :], float(EMB), 0.25, ALU.is_ge, ALU.mult))
            dve.wait_ge(filter_in, 16 * FILTER_LOADS)
            for o in range(ORDERS):
                link(dve.tensor_scalar(enc[:, o, :], t[0:2 * EMB, o, :], f6[:, o:o + 1], phase[:, :], ALU.mult, ALU.add))
                link(dve.tensor_scalar(rnd, enc[:, o, :], ROUND, None, ALU.add))
                link(dve.tensor_scalar(rnd, rnd, ROUND, None, ALU.subtract))
                dve.tensor_tensor(enc[:, o, :], enc[:, o, :], rnd, ALU.subtract).then_inc(angle_ready, 1)
            link(dve.tensor_scalar(ndec[:, :], dec[:, :], -1.0, None, ALU.mult))
            link(dve.tensor_tensor(ndec[:, :], ndec[:, :], dec[:, :], ALU.min))
            link(dve.tensor_scalar(ndec[:, :], ndec[:, :], float(L), None, ALU.mult))
            dve.memset(ones[:, :], 1.0).then_inc(ndec_ready, 1)
            dve.wait_ge(weights_in, 16 * WEIGHT_LOADS)
            dve.wait_ge(uT_mm, 1)
            dve.tensor_copy(uT[:, :], ps[0:RANK, 0:2, :].rearrange("p a b -> p (a b)"))
            dve.wait_ge(m1_mm, 1)
            dve.tensor_scalar(m1[:, :], ps[0:RANK, 2, 0:D], gcol[0:RANK, :], None, ALU.mult).then_inc(rank_ready, 1)
            for nat, tern, sc, th, m, width in ((fc_nat, fc_tern, fsc, fth, HT, D), (pr_nat, pr_tern, psc, pth, KT, HID)):
                link(dve.tensor_reduce(sc[:, :], nat, AX.X, ALU.add, apply_absolute_value=True))
                link(dve.tensor_scalar(sc[:, :], sc[:, :], 1.0 / width, 1e-5, ALU.mult, ALU.max))
                dve.tensor_scalar(th[:, 0:m], sc[:, :], 0.5, None, ALU.mult)
                link(dve.tensor_scalar(th[:, m:2 * m], sc[:, :], -0.5, None, ALU.mult))
                for i in range(m):
                    last = dve.tensor_scalar(tern[:, i, :], nat[:, i, :], th[:, m + i:m + i + 1], None, ALU.is_lt)
                link(last)
                for i in range(m):
                    last = dve.scalar_tensor_tensor(out=tern[:, i, :], in0=nat[:, i, :], scalar=th[:, i:i + 1],
                                                    in1=tern[:, i, :], op0=ALU.is_gt, op1=ALU.subtract)
                link(last)
            for i in range(HT):
                last = dve.tensor_scalar(fc_tern[:, i, :], fc_tern[:, i, :], fsc[:, i:i + 1], None, ALU.mult)
            last.then_inc(tern_ready, 1)
            dve.wait_ge(ident_ready, 1)
            for k in range(KT):
                last = dve.tensor_scalar(diag[:, k, :], ident[:, :], psc[:, k:k + 1], None, ALU.mult)
            last.then_inc(diag_ready, 1)
            dve.wait_ge(hi_ready, 2)
            dve.tensor_tensor(Win[1][:, :, :], win_f[:, :, :], Win[0][:, :, :].bitcast(F32), ALU.subtract)
            dve.tensor_tensor(Wgate[1][:, :, :], gw_f[:, :, :], Wgate[0][:, :, :].bitcast(F32), ALU.subtract)
            for w in range(4):
                dve.wait_ge(win_ready, w + 1)
                dve.wait_ge(l3_mm, w + 1)
                b4 = 4 * (w % 2)
                dve.scalar_tensor_tensor(out=hT[:, w, :], in0=ps[:, b4:b4 + 4, :].rearrange("p a b -> p (a b)"),
                                         scalar=b3s[:, w:w + 1], in1=hT[:, w, :], op0=ALU.add, op1=ALU.mult).then_inc(h_ready, 1)
            dve.wait_ge(h_ready, 4)
            for i, first in enumerate((MID_FROM, FAR_FROM)):
                dve.tensor_reduce(peaks[:, i, 0:KT], hT[:, 0:KT, 0:L - first], AX.X, ALU.max, apply_absolute_value=True)
                last = dve.tensor_reduce(peaks[:, i, KT:2 * KT], hT[:, KT:2 * KT, first:L], AX.X, ALU.max, apply_absolute_value=True)
            last.then_inc(peak_ready, 1)
            dve.wait_ge(fcT_mm, 1)
            link(dve.tensor_copy(Vf[:, 8192:10240], ps[:, 0:4, :].rearrange("p a b -> p (a b)")))
            dve.wait_ge(lr_mm, 1)
            dve.tensor_tensor(Vf[:, 8192:10240], Vf[:, 8192:10240],
                              ps[:, 4:8, :].rearrange("p a b -> p (a b)"), ALU.add).then_inc(weff_ready, 1)
            dve.wait_ge(weff_hi_ready, 1)
            dve.tensor_tensor(weff_lo[:, :, :], weff, weff_hi[:, :, :].bitcast(F32), ALU.subtract).then_inc(weff_lo_ready, 1)
            dve.wait_ge(projT_mm, 1)
            dve.tensor_copy(projT[:, :, :].rearrange("p m d -> p (m d)"), ps[:, 0:4, :].rearrange("p a b -> p (a b)")).then_inc(proj_ready, 1)
            dve.wait_ge(srow_mm, 1)
            dve.tensor_copy(srow[:, :], ps[:, 4, 0:D])
            dve.wait_ge(peakT_mm, 1)
            link(dve.tensor_reduce(reach[:, 0:1], ps[0:1, 6, :], AX.X, ALU.max))
            link(dve.tensor_reduce(reach[:, 1:1 + GROUPS], ps[0:1, 5, :].rearrange("p (g c) -> p g c", c=GC), AX.X, ALU.max))
            link(dve.tensor_scalar(reach[:, :], reach[:, :], LEAST_NORMAL, None, ALU.is_ge))
            link(dve.tensor_copy(flag[:, :], reach[:, :]))

        @block.scalar
        def _(act):
            for o in range(ORDERS):
                act.wait_ge(angle_ready, o + 1)
                act.activation(enc[:, o, :], enc[:, o, :], ACT.Sin, scale=TWO_PI).then_inc(enc_ready, 1)
            act.wait_ge(filter_in, 16 * FILTER_LOADS)
            for o in range(ORDERS):
                act.wait_ge(l1_mm, o + 1)
                act.activation(h1[:, o, :], ps[0:FO, 4 * o:4 * o + 4, :].rearrange("p a b -> p (a b)"), ACT.Gelu,
                               bias=b1s[:, o:o + 1]).then_inc(h1_ready, 1)
            for o in range(ORDERS):
                act.wait_ge(l2_mm, o + 1)
                act.activation(h2[:, o, :], ps[0:FO, 4 * o:4 * o + 4, :].rearrange("p a b -> p (a b)"), ACT.Gelu,
                               bias=b2s[:, o:o + 1]).then_inc(h2_ready, 1)
            act.wait_ge(ndec_ready, 1)
            for w in range(4):
                act.activation(hT[:, w, :], t[:, w // KT, :], ACT.Exp, scale=ndec[:, w:w + 1]).then_inc(win_ready, 1)
            act.wait_ge(weights_in, 16 * WEIGHT_LOADS)
            act.activation(Win[0][:, :, :], win_f[:, :, :], ACT.Copy).then_inc(hi_ready, 1)
            act.activation(Wgate[0][:, :, :], gw_f[:, :, :], ACT.Copy).then_inc(hi_ready, 1)
            act.wait_ge(weff_ready, 1)
            act.activation(weff_hi[:, :, :], weff, ACT.Copy).then_inc(weff_hi_ready, 1)

        @block.tensor
        def _(pe):
            pe.wait_ge(weights_in, 16 * WEIGHT_LOADS)
            pe.wait_ge(ident_ready, 1)
            for m in range(HT):
                last = pe.transpose(ps[0:RANK, m // 4, (m % 4) * P:(m % 4 + 1) * P], us[:, m, :], ident[:, :])
            last.then_inc(uT_mm, 1)
            pe.matmul(ps[0:RANK, 2, 0:D], fbT[:, :], vs[:, :], start=True, stop=True).then_inc(m1_mm, 1)
            pe.wait_ge(rank_ready, 1)
            pe.wait_ge(filter_in, 16 * FILTER_LOADS)
            for o in range(ORDERS):
                pe.wait_ge(enc_ready, o + 1)
                for j in range(4):
                    js = slice(j * 512, j * 512 + 512)
                    pe.matmul(ps[0:FO, 4 * o + j, :], w1sc[:, o, :], enc[:, o, js], start=True, stop=False)
                    last = pe.matmul(ps[0:FO, 4 * o + j, :], w1t[:, o, :], t[0:1, o, js], start=False, stop=True)
                last.then_inc(l1_mm, 1)
            for o in range(ORDERS):
                pe.wait_ge(h1_ready, o + 1)
                for j in range(4):
                    last = pe.matmul(ps[0:FO, 4 * o + j, :], w2s[:, o, :], h1[:, o, j * 512:j * 512 + 512], start=True, stop=True)
                last.then_inc(l2_mm, 1)
            pe.wait_ge(h2_ready, 2)
            for w in range(4):
                if w >= 2:
                    pe.wait_ge(h_ready, w - 1)
                o, c = w // KT, w % KT
                for j in range(4):
                    last = pe.matmul(ps[:, 4 * (w % 2) + j, :], w3s[:, o, c * P:(c + 1) * P], h2[:, o, j * 512:j * 512 + 512],
                                     start=True, stop=True)
                last.then_inc(l3_mm, 1)
            pe.wait_ge(tern_ready, 1)
            pe.wait_ge(h_ready, 3)
            for k in range(KT):
                for m in range(HT):
                    last = pe.transpose(ps[:, 2 * k + m // 4, (m % 4) * P:(m % 4 + 1) * P], fc_tern[:, m, k * P:(k + 1) * P], ident[:, :])
            last.then_inc(fcT_mm, 1)
            pe.wait_ge(h_ready, 4)
            for k in range(KT):
                for j in range(2):
                    last = pe.matmul(ps[:, 4 + 2 * k + j, :], m1[:, k * P:(k + 1) * P], uT[:, j * 512:j * 512 + 512],
                                     start=True, stop=True)
            last.then_inc(lr_mm, 1)
            pe.wait_ge(weff_ready, 1)
            for m in range(HT):
                for k in range(KT):
                    last = pe.transpose(ps[:, m // 2, (m % 2) * D + k * P:(m % 2) * D + (k + 1) * P],
                                        pr_tern[:, k, m * P:(m + 1) * P], ident[:, :])
            last.then_inc(projT_mm, 1)
            pe.wait_ge(diag_ready, 1)
            pe.matmul(ps[:, 4, 0:D], ones[:, :], diag[:, :, :].rearrange("p k c -> p (k c)"), start=True, stop=True).then_inc(srow_mm, 1)
            pe.wait_ge(peak_ready, 1)
            for i in range(2):
                for w in range(4):
                    last = pe.transpose(ps[0:1, 5 + i, w * P:(w + 1) * P], peaks[:, i, w:w + 1], ident[:, :])
            last.then_inc(peakT_mm, 1)


def wait_alone(eng, sem, value, passed):
    eng.wait_ge(sem, value)
    eng.sem_inc(passed, 1)


def split_mm(pe, out, w, x, start, stop, **more):
    pe.matmul(out, w[0], x[0], start=start, stop=False, **more)
    pe.matmul(out, w[1], x[0], start=False, stop=False, **more)
    return pe.matmul(out, w[0], x[1], start=False, stop=stop, **more)


def project_stage(nc, x, xnT_hbm, gc2_hbm, in_b, conv_w, conv_b, gate_b, ident, bv_row, V, GC1, Win, Wgate, eps, half):
    with ExitStack() as ctx:
        def sb(name, shape, dt=F32):
            return ctx.enter_context(nc.sbuf_tensor(name, shape, dt))

        def sem(name):
            return ctx.enter_context(nc.semaphore(name))

        xt = [sb(f"xt{i}", [P, TT, D]) for i in range(2)]
        norms = sb("norms", [P, TT, 11])
        stats, mv, ve, rs, nt = norms[:, :, 0:6], norms[:, :, 6:8], norms[:, :, 8], norms[:, :, 9], norms[:, :, 10]
        xn = [sb("xn_hi", [P, KT, CH], F32R), sb("xn_lo", [P, KT, CH], F32R)]
        ctrl = [sb(f"ctrl{i}", [P, 4, CH + 2]) for i in range(2)]
        xc = sb("xc", [P, 4, CH])
        xcs = [[sb(f"xc_{part}{o}", [P, KT, CH], F32R) for part in ("hi", "lo")] for o in range(ORDERS)]
        table = sb("table", [P, 1])
        taps = sb("taps", [P, 4, 6])
        kw, cb, kb, gb = taps[:, :, 0:3], taps[:, :, 3], taps[:, :, 4], taps[:, :, 5]
        pT = ctx.enter_context(nc.psum_tensor("pT", [P, KT, CH], F32))
        pn = ctx.enter_context(nc.psum_tensor("pn", [P, TT, D], F32))
        pc = ctx.enter_context(nc.psum_tensor("pc", [P, 4, CH], F32))

        bias_in = sem("bias_in")
        sp_passed, pool_passed, dve_passed = sem("sp_passed"), sem("pool_passed"), sem("dve_passed")
        x_loaded = [sem(f"x_loaded{i}") for i in range(2)]
        stat_done, aggr_done = sem("stat_done"), sem("aggr_done")
        rstd_step = sem("rstd_step")
        xn_ready = sem("xn_ready")
        xT_mm = sem("xT_mm")
        xn_hi_done, xn_split = sem("xn_hi_done"), sem("xn_split")
        xn_saved = [sem("xn_hi_saved"), sem("xn_lo_saved")]
        ctrl_mm, ctrl_copied = sem("ctrl_mm"), sem("ctrl_copied")
        v_mm, v_stored = sem("v_mm"), sem("v_stored")
        halo_done = sem("halo_done")
        tap0_done, tap1_done = sem("tap0_done"), sem("tap1_done")
        xc_ready = sem("xc_ready")
        xc_hi_done = sem("xc_hi_done")
        xc_split_dve, xc_split_pool = sem("xc_split_dve"), sem("xc_split_pool")
        gate_mm = sem("gate_mm")
        gate_done = sem("gate_done")
        gc_done = sem("gc_done")
        gcT_mm = sem("gcT_mm")
        gc1_stored = sem("gc1_stored")
        gc2_saved = sem("gc2_saved")
        ctx.enter_context(nc.allow_non_contiguous_dma(reason="a few small vectors, one value a partition"))
        block = ctx.enter_context(nc.Block())

        def steps(eng, step):
            step(-1, -1)
            step(0, 0)
            with eng.Fori(0, (NCH - 4) // 4) as m:
                batch_of[eng.engine] = m
                for j in range(4):
                    step(m * 4 + (j + 1), 1 + j)
            for s in range(NCH - 3, NCH + 1):
                step(s, s)

        batch_of = {}

        def batch(eng, s, s0):
            return s // CPB if isinstance(s, int) else batch_of[eng.engine] + s0 // CPB

        def tapped(buffer, c, k):
            at = 2 - k if c < KT else k
            return buffer[:, c, at:at + CH]

        def has(s0):
            return 0 <= s0 < NCH, s0 + 1 < NCH, s0 >= 1

        @block.sync
        def _(sp):
            sp.dma_start(cb, in_b[D:3 * D].rearrange("(c p) -> p c", p=P)).then_inc(bias_in, 16)
            for o in range(ORDERS):
                cs = slice(KT * o, KT * o + KT)
                for k in range(3):
                    sp.dma_start(kw[:, cs, k], conv_w[o, k, 0, :].rearrange("(c p) -> p c", p=P)).then_inc(bias_in, 16)
                sp.dma_start(kb[:, cs], conv_b[o, :].rearrange("(c p) -> p c", p=P)).then_inc(bias_in, 16)
                sp.dma_start(gb[:, cs], gate_b[o, :].rearrange("(c p) -> p c", p=P)).then_inc(bias_in, 16)
            sp.sem_inc(gc2_saved, 16)
            x_tiles = x.rearrange("n (q i p) d -> (n q) p i d", i=TT, p=P)

            def load_x(c, c0):
                sp.dma_start(xt[c0 % 2][:, :, :], x_tiles[bass.ds(c, 1)].rearrange("c p i d -> (c p) i d")).then_inc(x_loaded[c0 % 2], 16)

            load_x(0, 0)
            load_x(1, 1)

            def step(s, s0):
                front, ahead, back = has(s0)
                if s0 + 3 < NCH:
                    wait_alone(sp, xT_mm, s + 2, sp_passed)
                    load_x(s + 3, s0 + 3)
                if ahead:
                    for part, done in ((0, xn_hi_done), (1, xn_split)):
                        wait_alone(sp, done, s + 2, sp_passed)
                        sp.dma_start(xnT_hbm[part, bass.ds(s + 1, 1)].rearrange("c p k t -> (c p) k t"),
                                     xn[part][:, :, :].bitcast(F32)).then_inc(xn_saved[part], 16)
                if back:
                    wait_alone(sp, gc_done, 4 * s + 4, sp_passed)
                    sp.dma_start(gc2_hbm[bass.ds(s - 1, 1)].rearrange("c p k t -> (c p) k t"), xc[:, KT:2 * KT, :]).then_inc(gc2_saved, 16)

            steps(sp, step)
            for part in range(2):
                sp.wait_ge(xn_saved[part], 16 * NCH)
            sp.wait_ge(gc2_saved, 16 * NCH + 16)

        @block.gpsimd
        def _(pool):
            def rstd(c, first=False):
                r = 6 * c
                pool.wait_ge(aggr_done, 4 * c + 4)
                if not first:
                    pool.wait_ge(xn_ready, c)
                pool.tensor_tensor(ve, mv[:, :, 1], eps[:, :], ALU.add).then_inc(rstd_step, 1)
                pool.wait_ge(rstd_step, r + 1)
                pool.tensor_tensor(rs, ve, half[:, :], ALU.pow).then_inc(rstd_step, 1)
                pool.wait_ge(rstd_step, r + 2)
                pool.tensor_tensor(nt, rs, rs, ALU.mult).then_inc(rstd_step, 1)
                pool.wait_ge(rstd_step, r + 3)
                pool.tensor_tensor(nt, nt, ve, ALU.mult).then_inc(rstd_step, 1)
                wait_alone(pool, rstd_step, r + 4, pool_passed)
                pool.tensor_scalar(nt, nt, -0.5, 1.5, ALU.mult, ALU.add).then_inc(rstd_step, 1)
                pool.wait_ge(rstd_step, r + 5)
                pool.tensor_tensor(rs, rs, nt, ALU.mult).then_inc(rstd_step, 1)

            def step(s, s0):
                front, ahead, back = has(s0)
                if s0 + 2 < NCH:
                    rstd(s + 2)
                if back:
                    for c in (1, 3):
                        pool.wait_ge(xc_hi_done, 4 * s - 4 + c + 1)
                        pool.tensor_tensor(xcs[c // KT][1][:, c % KT, :], xc[:, c, :], xcs[c // KT][0][:, c % KT, :].bitcast(F32),
                                           ALU.subtract).then_inc(xc_split_pool, 1)
            rstd(0, True)
            steps(pool, step)

        @block.vector
        def _(dve):
            dve.sem_inc(gc1_stored, 1)
            dve.sem_inc(gc_done, 4)
            dve.sem_inc(xc_ready, 4)

            def statistics(c, c0):
                dve.wait_ge(x_loaded[c0 % 2], (c - c0 % 2) * 8 + 16)
                for i in range(TT):
                    dve.bn_stats(stats[:, i, :], xt[c0 % 2][:, i, :]).then_inc(stat_done, 1)
                for i in range(TT):
                    wait_alone(dve, stat_done, 4 * c + i + 1, dve_passed)
                    dve.bn_aggr(mv[:, i, :], stats[:, i, :]).then_inc(aggr_done, 1)

            def normalise(c, c0):
                dve.wait_ge(rstd_step, 6 * c + 6)
                buf = xt[c0 % 2]
                for i in range(TT):
                    last = dve.tensor_scalar(buf[:, i, :], buf[:, i, :], mv[:, i, 0:1], rs[:, i:i + 1], ALU.subtract, ALU.mult)
                last.then_inc(xn_ready, 1)

            def step(s, s0):
                front, ahead, back = has(s0)
                par, k = s0 % 2, s0 % 4

                def halo(o):
                    cs = slice(KT * o, KT * o + KT)
                    near, far, inner_far, inner_near = (0, CH + 1, CH, 1) if o else (CH + 1, 0, 1, CH)
                    if front:
                        dve.wait_ge(ctrl_copied, 4 * s + KT * o + KT)
                    if front and k == 0:
                        last = dve.memset(ctrl[par][:, cs, near:near + 1], 0.0)
                    elif front:
                        last = dve.tensor_copy(ctrl[par][:, cs, near:near + 1], ctrl[1 - par][:, cs, inner_far:inner_far + 1])
                    if back and k == 0:
                        last = dve.memset(ctrl[1 - par][:, cs, far:far + 1], 0.0)
                    elif back:
                        last = dve.tensor_copy(ctrl[1 - par][:, cs, far:far + 1], ctrl[par][:, cs, inner_near:inner_near + 1])
                    last.then_inc(halo_done, 1)

                def tap(o, k_, before, done):
                    for c in range(KT * o, KT * o + KT):
                        dve.wait_ge(before, 4 * s - 4 + c + 1)
                        dve.scalar_tensor_tensor(out=xc[:, c, :], in0=tapped(ctrl[1 - par], c, k_), scalar=kw[:, c, k_:k_ + 1],
                                                 in1=xc[:, c, :], op0=ALU.mult, op1=ALU.add).then_inc(done, 1)

                def low(c):
                    dve.wait_ge(xc_hi_done, 4 * s - 4 + c + 1)
                    dve.tensor_tensor(xcs[c // KT][1][:, c % KT, :], xc[:, c, :], xcs[c // KT][0][:, c % KT, :].bitcast(F32),
                                      ALU.subtract).then_inc(xc_split_dve, 1)

                def gated(c):
                    dve.wait_ge(gate_done, 4 * s - 4 + c + 1)
                    dve.tensor_tensor(xc[:, c, :], pc[:, c, :], xc[:, c, :], ALU.mult).then_inc(gc_done, 1)

                if s0 + 2 < NCH:
                    statistics(s + 2, s0 + 2)
                if s0 >= 0:
                    halo(0)
                if back:
                    tap(0, 1, tap0_done, tap1_done)
                    tap(0, 2, tap1_done, xc_ready)
                if s0 >= 0:
                    halo(1)
                if back:
                    low(0)
                    tap(1, 1, tap0_done, tap1_done)
                    tap(1, 2, tap1_done, xc_ready)
                    low(2)
                if front:
                    dve.wait_ge(v_mm, s + 1)
                    dve.tensor_tensor(V[:, :, bass.ds(batch(dve, s, s0), 1), TT * k:TT * k + TT].rearrange("p c n a -> p c (n a)"),
                                      pn[:, :, :].rearrange("p i c -> p c i"),
                                      bv_row[:, :].unsqueeze(2).broadcast_to([P, D, TT]), ALU.add).then_inc(v_stored, 1)
                if back:
                    gated(0)
                    gated(1)
                if ahead:
                    dve.wait_ge(xn_hi_done, s + 2)
                    if s0 >= 0:
                        dve.wait_ge(xn_saved[1], 16 * s + 16)
                    dve.tensor_tensor(xn[1][:, :, :], pT[:, :, :], xn[0][:, :, :].bitcast(F32), ALU.subtract).then_inc(xn_split, 1)
                if back:
                    gated(2)
                    gated(3)
                if s0 + 2 < NCH:
                    normalise(s + 2, s0 + 2)

            statistics(0, 0)
            normalise(0, 0)
            steps(dve, step)

        @block.scalar
        def _(act):
            act.activation(table[:, :], eps[:, 0:1], ACT.Sigmoid)
            act.wait_ge(bias_in, 16 * 11)

            def step(s, s0):
                front, ahead, back = has(s0)
                par = s0 % 2

                def controls(o):
                    if s0 >= 1 and o == 0:
                        act.wait_ge(xc_ready, 4 * s)
                    for c in range(KT * o, KT * o + KT):
                        act.wait_ge(ctrl_mm, 4 * s + c + 1)
                        act.activation(ctrl[par][:, c, 1:CH + 1], pc[:, c, ::-1] if c < KT else pc[:, c, :], ACT.Identity, bias=cb[:, c:c + 1]).then_inc(ctrl_copied, 1)

                def first_tap(o):
                    act.wait_ge(halo_done, 2 * s + o + 1)
                    if o == 0:
                        act.wait_ge(gcT_mm, s)
                    else:
                        act.wait_ge(gc2_saved, 16 * s)
                    for c in range(KT * o, KT * o + KT):
                        act.activation(xc[:, c, :], tapped(ctrl[1 - par], c, 0), ACT.Identity, bias=kb[:, c:c + 1],
                                       scale=kw[:, c, 0:1]).then_inc(tap0_done, 1)

                def high(o):
                    act.wait_ge(gate_mm, 4 * s - 4 + KT * o + KT)
                    for c in range(KT * o, KT * o + KT):
                        act.wait_ge(xc_ready, 4 * s + c + 1)
                        act.activation(xcs[o][0][:, c % KT, :], xc[:, c, :], ACT.Copy).then_inc(xc_hi_done, 1)

                def sigmoid(c):
                    act.wait_ge(gate_mm, 4 * s + c + 1)
                    act.activation(pc[:, c, :], pc[:, c, :], ACT.Sigmoid, bias=gb[:, c:c + 1]).then_inc(gate_done, 1)

                if front:
                    controls(0)
                if back:
                    first_tap(0)
                if front:
                    controls(1)
                if back:
                    high(0)
                    first_tap(1)
                    high(1)
                    sigmoid(0)
                    sigmoid(1)
                if ahead:
                    act.wait_ge(xT_mm, s + 2)
                    if s0 >= 0:
                        act.wait_ge(xn_saved[0], 16 * s + 16)
                    act.activation(xn[0][:, :, :], pT[:, :, :], ACT.Copy).then_inc(xn_hi_done, 1)
                if back:
                    sigmoid(2)
                    sigmoid(3)
                    act.wait_ge(gcT_mm, s + 1)
                    pk = (s0 - 1) % 4
                    act.activation(GC1[:, :, bass.ds(batch(act, s - 1, s0 - 1), 1), TT * pk:TT * pk + TT].rearrange("p c n a -> p c (n a)"),
                                   pn[:, :, :].rearrange("p i c -> p c i"), ACT.Copy).then_inc(gc1_stored, 1)

            steps(act, step)

        @block.tensor
        def _(pe):
            pe.sem_inc(gate_mm, 4)
            pe.sem_inc(gcT_mm, 1)

            def step(s, s0):
                front, ahead, back = has(s0)
                if front:
                    pe.wait_ge(xn_split, s + 1)
                    for c in range(4):
                        if s0 >= 1:
                            pe.wait_ge(gc_done, 4 * s - 4 + c + 1)
                        for k in range(KT):
                            ws = slice(D + c * P, D + (c + 1) * P)
                            last = split_mm(pe, pc[:, c, :], (Win[0][:, k, ws], Win[1][:, k, ws]),
                                            (xn[0][:, k, :], xn[1][:, k, :]), k == 0, k == KT - 1)
                        last.then_inc(ctrl_mm, 1)
                    if s0 >= 1:
                        pe.wait_ge(gc1_stored, s)
                    for i in range(TT):
                        ts = slice(i * P, (i + 1) * P)
                        for k in range(KT):
                            last = split_mm(pe, pn[:, i, :], (xn[0][:, k, ts], xn[1][:, k, ts]),
                                            (Win[0][:, k, 0:D], Win[1][:, k, 0:D]), k == 0, k == KT - 1)
                    last.then_inc(v_mm, 1)
                def gates(o):
                    pe.wait_ge(xc_split_dve, 2 * s - 2 + o + 1)
                    pe.wait_ge(xc_split_pool, 2 * s - 2 + o + 1)
                    for co in range(KT):
                        c = KT * o + co
                        if front:
                            pe.wait_ge(ctrl_copied, 4 * s + c + 1)
                        else:
                            pe.wait_ge(gc_done, 4 * s - 4 + c + 1)
                        for k in range(KT):
                            ws = slice(co * P, (co + 1) * P)
                            last = split_mm(pe, pc[:, c, :], (Wgate[0][:, KT * o + k, ws], Wgate[1][:, KT * o + k, ws]),
                                            (xcs[o][0][:, k, :], xcs[o][1][:, k, :]), k == 0, k == KT - 1)
                        last.then_inc(gate_mm, 1)
                if back:
                    gates(0)
                if ahead:
                    pe.wait_ge(xn_ready, s + 2)
                    if s0 >= 0:
                        pe.wait_ge(xn_split, s + 1)
                    for k in range(KT):
                        for i in range(TT):
                            last = pe.transpose(pT[:, k, i * P:(i + 1) * P], xt[(s0 + 1) % 2][:, i, k * P:(k + 1) * P], ident[:, :])
                    last.then_inc(xT_mm, 1)
                if back:
                    gates(1)
                    pe.wait_ge(gc_done, 4 * s + KT)
                    if front:
                        pe.wait_ge(v_stored, s + 1)
                    else:
                        pe.wait_ge(gc1_stored, s)
                    for i in range(TT):
                        for k in range(KT):
                            last = pe.transpose(pn[:, TT - 1 - i, k * P:(k + 1) * P], xc[:, k, i * P:(i + 1) * P], ident[:, :])
                    last.then_inc(gcT_mm, 1)

            steps(pe, step)


def mix_stage(nc, x, filters, fc_hi, fc_lo, proj_t, xnT_hbm, xf_hbm, out_b, srow, flag, V, GC1):
    with ExitStack() as ctx:
        def sb(name, shape, dt=F32):
            return ctx.enter_context(nc.sbuf_tensor(name, shape, dt))

        def sem(name):
            return ctx.enter_context(nc.semaphore(name))

        wfc = [sb("wfc_hi", [P, KT, HID], F32R), sb("wfc_lo", [P, KT, HID], F32R)]
        wproj = sb("wproj", [P, HT, D], F32R)
        T = sb("T", [P, TILES, TC, NEAR * P])
        Tmid = sb("Tmid", [P, GC, P])
        xn = [[sb(f"xm_{part}{i}", [P, KT, CH], F32R) for part in ("hi", "lo")] for i in range(2)]
        xb = sb("xb", [P, TT, D])
        bo_row = sb("bo_row", [P, D])
        r = [sb(f"r{i}", [P, CH]) for i in range(2)]
        r_hi = [sb(f"r_hi{i}", [P, CH], F32R) for i in range(2)]
        r_lo = [sb(f"r_lo{i}", [P, CH], F32R) for i in range(2)]
        py = [ctx.enter_context(nc.psum_tensor(f"py{i}", [P, GC, B, NA], F32)) for i in range(2)]
        pf = [ctx.enter_context(nc.psum_tensor(f"pf{i}", [P, CH], F32)) for i in range(2)]
        pp = ctx.enter_context(nc.psum_tensor("pp", [P, TT, D], F32))

        w_in, bo_in = sem("w_in"), sem("bo_in")
        sp_passed, pool_passed = sem("sp_passed"), sem("pool_passed")
        T_loaded = [sem(f"T_loaded{q}") for q in range(TILES)]
        tile_mm = sem("tile_mm")
        far_loaded, far_used = sem("far_loaded"), sem("far_used")
        y_out = sem("y_out")
        mid_loaded = sem("mid_loaded")
        xn_loaded = [sem(f"xn_loaded{i}") for i in range(2)]
        xb_loaded, xb_biased = sem("xb_loaded"), sem("xb_biased")
        scaled, xf_saved = sem("scaled"), sem("xf_saved")
        xf_ready = sem("xf_ready")
        fc_mm = sem("fc_mm")
        relu_done = sem("relu_done")
        sq_done, r_hi_done = sem("sq_done"), sem("r_hi_done")
        r_split = sem("r_split")
        proj_mm = sem("proj_mm")
        ctx.enter_context(nc.allow_non_contiguous_dma(reason="a few small vectors, one value a partition"))
        block = ctx.enter_context(nc.Block())

        hankel = bass.AP(filters.tensor, 0, [[1, P], [PADDED, ORDERS * D], [1, L]])
        FAR = FARS * TILES

        def groups(eng, order, body):
            with eng.Fori(0, ITERS // 2) as half_m:
                for i in range(2):
                    body(half_m * 2 + i, half_m * 2 + (i + ITERS * order), i)

        def lags(order, A0, count):
            return P * (NA - A0 - count) if order == 0 else P * A0

        @block.sync
        def _(sp):
            for dst, src in ((wfc[0], fc_hi), (wfc[1], fc_lo), (wproj, proj_t)):
                sp.dma_start(dst[:, :, :].bitcast(F32), src).then_inc(w_in, 16)
            sp.sem_inc(tile_mm, TILES)
            sp.sem_inc(mid_loaded, 16)
            tail = sp.value_load(flag[0:1, 0:1], min_val=0, max_val=1)
            for order in range(ORDERS):
                def body(m, it, i):
                    for g in range(GPI):
                        G = it * GPI + g
                        row = m * (GPI * GC) + (order * D + g * GC)

                        def load(slot, q, A0, s):
                            first = lags(order, A0, NEAR)
                            sp.dma_start(T[:, slot, :, :], hankel[:, bass.ds(row + q * TC, TC), first:first + NEAR * P]).then_inc(s, 16)

                        wait_alone(sp, tile_mm, G * TILES + 1, sp_passed)
                        load(0, 0, 0, T_loaded[0])
                        wait_alone(sp, tile_mm, G * TILES + 2, sp_passed)
                        middle = sp.value_load(flag[0:1, bass.ds(G + 1, 1)], min_val=0, max_val=1)
                        with sp.If(middle > 0):
                            first = lags(order, NEAR, 1)
                            sp.dma_start(Tmid[:, :, :], hankel[:, bass.ds(row, GC), first:first + P]).then_inc(mid_loaded, 16)
                        with sp.Else():
                            wait_alone(sp, mid_loaded, G * 16 + 16, sp_passed)
                            sp.sem_inc(mid_loaded, 16)
                        with sp.If(tail > 0):
                            for j in range(FAR):
                                load(1, j % TILES, NEAR + 1 + NEAR * (j // TILES), far_loaded)
                                wait_alone(sp, far_used, G * FAR + (j + 1), sp_passed)
                        for q in range(1, TILES):
                            if q > 1:
                                wait_alone(sp, tile_mm, G * TILES + q + 1, sp_passed)
                            load(q, q, 0, T_loaded[q])
                groups(sp, order, body)

        @block.gpsimd
        def _(pool):
            x_tiles = x.rearrange("n (q i p) d -> (n q) p i d", i=TT, p=P)

            def load_xn(c, i):
                for part in range(2):
                    pool.dma_start(xn[i][part][:, :, :].bitcast(F32), xnT_hbm[part, bass.ds(c, 1)].rearrange("c p k t -> (c p) k t")).then_inc(xn_loaded[i], 16)

            def load_xb(it):
                pool.dma_start(xb[:, :, :], x_tiles[bass.ds(it, 1)].rearrange("c p i d -> (c p) i d")).then_inc(xb_loaded, 16)
                wait_alone(pool, xb_loaded, it * 16 + 16, pool_passed)
                pool.tensor_tensor(xb[:, :, :], xb[:, :, :], bo_row[:, :].unsqueeze(1).broadcast_to([P, TT, D]), ALU.add).then_inc(xb_biased, 1)

            def save_xf(it):
                wait_alone(pool, xf_ready, it + 2, pool_passed)
                pool.dma_start(xf_hbm[bass.ds(it, 1)].rearrange("c p i d -> (c p) i d"), xb[:, :, :]).then_inc(xf_saved, 16)
                wait_alone(pool, xf_saved, it * 16 + 16, pool_passed)

            pool.dma_start(bo_row[:, :], bass.AP(out_b.tensor, 0, [[0, P], [1, D]])).then_inc(bo_in, 16)
            pool.wait_ge(bo_in, 16)
            load_xn(0, 0)
            load_xn(1, 1)
            load_xb(0)
            with pool.Fori(0, NCH // 2 - 1) as pair:
                for i in range(2):
                    c = pair * 2 + (1 + i)
                    wait_alone(pool, fc_mm, c * HT + HT, pool_passed)
                    load_xn(c + 1, i)
                    save_xf(c - 1)
                    load_xb(c)
            save_xf(NCH - 2)
            load_xb(NCH - 1)
            save_xf(NCH - 1)

        @block.vector
        def _(dve):
            dve.sem_inc(y_out, 2)
            dve.sem_inc(r_split, 2)

            def finish(it):
                dve.wait_ge(proj_mm, it * HT + HT + 2)
                dve.tensor_tensor(pp[:, :, :], pp[:, :, :], srow[:, :].unsqueeze(1).broadcast_to([P, TT, D]), ALU.mult).then_inc(scaled, 1)
                dve.wait_ge(scaled, it + 1)
                dve.wait_ge(xb_biased, it + 1)
                dve.tensor_tensor(xb[:, :, :], pp[:, :, :], xb[:, :, :], ALU.add).then_inc(xf_ready, 1)

            def body(m, it, order):
                for g in range(GPI):
                    for j in range(2):
                        uu = it * HT + (2 * g + j)
                        dve.wait_ge(relu_done, uu + 3)
                        dve.tensor_tensor(r[j][:, :], r[j][:, :], r[j][:, :], ALU.mult).then_inc(sq_done, 1)
                        dve.wait_ge(r_hi_done, uu + 1)
                        dve.tensor_tensor(r_lo[j][:, :], r[j][:, :], r_hi[j][:, :].bitcast(F32), ALU.subtract).then_inc(r_split, 1)
                    G = it * GPI + g
                    c0 = m * (GPI * GC) + g * GC
                    out = V[:, bass.ds(c0, GC)].rearrange("p c n a -> p (c n a)")
                    y = py[g % 2][:, :, :, :].rearrange("p c n a -> p (c n a)")
                    dve.wait_ge(tile_mm, G * TILES + 2 * TILES)
                    if order == 0:
                        dve.tensor_tensor(out, y, GC1[:, bass.ds(c0, GC)].rearrange("p c n a -> p (c n a)"), ALU.mult).then_inc(y_out, 1)
                    else:
                        dve.tensor_copy(out, y).then_inc(y_out, 1)

                finish(it)

            for order in range(ORDERS):
                groups(dve, order, lambda m, it, i: body(m, it, order))

        @block.scalar
        def _(act):
            act.sem_inc(relu_done, 2)
            with act.Fori(0, NCH) as it:
                for m in range(HT):
                    uu, j = it * HT + m, m % 2
                    act.wait_ge(fc_mm, uu + HT + 1)
                    act.wait_ge(r_split, uu + 1)
                    act.activation(r[j][:, :], pf[j][:, :], ACT.Relu).then_inc(relu_done, 1)
                    act.wait_ge(sq_done, uu + 1)
                    act.wait_ge(proj_mm, uu + 1)
                    act.activation(r_hi[j][:, :], r[j][:, :], ACT.Copy).then_inc(r_hi_done, 1)

        @block.tensor
        def _(pe):
            pe.sem_inc(fc_mm, HT)
            pe.sem_inc(proj_mm, 2)
            pe.sem_inc(xf_ready, 1)
            tail = pe.value_load(flag[0:1, 0:1], min_val=0, max_val=1)
            pe.wait_ge(w_in, 16 * 3)

            def fc(it, m, i):
                if m == 0:
                    pe.wait_ge(xn_loaded[i], (it - i) * 16 + 32)
                pe.wait_ge(relu_done, it * HT + (m + 1))
                ws = slice(m * P, (m + 1) * P)
                for k in range(KT):
                    last = split_mm(pe, pf[m % 2][:, :], (wfc[0][:, k, ws], wfc[1][:, k, ws]),
                                    (xn[i][0][:, k, :], xn[i][1][:, k, :]), k == 0, k == KT - 1)
                last.then_inc(fc_mm, 1)

            def proj(it, m):
                pe.wait_ge(r_split, it * HT + (m + 3))
                if m == 0:
                    pe.wait_ge(xf_ready, it + 1)
                for i in range(TT):
                    for n, part in enumerate((r_hi, r_lo)):
                        last = pe.matmul(pp[:, i, :], part[m % 2][:, i * P:(i + 1) * P], wproj[:, m, :],
                                         start=(m == 0 and n == 0 and i % 2 == 0), stop=(m == HT - 1 and n == 1),
                                         skip_group_check=True)
                last.then_inc(proj_mm, 1)

            for order in range(ORDERS):
                def body(m, it, i):
                    for g in range(GPI):
                        G = it * GPI + g
                        y = py[g % 2]

                        def conv(tile, c, A0, count):
                            for A in range(A0, A0 + count):
                                j = A - A0 if order else A0 + count - 1 - A
                                last = pe.matmul(y[:, c, :, A:NA], tile[:, j * P:(j + 1) * P],
                                                 V[:, bass.ds(m * (GPI * GC) + (g * GC + c), 1), :, 0:NA - A]
                                                 .rearrange("p c n a -> p (c n) a"),
                                                 start=(c == 0 and A == 0), stop=True, skip_group_check=True)
                            return last

                        def near(q):
                            pe.wait_ge(T_loaded[q], G * 16 + 16)
                            for c in range(TC):
                                last = conv(T[:, q, c, :], q * TC + c, 0, NEAR)
                            last.then_inc(tile_mm, 1)

                        pe.wait_ge(y_out, G + 1)
                        near(0)
                        middle = pe.value_load(flag[0:1, bass.ds(G + 1, 1)], min_val=0, max_val=1)
                        with pe.If(middle > 0):
                            pe.wait_ge(mid_loaded, G * 16 + 32)
                            for c in range(GC):
                                conv(Tmid[:, c, :], c, NEAR, 1)
                        with pe.If(tail > 0):
                            for j in range(FAR):
                                pe.wait_ge(far_loaded, G * (16 * FAR) + 16 * (j + 1))
                                for c in range(TC):
                                    last = conv(T[:, 1, c, :], (j % TILES) * TC + c, NEAR + 1 + NEAR * (j // TILES), NEAR)
                                last.then_inc(far_used, 1)
                        fc(it, 2 * g, i)
                        near(1)
                        if g > 0:
                            proj(it, 2 * g - 1)
                        fc(it, 2 * g + 1, i)
                        near(2)
                        near(3)
                        proj(it, 2 * g)
                    proj(it, HT - 1)
                groups(pe, order, body)


def output_stage(nc, out, out_w, gc2_hbm, xf_hbm, ident, V):
    with ExitStack() as ctx:
        def sb(name, shape, dt=F32):
            return ctx.enter_context(nc.sbuf_tensor(name, shape, dt))

        def sem(name):
            return ctx.enter_context(nc.semaphore(name))

        wo = sb("wo", [P, KT, D])
        ys = [sb(f"ys{i}", [P, TT, D]) for i in range(2)]
        gc2 = [sb(f"gc2_{i}", [P, KT, CH]) for i in range(2)]
        yg = [sb(f"yg{i}", [P, KT, CH]) for i in range(2)]
        xf = [sb(f"xf{i}", [P, TT, D]) for i in range(2)]
        pT = [ctx.enter_context(nc.psum_tensor(f"pyT{i}", [P, KT, CH], F32)) for i in range(2)]
        po = [ctx.enter_context(nc.psum_tensor(f"po{i}", [P, TT, D], F32)) for i in range(2)]

        wo_in = sem("wo_in")
        sp_passed, pool_passed = sem("sp_passed"), sem("pool_passed")
        ys_ready = sem("ys_ready")
        yT_mm = sem("yT_mm")
        gc2_loaded = [sem(f"gc2_loaded{i}") for i in range(2)]
        xf_loaded = [sem(f"xf_loaded{i}") for i in range(2)]
        yg_ready = sem("yg_ready")
        out_mm = sem("out_mm")
        out_ready = sem("out_ready")
        out_saved = [sem(f"out_saved{i}") for i in range(2)]
        block = ctx.enter_context(nc.Block())
        out_tiles = out.rearrange("n (q i p) d -> (n q) p i d", i=TT, p=P)

        @block.sync
        def _(sp):
            sp.dma_start(wo[:, :, :], out_w.rearrange("(k p) c -> p k c", p=P)).then_inc(wo_in, 16)

            def load(m, first):
                for i in range(2):
                    c = m * 2 + i
                    if not first:
                        wait_alone(sp, yg_ready, c + 1, sp_passed)
                    sp.dma_start(gc2[i][:, :, :], gc2_hbm[bass.ds(c, 1)].rearrange("c p k t -> (c p) k t")).then_inc(gc2_loaded[i], 16)
                    if not first:
                        wait_alone(sp, out_saved[i], m * 16, sp_passed)
                    sp.dma_start(xf[i][:, :, :], xf_hbm[bass.ds(c, 1)].rearrange("c p i d -> (c p) i d")).then_inc(xf_loaded[i], 16)

            load(0, True)
            with sp.Fori(1, NCH // 2) as m:
                load(m, False)

        @block.gpsimd
        def _(pool):
            with pool.Fori(0, NCH // 2) as m:
                for i in range(2):
                    c = m * 2 + i
                    wait_alone(pool, out_ready, c + 3, pool_passed)
                    pool.dma_start(out_tiles[bass.ds(c, 1)].rearrange("c p i d -> (c p) i d"), xf[i][:, :, :]).then_inc(out_saved[i], 16)
            for i in range(2):
                pool.wait_ge(out_saved[i], 8 * NCH)

        @block.scalar
        def _(act):
            act.sem_inc(yT_mm, 2)
            with act.Fori(0, B) as n:
                for k in range(CPB):
                    c = n * CPB + k
                    act.wait_ge(yT_mm, c + 1)
                    act.activation(ys[k % 2][:, :, :].rearrange("p i c -> p c i"),
                                   V[:, :, bass.ds(n, 1), TT * k:TT * k + TT].rearrange("p c n a -> p c (n a)"),
                                   ACT.Copy).then_inc(ys_ready, 1)

        @block.vector
        def _(dve):
            dve.sem_inc(yg_ready, 2)
            dve.sem_inc(out_ready, 2)
            dve.sem_inc(out_mm, 2)
            with dve.Fori(0, NCH // 2) as m:
                for i in range(2):
                    c = m * 2 + i
                    dve.wait_ge(yT_mm, c + 3)
                    dve.wait_ge(gc2_loaded[i], m * 16 + 16)
                    dve.wait_ge(out_mm, c + 1)
                    dve.tensor_tensor(yg[i][:, :, :], pT[i][:, :, :], gc2[i][:, :, :], ALU.mult).then_inc(yg_ready, 1)
                    dve.wait_ge(out_mm, c + 3)
                    dve.wait_ge(xf_loaded[i], m * 16 + 16)
                    dve.tensor_tensor(xf[i][:, :, :], po[i][:, :, :], xf[i][:, :, :], ALU.add).then_inc(out_ready, 1)

        @block.tensor
        def _(pe):
            pe.wait_ge(wo_in, 16)
            with pe.Fori(0, NCH // 2) as m:
                for i in range(2):
                    c = m * 2 + i
                    pe.wait_ge(ys_ready, c + 1)
                    pe.wait_ge(yg_ready, c + 1)
                    for k in range(KT):
                        for t in range(TT):
                            last = pe.transpose(pT[i][:, k, t * P:(t + 1) * P], ys[i][:, t, k * P:(k + 1) * P], ident[:, :])
                    last.then_inc(yT_mm, 1)
                    pe.wait_ge(yg_ready, c + 3)
                    pe.wait_ge(out_ready, c + 1)
                    for t in range(TT):
                        for k in range(KT):
                            last = pe.matmul(po[i][:, t, :], yg[i][:, k, t * P:(t + 1) * P], wo[:, k, :], start=(k == 0), stop=(k == KT - 1))
                    last.then_inc(out_mm, 1)


def conv_ffn_kernel(nc, x, in_w, in_b, out_w, out_b, freqs, w1, b1, w2, b2, w3, b3, decay, conv_w, conv_b,
                    gate_w, gate_b, fast_b, w_fc, w_proj, u, v, gate, out):
    filters = nc.dram_tensor("filters", [ORDERS * D, PADDED], F32).ap()
    fc_hi = nc.dram_tensor("fc_hi", [P, KT, HID], F32).ap()
    fc_lo = nc.dram_tensor("fc_lo", [P, KT, HID], F32).ap()
    proj_t = nc.dram_tensor("proj_t", [P, HT, D], F32).ap()
    xnT_hbm = nc.dram_tensor("xnT_hbm", [2, NCH, P, KT, CH], F32).ap()
    gc2_hbm = nc.dram_tensor("gc2_hbm", [NCH, P, KT, CH], F32).ap()
    xf_hbm = nc.dram_tensor("xf_hbm", [NCH, P, TT, D], F32).ap()

    with ExitStack() as ctx:
        def sb(name, shape, dt=F32):
            return ctx.enter_context(nc.sbuf_tensor(name, shape, dt))

        ident = sb("ident", [P, P])
        bv_row, srow = sb("bv_row", [P, D]), sb("srow", [P, D])
        flag = sb("flag", [1, 1 + GROUPS], I32)
        eps, half = sb("eps", [P, TT]), sb("half", [P, TT])
        V = sb("V", [P, D, B, NA])
        GC1 = sb("GC1", [P, D, B, NA])
        with ExitStack() as weights:
            Win = [weights.enter_context(nc.sbuf_tensor(f"win_{part}", [P, KT, 3 * D], F32R)) for part in ("hi", "lo")]
            Wgate = [weights.enter_context(nc.sbuf_tensor(f"wgate_{part}", [P, ORDERS * KT, D], F32R)) for part in ("hi", "lo")]
            hbm = (in_w, in_b, out_b, freqs, w1, b1, w2, b2, w3, b3, decay, gate_w, fast_b, w_fc, w_proj, u, v, gate,
                   filters, fc_hi, fc_lo, proj_t)
            setup_stage(nc, hbm, ident, bv_row, srow, flag, V, GC1, Win, Wgate, eps, half)
            project_stage(nc, x, xnT_hbm, gc2_hbm, in_b, conv_w, conv_b, gate_b, ident, bv_row, V, GC1, Win, Wgate, eps, half)
        mix_stage(nc, x, filters, fc_hi, fc_lo, proj_t, xnT_hbm, xf_hbm, out_b, srow, flag, V, GC1)
        output_stage(nc, out, out_w, gc2_hbm, xf_hbm, ident, V)


_INS = ["attn_x", "attn_in_proj_w", "attn_in_proj_b", "attn_out_proj_w", "attn_out_proj_b", "attn_freqs",
        "attn_mlp_w1", "attn_mlp_b1", "attn_mlp_w2", "attn_mlp_b2", "attn_mlp_w3", "attn_mlp_b3", "attn_decay",
        "attn_conv_w", "attn_conv_b", "attn_gate_w", "attn_gate_b", "ffn_fast_b", "ffn_w_fc", "ffn_w_proj",
        "ffn_u", "ffn_v", "ffn_gate"]


def kernel(**inputs):
    import numpy as _np
    import concourse.bacc as _bacc
    from concourse import mybir as _mybir
    from concourse.bass_utils import run_bass_kernel_spmd as _run

    nc = _bacc.Bacc("TRN2", target_bir_lowering=False, num_devices=1)
    arrays, args = {}, []
    for name in _INS:
        a = _np.ascontiguousarray(inputs["L0_" + name])
        arrays[f"in_{name}"] = a
        args.append(nc.dram_tensor(f"in_{name}", a.shape, _mybir.dt.from_np(a.dtype), kind="ExternalInput").ap())
    args.append(nc.dram_tensor("out_0", (B, L, D), F32, kind="ExternalOutput").ap())
    conv_ffn_kernel(nc, *args)
    r = _run(nc, [arrays], core_ids=[0])
    return r.results[0]["out_0"]
```

```python
from contextlib import ExitStack

import concourse.bass as bass
from concourse import mybir

F32 = mybir.dt.float32
F32R = mybir.dt.float32r
I32 = mybir.dt.int32
ALU = mybir.AluOpType
ACT = mybir.ActivationFunctionType
AX = mybir.AxisListType

P = 128
B, L, D = 4, 2048, 256
KT = D // P
HID, RANK = 1024, 16
HT = HID // P
ORDERS, FO, EMB = 2, 64, 3
CH = 512
TT = CH // P
CPB = L // CH
NCH = B * CPB
NA = L // P
COLS = B * NA
PADDED = P - 1 + L
NEAR = 3
MID_FROM = (NEAR - 1) * P + 1
FAR_FROM = NEAR * P + 1
FARS = (NA - NEAR - 1) // NEAR
GC = 8
TC = 2
TILES = GC // TC
GROUPS = ORDERS * D // GC
GPI = D // GC // (NCH // ORDERS)
ITERS = NCH // ORDERS
ROUND = 12582912.0
TWO_PI = 6.283185
LEAST_NORMAL = 1.17549435e-38
SLOTS = 4
TIME_ROW = 64


def setup_stage(nc, hbm, ident, bv_row, srow, flag, V, GC1, Win, Wgate, eps, half, load_first, norm):
    (in_w, in_b, out_b, freqs, w1, b1, w2, b2, w3, b3, decay, gate_w, fast_b, w_fc, w_proj, u, v, gate,
     filters, fc_hi, fc_lo, proj_t) = hbm
    with ExitStack() as ctx:
        def sb(name, shape, dt=F32):
            return ctx.enter_context(nc.sbuf_tensor(name, shape, dt))

        def sem(name):
            return ctx.enter_context(nc.semaphore(name))

        Vf = V[:, :, :, :].rearrange("p c n a -> p (c n a)")
        Gf = GC1[:, :, :, :].rearrange("p c n a -> p (c n a)")
        hT = Vf[:, 0:4 * L].rearrange("p (w j) -> p w j", w=4)
        fc_nat = Vf[:, 8192:10240].rearrange("p (m d) -> p m d", m=HT)
        fc_tern = Vf[:, 10240:12288].rearrange("p (m d) -> p m d", m=HT)
        pr_nat = Vf[:, 12288:14336].rearrange("p (k h) -> p k h", k=KT)
        pr_tern = Vf[:, 14336:16384].rearrange("p (k h) -> p k h", k=KT)
        t = Gf[:, 0:L]
        jint = Gf[:, L:2 * L].bitcast(I32)
        enc = Gf[0:TIME_ROW + 1, 2 * L:3 * L]
        rnd = Gf[0:TIME_ROW, 3 * L:4 * L]
        h1, h2 = Gf[:, 4 * L:5 * L], Gf[:, 5 * L:6 * L]
        projT = Gf[:, 6 * L:7 * L]

        prow = sb("prow", [TIME_ROW, 1], I32)
        prow_f = sb("prow_f", [TIME_ROW, 1])
        quarter = sb("quarter", [TIME_ROW, 3])
        phase = sb("phase", [TIME_ROW, 1])
        freq = sb("freq", [TIME_ROW, 1])
        w1s = sb("w1s", [TIME_ROW + 1, ORDERS * FO])
        w2s = sb("w2s", [ORDERS * FO, ORDERS * FO])
        w3s = sb("w3s", [ORDERS * FO, ORDERS, D])
        b1s = sb("b1s", [ORDERS * FO, 1])
        b2s = sb("b2s", [ORDERS * FO, 1])
        b3s = sb("b3s", [P, ORDERS * KT])
        dec = sb("dec", [P, ORDERS * KT])
        ndec = sb("ndec", [P, ORDERS * KT])
        zpad = sb("zpad", [P, 4, P - 1])
        ones = sb("ones", [P, P])
        win_f = sb("win_f", [P, KT, 3 * D])
        gw_f = sb("gw_f", [P, ORDERS * KT, D])
        us = sb("us", [P, HT, RANK])
        vs = sb("vs", [RANK, D])
        fbT = sb("fbT", [RANK, RANK])
        gcol = sb("gcol", [P, 1])
        uT = sb("uT", [RANK, HID])
        m1 = sb("m1", [RANK, D])
        fsc = sb("fsc", [P, HT])
        fth = sb("fth", [P, 2 * HT])
        psc = sb("psc", [P, KT])
        pth = sb("pth", [P, 2 * KT])
        diag = sb("diag", [P, KT, P])
        weff_hi = sb("weff_hi", [P, KT, HID], F32R)
        weff_lo = sb("weff_lo", [P, KT, HID], F32R)
        peaks = sb("peaks", [P, 2, 4])
        reach = sb("reach", [1, 1 + GROUPS])
        tile_reach = sb("tile_reach", [1, GROUPS, TILES])
        ps = ctx.enter_context(nc.psum_tensor("ps_setup", [P, 8, 512], F32))
        lower, upper = (ps[:, i:i + 4, :].rearrange("p a b -> p (a b)") for i in (0, 4))

        rank_in, filter_in, proj_in, tern_in = sem("rank_in"), sem("filter_in"), sem("proj_in"), sem("tern_in")
        freq_in = sem("freq_in")
        FREQ_LOADS, RANK_LOADS, FILTER_LOADS, PROJ_LOADS, TERN_LOADS = 4, 4, 11, 3, 2
        zeros_ready, ident_zero, ident_ready, iota_ready = sem("zeros_ready"), sem("ident_zero"), sem("ident_ready"), sem("iota_ready")
        dve_step = sem("dve_step")
        t_ready, t_row_ready, angle_ready, enc_ready = sem("t_ready"), sem("t_row_ready"), sem("angle_ready"), sem("enc_ready")
        pad_ready, ndec_ready, win_ready, h_ready = sem("pad_ready"), sem("ndec_ready"), sem("win_ready"), sem("h_ready")
        l1_mm, l2_mm, l3_mm = sem("l1_mm"), sem("l2_mm"), sem("l3_mm")
        h1_ready, h2_ready = sem("h1_ready"), sem("h2_ready")
        uT_mm, m1_mm, rank_ready, rank_mm = sem("uT_mm"), sem("m1_mm"), sem("rank_ready"), sem("rank_mm")
        tern_ready, weff_mm, weff_hi_ready, weff_lo_ready = sem("tern_ready"), sem("weff_mm"), sem("weff_hi_ready"), sem("weff_lo_ready")
        projT_mm, proj_ready, srow_mm, diag_ready = sem("projT_mm"), sem("proj_ready"), sem("srow_mm"), sem("diag_ready")
        peak_ready, peakT_mm = sem("peak_ready"), sem("peakT_mm")
        hi_ready, eps_ready = sem("hi_ready"), sem("eps_ready")
        statistics, rstd, normalise = norm
        stored = sem("stored")
        ctx.enter_context(nc.allow_non_contiguous_dma(reason="a few small vectors, one value a partition"))
        block = ctx.enter_context(nc.Block())

        @block.sync
        def _(sp):
            def load(dst, src, s):
                sp.dma_start(dst, src).then_inc(s, 16)

            sp.wait_ge(zeros_ready, 1)
            for o in range(ORDERS):
                for half_ in range(2):
                    at = 32 * o + half_ * EMB
                    load(freq[at:at + EMB, :], freqs[o:o + 1, :].rearrange("o k -> k o"), freq_in)
            load(us[:, :, :], u.rearrange("(m p) r -> p m r", p=P), rank_in)
            load(vs[:, :], v, rank_in)
            load(fbT[:, :], fast_b.rearrange("i j -> j i"), rank_in)
            load(gcol[:, :], bass.AP(gate.tensor, 0, [[0, P], [1, 1]]), rank_in)
            load(dec[:, :], bass.AP(decay.tensor, 0, [[1, P], [P, ORDERS * KT]]), filter_in)
            sp.wait_ge(zeros_ready, 4)
            for o in range(ORDERS):
                load(w1s[32 * o:32 * o + 2 * EMB, o * FO:(o + 1) * FO], w1[o, 0:2 * EMB, :], filter_in)
            load(w1s[TIME_ROW:TIME_ROW + 1, :].rearrange("p (o f) -> p o f", o=ORDERS),
                 bass.AP(w1.tensor, 2 * EMB * FO, [[1, 1], [(2 * EMB + 1) * FO, ORDERS], [1, FO]]), filter_in)
            load(b1s[:, :], bass.AP(b1.tensor, 0, [[1, ORDERS * FO], [1, 1]]), filter_in)
            load(b2s[:, :], bass.AP(b2.tensor, 0, [[1, ORDERS * FO], [1, 1]]), filter_in)
            load(b3s[:, :], bass.AP(b3.tensor, 0, [[1, P], [P, ORDERS * KT]]), filter_in)
            for o in range(ORDERS):
                rows = slice(o * FO, (o + 1) * FO)
                load(w2s[rows, rows], w2[o], filter_in)
                load(w3s[rows, o, :], w3[o], filter_in)
            load(fc_nat, w_fc.rearrange("(m p) d -> p m d", p=P), tern_in)
            load(pr_nat, w_proj.rearrange("(k p) h -> p k h", p=P), tern_in)
            load(win_f[:, :, :], in_w.rearrange("(k p) c -> p k c", p=P), proj_in)
            load(gw_f[:, :, :], gate_w.rearrange("o (k p) c -> p (o k) c", p=P), proj_in)
            load(bv_row[:, :], bass.AP(in_b.tensor, 0, [[0, P], [1, D]]), proj_in)
            load_first(sp)
            rows = filters.rearrange("(w p) j -> p w j", p=P)
            sp.wait_ge(pad_ready, 1)
            load(rows[:, 0:KT, L:PADDED], zpad[:, 0:KT, :], stored)
            load(rows[:, KT:2 * KT, 0:P - 1], zpad[:, KT:2 * KT, :], stored)
            for w in range(4):
                sp.wait_ge(h_ready, w + 1)
                at = 0 if w < KT else P - 1
                load(filters[w * P:(w + 1) * P, at:at + L], hT[:, w, :], stored)
            sp.wait_ge(weff_hi_ready, 1)
            load(fc_hi, weff_hi[:, :, :].bitcast(F32), stored)
            sp.wait_ge(weff_lo_ready, 1)
            load(fc_lo, weff_lo[:, :, :].bitcast(F32), stored)
            sp.wait_ge(proj_ready, 1)
            load(proj_t, projT.rearrange("p (m d) -> p m d", m=HT), stored)
            sp.wait_ge(stored, 16 * 9)
            sp.wait_ge(proj_in, 16 * PROJ_LOADS)

        @block.gpsimd
        def _(pool):
            pool.iota(jint, [[1, L]], base=0, channel_multiplier=0).then_inc(iota_ready, 1)
            pool.iota(prow[:, :], [[0, 1]], base=0, channel_multiplier=1).then_inc(iota_ready, 1)
            pool.memset(ident[:, :], 0.0).then_inc(ident_zero, 1)
            pool.wait_ge(ident_zero, 1)
            pool.affine_select(out=ident[:, :], in_=ident[:, :], compare_op=ALU.not_equal, fill=1.0, base=0,
                               pattern=[[-1, P]], channel_multiplier=1).then_inc(ident_ready, 1)
            pool.memset(eps[:, :], 1e-5).then_inc(eps_ready, 1)
            pool.memset(half[:, :], -0.5).then_inc(eps_ready, 1)
            pool.wait_ge(eps_ready, 2)
            rstd(pool, 0, True)
            normalise(pool, 0, 0)

        @block.vector
        def _(dve):
            steps = [0]

            def link(ins):
                steps[0] += 1
                ins.then_inc(dve_step, 1)
                dve.wait_ge(dve_step, steps[0])

            for buf in (freq[:, :], w1s[:, :], w2s[:, :], w3s[:, :, :]):
                dve.memset(buf, 0.0).then_inc(zeros_ready, 1)
            dve.memset(zpad[:, :, :], 0.0).then_inc(pad_ready, 1)
            dve.memset(ones[:, :], 1.0)
            dve.wait_ge(iota_ready, 2)
            link(dve.tensor_copy(t, jint))
            dve.tensor_scalar(t, t, 1.0 / (L - 1), None, ALU.mult).then_inc(t_ready, 1)
            dve.wait_ge(t_ready, 1)
            link(dve.tensor_copy(prow_f[:, :], prow[:, :]))
            for i, (first, turn) in enumerate(((EMB, 0.25), (32, -0.25), (32 + EMB, 0.25))):
                last = dve.tensor_scalar(quarter[:, i:i + 1], prow_f[:, :], float(first), turn, ALU.is_ge, ALU.mult)
            link(last)
            link(dve.tensor_reduce(phase[:, :], quarter[:, :], AX.X, ALU.add))
            dve.wait_ge(freq_in, 16 * FREQ_LOADS)
            turns = enc[0:TIME_ROW, :]
            link(dve.tensor_scalar(turns, t[0:TIME_ROW, :], freq[:, :], phase[:, :], ALU.mult, ALU.add))
            link(dve.tensor_scalar(rnd, turns, ROUND, None, ALU.add))
            link(dve.tensor_scalar(rnd, rnd, ROUND, None, ALU.subtract))
            dve.tensor_tensor(turns, turns, rnd, ALU.subtract).then_inc(angle_ready, 1)
            dve.wait_ge(filter_in, 16 * FILTER_LOADS)
            link(dve.tensor_scalar(ndec[:, :], dec[:, :], -1.0, None, ALU.mult))
            link(dve.tensor_tensor(ndec[:, :], ndec[:, :], dec[:, :], ALU.min))
            dve.tensor_scalar(ndec[:, :], ndec[:, :], float(L), None, ALU.mult).then_inc(ndec_ready, 1)
            dve.wait_ge(tern_in, 16 * TERN_LOADS)

            def ternary(nat, tern, sc, th, m, width):
                link(dve.tensor_reduce(sc[:, :], nat, AX.X, ALU.add, apply_absolute_value=True))
                link(dve.tensor_scalar(sc[:, :], sc[:, :], 1.0 / width, 1e-5, ALU.mult, ALU.max))
                dve.tensor_scalar(th[:, 0:m], sc[:, :], 0.5, None, ALU.mult)
                link(dve.tensor_scalar(th[:, m:2 * m], sc[:, :], -0.5, None, ALU.mult))
                for i in range(m):
                    last = dve.tensor_scalar(tern[:, i, :], nat[:, i, :], th[:, m + i:m + i + 1], None, ALU.is_lt)
                link(last)
                for i in range(m):
                    last = dve.scalar_tensor_tensor(out=tern[:, i, :], in0=nat[:, i, :], scalar=th[:, i:i + 1],
                                                    in1=tern[:, i, :], op0=ALU.is_gt, op1=ALU.subtract)
                return last

            link(ternary(fc_nat, fc_tern, fsc, fth, HT, D))
            dve.wait_ge(rank_mm, 1)
            for i in range(HT):
                last = dve.scalar_tensor_tensor(out=fc_tern[:, i, :], in0=fc_tern[:, i, :], scalar=fsc[:, i:i + 1],
                                                in1=ps[:, 4 + i // 2, (i % 2) * D:(i % 2 + 1) * D], op0=ALU.mult, op1=ALU.add)
            last.then_inc(tern_ready, 1)

            def filter_tile(w):
                dve.wait_ge(win_ready, w + 1)
                dve.wait_ge(l3_mm, w + 1)
                features = (upper, lower)[w % 2]
                dve.scalar_tensor_tensor(out=hT[:, w, :], in0=features[:, ::-1] if w < KT else features,
                                         scalar=b3s[:, w:w + 1], in1=hT[:, w, :], op0=ALU.add, op1=ALU.mult).then_inc(h_ready, 1)
                dve.wait_ge(h_ready, w + 1)
                for i, (first, end) in enumerate(((MID_FROM, FAR_FROM), (FAR_FROM, L))):
                    part = hT[:, w, L - end:L - first] if w < KT else hT[:, w, first:end]
                    dve.tensor_reduce(peaks[:, i, w:w + 1], part, AX.X, ALU.max, apply_absolute_value=True).then_inc(peak_ready, 1)

            ternary(pr_nat, pr_tern, psc, pth, KT, HID).then_inc(tern_ready, 1)
            filter_tile(0)
            filter_tile(1)
            dve.wait_ge(hi_ready, 2)
            dve.tensor_tensor(Win[1][:, :, :], win_f[:, :, :], Win[0][:, :, :].bitcast(F32), ALU.subtract)
            dve.tensor_tensor(Wgate[1][:, :, :], gw_f[:, :, :], Wgate[0][:, :, :].bitcast(F32), ALU.subtract)
            filter_tile(2)
            dve.wait_ge(ident_ready, 1)
            for k in range(KT):
                last = dve.tensor_scalar(diag[:, k, :], ident[:, :], psc[:, k:k + 1], None, ALU.mult)
            last.then_inc(diag_ready, 1)
            filter_tile(3)
            statistics(dve, 0, 0, True)
            dve.wait_ge(peak_ready, 8)
            dve.tensor_tensor(peaks[:, 0, :], peaks[:, 0, :], peaks[:, 1, :], ALU.max).then_inc(peak_ready, 1)
            dve.wait_ge(weff_hi_ready, 1)
            dve.tensor_tensor(weff_lo[:, :, :].rearrange("p k h -> p (k h)"), upper,
                              weff_hi[:, :, :].bitcast(F32).rearrange("p k h -> p (k h)"), ALU.subtract).then_inc(weff_lo_ready, 1)
            dve.wait_ge(srow_mm, 1)
            dve.tensor_copy(srow[:, :], ps[:, 4, 0:D])
            dve.wait_ge(peakT_mm, 1)
            link(dve.tensor_reduce(reach[:, 0:1], ps[0:1, 6, :], AX.X, ALU.max))
            link(dve.tensor_reduce(tile_reach[:, :, :], ps[0:1, 5, :].rearrange("p (g q c) -> p g q c", q=TILES, c=TC), AX.X, ALU.max))
            link(dve.tensor_scalar(reach[:, 0:1], reach[:, 0:1], LEAST_NORMAL, None, ALU.is_ge))
            link(dve.tensor_scalar(tile_reach[:, :, :], tile_reach[:, :, :], LEAST_NORMAL, None, ALU.is_ge))
            groups = reach[:, 1:1 + GROUPS]
            link(dve.tensor_scalar(groups, tile_reach[:, :, TILES - 1], 2.0, None, ALU.mult))
            for q in range(TILES - 2, -1, -1):
                link(dve.tensor_tensor(groups, groups, tile_reach[:, :, q], ALU.add))
                if q:
                    link(dve.tensor_scalar(groups, groups, 2.0, None, ALU.mult))
            dve.tensor_copy(flag[:, :], reach[:, :])

        @block.scalar
        def _(act):
            act.wait_ge(uT_mm, 1)
            act.activation(uT[:, :], ps[0:RANK, 0:2, :].rearrange("p a b -> p (a b)"), ACT.Copy).then_inc(rank_ready, 1)
            act.wait_ge(m1_mm, 1)
            act.activation(m1[:, :], ps[0:RANK, 2, 0:D], ACT.Identity, scale=gcol[0:RANK, :]).then_inc(rank_ready, 1)
            act.wait_ge(t_ready, 1)
            act.activation(enc[TIME_ROW:TIME_ROW + 1, :], t[TIME_ROW:TIME_ROW + 1, :], ACT.Copy).then_inc(t_row_ready, 1)
            act.wait_ge(angle_ready, 1)
            act.activation(enc[0:TIME_ROW, :], enc[0:TIME_ROW, :], ACT.Sin, scale=TWO_PI).then_inc(enc_ready, 1)

            def window(w):
                act.activation(hT[:, w, :], t[:, ::-1] if w < KT else t, ACT.Exp, scale=ndec[:, w:w + 1]).then_inc(win_ready, 1)

            act.wait_ge(ndec_ready, 1)
            window(0)
            window(1)
            act.wait_ge(l1_mm, 1)
            act.activation(h1, lower, ACT.Gelu, bias=b1s[:, :]).then_inc(h1_ready, 1)
            act.wait_ge(proj_in, 16 * PROJ_LOADS)
            act.activation(Win[0][:, :, :], win_f[:, :, :], ACT.Copy).then_inc(hi_ready, 1)
            act.wait_ge(l2_mm, 1)
            act.activation(h2, lower, ACT.Gelu, bias=b2s[:, :]).then_inc(h2_ready, 1)
            act.activation(Wgate[0][:, :, :], gw_f[:, :, :], ACT.Copy).then_inc(hi_ready, 1)
            window(2)
            window(3)
            act.wait_ge(weff_mm, 1)
            act.activation(weff_hi[:, :, :].rearrange("p k h -> p (k h)"), upper, ACT.Copy).then_inc(weff_hi_ready, 1)
            act.wait_ge(projT_mm, 1)
            act.activation(projT, lower, ACT.Copy).then_inc(proj_ready, 1)

        @block.tensor
        def _(pe):
            pe.wait_ge(rank_in, 16 * RANK_LOADS)
            pe.wait_ge(ident_ready, 1)
            for m in range(HT):
                last = pe.transpose(ps[0:RANK, m // 4, (m % 4) * P:(m % 4 + 1) * P], us[:, m, :], ident[:, :])
            last.then_inc(uT_mm, 1)
            pe.matmul(ps[0:RANK, 2, 0:D], fbT[:, :], vs[:, :], start=True, stop=True).then_inc(m1_mm, 1)
            pe.wait_ge(rank_ready, 2)
            for m in range(HT):
                last = pe.matmul(ps[:, 4 + m // 2, (m % 2) * D:(m % 2 + 1) * D], uT[:, m * P:(m + 1) * P], m1[:, :],
                                 start=True, stop=True)
            last.then_inc(rank_mm, 1)
            pe.wait_ge(filter_in, 16 * FILTER_LOADS)
            pe.wait_ge(t_row_ready, 1)
            pe.wait_ge(enc_ready, 1)
            for j in range(4):
                last = pe.matmul(ps[:, j, :], w1s[:, :], enc[:, j * 512:j * 512 + 512], start=True, stop=True)
            last.then_inc(l1_mm, 1)
            pe.wait_ge(h1_ready, 1)
            for j in range(4):
                last = pe.matmul(ps[:, j, :], w2s[:, :], h1[:, j * 512:j * 512 + 512], start=True, stop=True)
            last.then_inc(l2_mm, 1)
            pe.wait_ge(h2_ready, 1)
            pe.wait_ge(tern_ready, 1)
            for w in range(4):
                if w >= 2:
                    pe.wait_ge(h_ready, w - 1)
                o, c = w // KT, w % KT
                for j in range(4):
                    last = pe.matmul(ps[:, 4 * (1 - w % 2) + j, :], w3s[:, o, c * P:(c + 1) * P], h2[:, j * 512:j * 512 + 512],
                                     start=True, stop=True)
                last.then_inc(l3_mm, 1)
            pe.wait_ge(h_ready, 3)
            for k in range(KT):
                for m in range(HT):
                    last = pe.transpose(ps[:, 4 + 2 * k + m // 4, (m % 4) * P:(m % 4 + 1) * P], fc_tern[:, m, k * P:(k + 1) * P], ident[:, :])
            last.then_inc(weff_mm, 1)
            pe.wait_ge(tern_ready, 2)
            pe.wait_ge(h_ready, 4)
            for m in range(HT):
                for k in range(KT):
                    last = pe.transpose(ps[:, m // 2, (m % 2) * D + k * P:(m % 2) * D + (k + 1) * P],
                                        pr_tern[:, k, m * P:(m + 1) * P], ident[:, :])
            last.then_inc(projT_mm, 1)
            pe.wait_ge(diag_ready, 1)
            pe.wait_ge(weff_lo_ready, 1)
            pe.matmul(ps[:, 4, 0:D], ones[:, :], diag[:, :, :].rearrange("p k c -> p (k c)"), start=True, stop=True).then_inc(srow_mm, 1)
            pe.wait_ge(peak_ready, 9)
            for i in range(2):
                for w in range(4):
                    last = pe.transpose(ps[0:1, 5 + i, w * P:(w + 1) * P], peaks[:, i, w:w + 1], ident[:, :])
            last.then_inc(peakT_mm, 1)


def wait_alone(eng, sem, value, passed):
    eng.wait_ge(sem, value)
    eng.sem_inc(passed, 1)


def split_mm(pe, out, w, x, start, stop, **more):
    pe.matmul(out, w[0], x[0], start=start, stop=False, **more)
    pe.matmul(out, w[1], x[0], start=False, stop=False, **more)
    return pe.matmul(out, w[0], x[1], start=False, stop=stop, **more)


def norm_steps(xt, norms, eps, half, x_loaded, stat_done, aggr_done, rstd_step, xn_ready, dve_passed, pool_passed):
    stats, mv, ve, rs, nt = norms[:, :, 0:6], norms[:, :, 6:8], norms[:, :, 8], norms[:, :, 9], norms[:, :, 10]

    def statistics(dve, c, c0, first=False):
        if not first:
            dve.wait_ge(xn_ready, c)
        dve.wait_ge(x_loaded[c0 % 2], (c - c0 % 2) * 8 + 16)
        for i in range(TT):
            dve.bn_stats(stats[:, i, :], xt[c0 % 2][:, i, :]).then_inc(stat_done, 1)
        for i in range(TT):
            wait_alone(dve, stat_done, 4 * c + i + 1, dve_passed)
            dve.bn_aggr(mv[:, i, :], stats[:, i, :]).then_inc(aggr_done, 1)

    def rstd(pool, c, first=False):
        r = 6 * c
        pool.wait_ge(aggr_done, 4 * c + 4)
        if not first:
            pool.wait_ge(xn_ready, c)
        pool.tensor_tensor(ve, mv[:, :, 1], eps[:, :], ALU.add).then_inc(rstd_step, 1)
        pool.wait_ge(rstd_step, r + 1)
        pool.tensor_tensor(rs, ve, half[:, :], ALU.pow).then_inc(rstd_step, 1)
        pool.wait_ge(rstd_step, r + 2)
        pool.tensor_tensor(nt, rs, rs, ALU.mult).then_inc(rstd_step, 1)
        pool.wait_ge(rstd_step, r + 3)
        pool.tensor_tensor(nt, nt, ve, ALU.mult).then_inc(rstd_step, 1)
        wait_alone(pool, rstd_step, r + 4, pool_passed)
        pool.tensor_scalar(nt, nt, -0.5, 1.5, ALU.mult, ALU.add).then_inc(rstd_step, 1)
        pool.wait_ge(rstd_step, r + 5)
        pool.tensor_tensor(rs, rs, nt, ALU.mult).then_inc(rstd_step, 1)

    def normalise(pool, c, c0):
        wait_alone(pool, rstd_step, 6 * c + 6, pool_passed)
        buf = xt[c0 % 2]
        for i in range(TT):
            last = pool.tensor_scalar(buf[:, i, :], buf[:, i, :], mv[:, i, 0:1], rs[:, i:i + 1], ALU.subtract, ALU.mult)
        last.then_inc(xn_ready, 1)

    return statistics, rstd, normalise


def x_tile(x, c):
    return x.rearrange("n (q i p) d -> (n q) p i d", i=TT, p=P)[bass.ds(c, 1)].rearrange("c p i d -> (c p) i d")


def project_stage(nc, x, xnT_hbm, gc2_hbm, ident, bv_row, V, GC1, Win, Wgate, eps, xt, x_loaded, xn_ready, norm, taps, bias_in, gc2_saved):
    with ExitStack() as ctx:
        def sb(name, shape, dt=F32):
            return ctx.enter_context(nc.sbuf_tensor(name, shape, dt))

        def sem(name):
            return ctx.enter_context(nc.semaphore(name))

        statistics, rstd, normalise = norm
        xn = [sb("xn_hi", [P, KT, CH], F32R), sb("xn_lo", [P, KT, CH], F32R)]
        ctrl = [sb(f"ctrl{i}", [P, 4, CH + 2]) for i in range(2)]
        xcs = [[sb(f"xc_{part}{o}", [P, KT, CH], F32R) for part in ("hi", "lo")] for o in range(ORDERS)]
        table = sb("table", [P, 1])
        xc = sb("xc", [P, 4, CH])
        kw, cb, kb, gb = taps[:, :, 0:3], taps[:, :, 3], taps[:, :, 4], taps[:, :, 5]
        pT = ctx.enter_context(nc.psum_tensor("pT", [P, KT, CH], F32))
        pn = ctx.enter_context(nc.psum_tensor("pn", [P, TT, D], F32))
        pc = ctx.enter_context(nc.psum_tensor("pc", [P, 4, CH], F32))

        sp_passed = sem("sp_passed")
        xT_mm = sem("xT_mm")
        xn_hi_done, xn_split = sem("xn_hi_done"), sem("xn_split")
        xn_saved = [sem("xn_hi_saved"), sem("xn_lo_saved")]
        ctrl_mm, ctrl_copied = sem("ctrl_mm"), sem("ctrl_copied")
        v_mm, v_stored = sem("v_mm"), sem("v_stored")
        halo_done = sem("halo_done")
        tap0_done, tap1_done = sem("tap0_done"), sem("tap1_done")
        xc_ready = sem("xc_ready")
        xc_hi_done = sem("xc_hi_done")
        xc_split = sem("xc_split")
        gate_mm = sem("gate_mm")
        gate_done = sem("gate_done")
        gc_done = sem("gc_done")
        gcT_mm = sem("gcT_mm")
        gc1_stored = sem("gc1_stored")
        ctx.enter_context(nc.allow_non_contiguous_dma(reason="a few small vectors, one value a partition"))
        block = ctx.enter_context(nc.Block())

        def steps(eng, step):
            step(-1, -1)
            step(0, 0)
            with eng.Fori(0, (NCH - 4) // 4) as m:
                batch_of[eng.engine] = m
                for j in range(4):
                    step(m * 4 + (j + 1), 1 + j)
            for s in range(NCH - 3, NCH + 1):
                step(s, s)

        batch_of = {}

        def batch(eng, s, s0):
            return s // CPB if isinstance(s, int) else batch_of[eng.engine] + s0 // CPB

        def tapped(buffer, c, k):
            at = 2 - k if c < KT else k
            return buffer[:, c, at:at + CH]

        def has(s0):
            return 0 <= s0 < NCH, s0 + 1 < NCH, s0 >= 1

        @block.sync
        def _(sp):
            sp.sem_inc(gc2_saved, 16)

            def load_x(c, c0):
                sp.dma_start(xt[c0 % 2][:, :, :], x_tile(x, c)).then_inc(x_loaded[c0 % 2], 16)

            def step(s, s0):
                front, ahead, back = has(s0)
                if s0 + 3 < NCH:
                    wait_alone(sp, xT_mm, s + 2, sp_passed)
                    load_x(s + 3, s0 + 3)
                if ahead:
                    for part, done in ((0, xn_hi_done), (1, xn_split)):
                        wait_alone(sp, done, s + 2, sp_passed)
                        sp.dma_start(xnT_hbm[part, bass.ds(s + 1, 1)].rearrange("c p k t -> (c p) k t"),
                                     xn[part][:, :, :].bitcast(F32)).then_inc(xn_saved[part], 16)
                if back:
                    wait_alone(sp, gc_done, 4 * s + 4, sp_passed)
                    sp.dma_start(gc2_hbm[bass.ds(s - 1, 1)].rearrange("c p k t -> (c p) k t"), xc[:, KT:2 * KT, :]).then_inc(gc2_saved, 16)

            steps(sp, step)
            for part in range(2):
                sp.wait_ge(xn_saved[part], 16 * NCH)

        @block.gpsimd
        def _(pool):
            def step(s, s0):
                if s0 + 2 < NCH:
                    rstd(pool, s + 2)
                    normalise(pool, s + 2, s0 + 2)

            steps(pool, step)

        @block.vector
        def _(dve):
            dve.sem_inc(gc1_stored, 1)
            dve.sem_inc(gc_done, 4)
            dve.sem_inc(xc_ready, 4)

            def step(s, s0):
                front, ahead, back = has(s0)
                par, k = s0 % 2, s0 % 4

                def halo(c):
                    near, far, inner_far, inner_near = (0, CH + 1, CH, 1) if c >= KT else (CH + 1, 0, 1, CH)
                    if front:
                        dve.wait_ge(ctrl_copied, 4 * s + c + 1)
                    if front and k == 0:
                        last = dve.memset(ctrl[par][:, c, near:near + 1], 0.0)
                    elif front:
                        last = dve.tensor_copy(ctrl[par][:, c, near:near + 1], ctrl[1 - par][:, c, inner_far:inner_far + 1])
                    if back and k == 0:
                        last = dve.memset(ctrl[1 - par][:, c, far:far + 1], 0.0)
                    elif back:
                        last = dve.tensor_copy(ctrl[1 - par][:, c, far:far + 1], ctrl[par][:, c, inner_near:inner_near + 1])
                    last.then_inc(halo_done, 1)

                def tap(c, k_, before, done):
                    if back:
                        dve.wait_ge(before, 4 * s - 4 + c + 1)
                        dve.scalar_tensor_tensor(out=xc[:, c, :], in0=tapped(ctrl[1 - par], c, k_), scalar=kw[:, c, k_:k_ + 1],
                                                 in1=xc[:, c, :], op0=ALU.mult, op1=ALU.add).then_inc(done, 1)

                def low(c):
                    if back:
                        dve.wait_ge(xc_hi_done, 4 * s - 4 + c + 1)
                        dve.tensor_tensor(xcs[c // KT][1][:, c % KT, :], xc[:, c, :], xcs[c // KT][0][:, c % KT, :].bitcast(F32),
                                          ALU.subtract).then_inc(xc_split, 1)

                def gated(c):
                    dve.wait_ge(gate_done, 4 * s - 4 + c + 1)
                    dve.tensor_tensor(xc[:, c, :], pc[:, c, :], xc[:, c, :], ALU.mult).then_inc(gc_done, 1)

                if s0 >= 0:
                    halo(0)
                    tap(0, 1, tap0_done, tap1_done)
                    halo(1)
                    tap(0, 2, tap1_done, xc_ready)
                    tap(1, 1, tap0_done, tap1_done)
                    halo(2)
                    tap(1, 2, tap1_done, xc_ready)
                    halo(3)
                    low(0)
                    tap(2, 1, tap0_done, tap1_done)
                    low(1)
                    tap(3, 1, tap0_done, tap1_done)
                    tap(2, 2, tap1_done, xc_ready)
                    tap(3, 2, tap1_done, xc_ready)
                    low(2)
                    low(3)
                if front:
                    dve.wait_ge(v_mm, s + 1)
                    dve.tensor_tensor(V[:, :, bass.ds(batch(dve, s, s0), 1), TT * k:TT * k + TT].rearrange("p c n a -> p c (n a)"),
                                      pn[:, :, :].rearrange("p i c -> p c i"),
                                      bv_row[:, :].unsqueeze(2).broadcast_to([P, D, TT]), ALU.add).then_inc(v_stored, 1)
                if back:
                    gated(0)
                    gated(1)
                if ahead:
                    dve.wait_ge(xn_hi_done, s + 2)
                    if s0 >= 0:
                        dve.wait_ge(xn_saved[1], 16 * s + 16)
                    dve.tensor_tensor(xn[1][:, :, :], pT[:, :, :], xn[0][:, :, :].bitcast(F32), ALU.subtract).then_inc(xn_split, 1)
                if s0 + 2 < NCH:
                    statistics(dve, s + 2, s0 + 2)
                if back:
                    gated(2)
                    gated(3)
            steps(dve, step)

        @block.scalar
        def _(act):
            act.activation(table[:, :], eps[:, 0:1], ACT.Sigmoid)
            act.wait_ge(bias_in, 16 * 11)

            def step(s, s0):
                front, ahead, back = has(s0)
                par = s0 % 2

                def control(c):
                    if front:
                        act.wait_ge(ctrl_mm, 4 * s + c + 1)
                        act.activation(ctrl[par][:, c, 1:CH + 1], pc[:, c, ::-1] if c < KT else pc[:, c, :], ACT.Identity, bias=cb[:, c:c + 1]).then_inc(ctrl_copied, 1)

                def first_tap(c):
                    if back:
                        act.wait_ge(halo_done, 4 * s + c + 1)
                        act.activation(xc[:, c, :], tapped(ctrl[1 - par], c, 0), ACT.Identity, bias=kb[:, c:c + 1],
                                       scale=kw[:, c, 0:1]).then_inc(tap0_done, 1)

                def high(c):
                    if back:
                        act.wait_ge(xc_ready, 4 * s + c + 1)
                        act.activation(xcs[c // KT][0][:, c % KT, :], xc[:, c, :], ACT.Copy).then_inc(xc_hi_done, 1)

                def sigmoid(c):
                    act.wait_ge(gate_mm, 4 * s + c + 1)
                    act.activation(pc[:, c, :], pc[:, c, :], ACT.Sigmoid, bias=gb[:, c:c + 1]).then_inc(gate_done, 1)

                if front and s0 >= 1:
                    act.wait_ge(xc_ready, 4 * s)
                control(0)
                if back:
                    act.wait_ge(gcT_mm, s)
                first_tap(0)
                control(1)
                first_tap(1)
                control(2)
                control(3)
                if back:
                    act.wait_ge(gate_mm, 4 * s)
                high(0)
                if back:
                    act.wait_ge(gc2_saved, 16 * s)
                first_tap(2)
                high(1)
                first_tap(3)
                high(2)
                high(3)
                if back:
                    sigmoid(0)
                    sigmoid(1)
                if ahead:
                    act.wait_ge(xT_mm, s + 2)
                    if s0 >= 0:
                        act.wait_ge(xn_saved[0], 16 * s + 16)
                    act.activation(xn[0][:, :, :], pT[:, :, :], ACT.Copy).then_inc(xn_hi_done, 1)
                if back:
                    sigmoid(2)
                    sigmoid(3)
                    act.wait_ge(gcT_mm, s + 1)
                    pk = (s0 - 1) % 4
                    act.activation(GC1[:, :, bass.ds(batch(act, s - 1, s0 - 1), 1), TT * pk:TT * pk + TT].rearrange("p c n a -> p c (n a)"),
                                   pn[:, :, :].rearrange("p i c -> p c i"), ACT.Copy).then_inc(gc1_stored, 1)

            steps(act, step)

        @block.tensor
        def _(pe):
            pe.sem_inc(gate_mm, 4)
            pe.sem_inc(gcT_mm, 1)

            def step(s, s0):
                front, ahead, back = has(s0)
                if front:
                    pe.wait_ge(xn_split, s + 1)
                    for c in range(4):
                        if s0 >= 1:
                            pe.wait_ge(gc_done, 4 * s - 4 + c + 1)
                        for k in range(KT):
                            ws = slice(D + c * P, D + (c + 1) * P)
                            last = split_mm(pe, pc[:, c, :], (Win[0][:, k, ws], Win[1][:, k, ws]),
                                            (xn[0][:, k, :], xn[1][:, k, :]), k == 0, k == KT - 1)
                        last.then_inc(ctrl_mm, 1)
                    if s0 >= 1:
                        pe.wait_ge(gc1_stored, s)
                    for i in range(TT):
                        ts = slice(i * P, (i + 1) * P)
                        for k in range(KT):
                            last = split_mm(pe, pn[:, i, :], (xn[0][:, k, ts], xn[1][:, k, ts]),
                                            (Win[0][:, k, 0:D], Win[1][:, k, 0:D]), k == 0, k == KT - 1)
                    last.then_inc(v_mm, 1)
                def gates(o):
                    pe.wait_ge(xc_split, 4 * s - 4 + KT * o + KT)
                    for co in range(KT):
                        c = KT * o + co
                        if front:
                            pe.wait_ge(ctrl_copied, 4 * s + c + 1)
                        else:
                            pe.wait_ge(gc_done, 4 * s - 4 + c + 1)
                        for k in range(KT):
                            ws = slice(co * P, (co + 1) * P)
                            last = split_mm(pe, pc[:, c, :], (Wgate[0][:, KT * o + k, ws], Wgate[1][:, KT * o + k, ws]),
                                            (xcs[o][0][:, k, :], xcs[o][1][:, k, :]), k == 0, k == KT - 1)
                        last.then_inc(gate_mm, 1)
                if back:
                    gates(0)
                if ahead:
                    pe.wait_ge(xn_ready, s + 2)
                    if s0 >= 0:
                        pe.wait_ge(xn_split, s + 1)
                    for k in range(KT):
                        for i in range(TT):
                            last = pe.transpose(pT[:, k, i * P:(i + 1) * P], xt[(s0 + 1) % 2][:, i, k * P:(k + 1) * P], ident[:, :])
                    last.then_inc(xT_mm, 1)
                if back:
                    gates(1)
                    pe.wait_ge(gc_done, 4 * s + KT)
                    if front:
                        pe.wait_ge(v_stored, s + 1)
                    else:
                        pe.wait_ge(gc1_stored, s)
                    for i in range(TT):
                        for k in range(KT):
                            last = pe.transpose(pn[:, TT - 1 - i, k * P:(k + 1) * P], xc[:, k, i * P:(i + 1) * P], ident[:, :])
                    last.then_inc(gcT_mm, 1)

            steps(pe, step)


def mix_stage(nc, load_output, xf_saved, gc2_saved, x, filters, fc_hi, fc_lo, proj_t, xnT_hbm, xf_hbm, out_b, srow, flag, V, GC1):
    with ExitStack() as ctx:
        def sb(name, shape, dt=F32):
            return ctx.enter_context(nc.sbuf_tensor(name, shape, dt))

        def sem(name):
            return ctx.enter_context(nc.semaphore(name))

        wfc = [sb("wfc_hi", [P, KT, HID], F32R), sb("wfc_lo", [P, KT, HID], F32R)]
        wproj = sb("wproj", [P, HT, D], F32R)
        T = sb("T", [P, TILES, TC, NEAR * P])
        Tmid = sb("Tmid", [P, GC, P])
        xn = [[sb(f"xm_{part}{i}", [P, KT, CH], F32R) for part in ("hi", "lo")] for i in range(2)]
        xb = sb("xb", [P, TT, D])
        bo_row = sb("bo_row", [P, D])
        r = [sb(f"r{i}", [P, CH]) for i in range(2)]
        r_hi = [sb(f"r_hi{i}", [P, CH], F32R) for i in range(2)]
        r_lo = [sb(f"r_lo{i}", [P, CH], F32R) for i in range(2)]
        py = [ctx.enter_context(nc.psum_tensor(f"py{i}", [P, GC, B, NA], F32)) for i in range(2)]
        pf = [ctx.enter_context(nc.psum_tensor(f"pf{i}", [P, CH], F32)) for i in range(2)]
        pp = ctx.enter_context(nc.psum_tensor("pp", [P, TT, D], F32))

        w_in = [sem("fc_hi_in"), sem("fc_lo_in"), sem("proj_in")]
        bo_in = sem("bo_in")
        sp_passed, pool_passed = sem("sp_passed"), sem("pool_passed")
        T_loaded = [sem(f"T_loaded{q}") for q in range(TILES)]
        tile_mm = sem("tile_mm")
        far_loaded, far_used = sem("far_loaded"), sem("far_used")
        y_out = sem("y_out")
        mid_loaded = sem("mid_loaded")
        xn_loaded = [sem(f"xn_loaded{i}") for i in range(2)]
        xb_loaded, xb_biased = sem("xb_loaded"), sem("xb_biased")
        scaled = sem("scaled")
        xf_ready = sem("xf_ready")
        fc_mm = sem("fc_mm")
        relu_done = sem("relu_done")
        sq_done, r_hi_done = sem("sq_done"), sem("r_hi_done")
        r_split = sem("r_split")
        proj_mm = sem("proj_mm")
        ctx.enter_context(nc.allow_non_contiguous_dma(reason="a few small vectors, one value a partition"))
        block = ctx.enter_context(nc.Block())

        hankel = bass.AP(filters.tensor, 0, [[1, P], [PADDED, ORDERS * D], [1, L]])
        FAR = FARS * TILES

        def groups(eng, order, body):
            with eng.Fori(0, ITERS // 2) as half_m:
                for i in range(2):
                    body(half_m * 2 + i, half_m * 2 + (i + ITERS * order), i)

        def lags(order, A0, count):
            return P * (NA - A0 - count) if order == 0 else P * A0

        @block.sync
        def _(sp):
            sp.sem_inc(tile_mm, TILES)
            sp.sem_inc(mid_loaded, 16)
            tail = sp.value_load(flag[0:1, 0:1], min_val=0, max_val=1)
            for order in range(ORDERS):
                def body(m, it, i):
                    for g in range(GPI):
                        G = it * GPI + g
                        row = m * (GPI * GC) + (order * D + g * GC)

                        def load(slot, q, A0, s):
                            first = lags(order, A0, NEAR)
                            sp.dma_start(T[:, slot, :, :], hankel[:, bass.ds(row + q * TC, TC), first:first + NEAR * P]).then_inc(s, 16)

                        wait_alone(sp, tile_mm, G * TILES + 1, sp_passed)
                        load(0, 0, 0, T_loaded[0])
                        wait_alone(sp, tile_mm, G * TILES + 2, sp_passed)
                        middle = sp.value_load(flag[0:1, bass.ds(G + 1, 1)], min_val=0, max_val=2 ** TILES - 1)
                        with sp.If(middle > 0):
                            first = lags(order, NEAR, 1)
                            sp.dma_start(Tmid[:, :, :], hankel[:, bass.ds(row, GC), first:first + P]).then_inc(mid_loaded, 16)
                        with sp.Else():
                            wait_alone(sp, mid_loaded, G * 16 + 16, sp_passed)
                            sp.sem_inc(mid_loaded, 16)
                        with sp.If(tail > 0):
                            for j in range(FAR):
                                load(1, j % TILES, NEAR + 1 + NEAR * (j // TILES), far_loaded)
                                wait_alone(sp, far_used, G * FAR + (j + 1), sp_passed)
                        for q in range(1, TILES):
                            if q > 1:
                                wait_alone(sp, tile_mm, G * TILES + q + 1, sp_passed)
                            load(q, q, 0, T_loaded[q])
                groups(sp, order, body)
            sp.wait_ge(y_out, GROUPS // ORDERS + 2)
            sp.wait_ge(xf_saved, 16 * SLOTS)
            load_output(sp)

        @block.gpsimd
        def _(pool):
            x_tiles = x.rearrange("n (q i p) d -> (n q) p i d", i=TT, p=P)

            def load_xn(c, i):
                for part in range(2):
                    pool.dma_start(xn[i][part][:, :, :].bitcast(F32), xnT_hbm[part, bass.ds(c, 1)].rearrange("c p k t -> (c p) k t")).then_inc(xn_loaded[i], 16)

            def load_xb(it, first=False):
                if not first:
                    wait_alone(pool, xf_saved, it * 16, pool_passed)
                pool.dma_start(xb[:, :, :], x_tiles[bass.ds(it, 1)].rearrange("c p i d -> (c p) i d")).then_inc(xb_loaded, 16)
                wait_alone(pool, xb_loaded, it * 16 + 16, pool_passed)
                pool.tensor_tensor(xb[:, :, :], xb[:, :, :], bo_row[:, :].unsqueeze(1).broadcast_to([P, TT, D]), ALU.add).then_inc(xb_biased, 1)

            def save_xf(it):
                wait_alone(pool, xf_ready, it + 2, pool_passed)
                pool.dma_start(xf_hbm[bass.ds(it, 1)].rearrange("c p i d -> (c p) i d"), xb[:, :, :]).then_inc(xf_saved, 16)

            load_xn(0, 0)
            pool.dma_start(bo_row[:, :], bass.AP(out_b.tensor, 0, [[0, P], [1, D]])).then_inc(bo_in, 16)
            load_xn(1, 1)
            pool.wait_ge(bo_in, 16)
            load_xb(0, True)
            with pool.Fori(0, NCH // 2 - 1) as pair:
                for i in range(2):
                    c = pair * 2 + (1 + i)
                    wait_alone(pool, fc_mm, c * HT + HT, pool_passed)
                    load_xn(c + 1, i)
                    save_xf(c - 1)
                    load_xb(c)
            save_xf(NCH - 2)
            load_xb(NCH - 1)
            save_xf(NCH - 1)

        @block.vector
        def _(dve):
            dve.wait_ge(gc2_saved, 16 * NCH + 16)
            dve.sem_inc(y_out, 2)
            dve.sem_inc(r_split, 2)

            def finish(it):
                dve.wait_ge(proj_mm, it * HT + HT + 2)
                dve.tensor_tensor(pp[:, :, :], pp[:, :, :], srow[:, :].unsqueeze(1).broadcast_to([P, TT, D]), ALU.mult).then_inc(scaled, 1)
                dve.wait_ge(scaled, it + 1)
                dve.wait_ge(xb_biased, it + 1)
                dve.tensor_tensor(xb[:, :, :], pp[:, :, :], xb[:, :, :], ALU.add).then_inc(xf_ready, 1)

            def body(m, it, order):
                for g in range(GPI):
                    for j in range(2):
                        uu = it * HT + (2 * g + j)
                        dve.wait_ge(relu_done, uu + 3)
                        dve.tensor_tensor(r[j][:, :], r[j][:, :], r[j][:, :], ALU.mult).then_inc(sq_done, 1)
                        dve.wait_ge(r_hi_done, uu + 1)
                        dve.tensor_tensor(r_lo[j][:, :], r[j][:, :], r_hi[j][:, :].bitcast(F32), ALU.subtract).then_inc(r_split, 1)
                    G = it * GPI + g
                    c0 = m * (GPI * GC) + g * GC
                    out = V[:, bass.ds(c0, GC)].rearrange("p c n a -> p (c n a)")
                    y = py[g % 2][:, :, :, :].rearrange("p c n a -> p (c n a)")
                    dve.wait_ge(tile_mm, G * TILES + 2 * TILES)
                    if order == 0:
                        dve.tensor_tensor(out, y, GC1[:, bass.ds(c0, GC)].rearrange("p c n a -> p (c n a)"), ALU.mult).then_inc(y_out, 1)
                    else:
                        dve.tensor_copy(out, y).then_inc(y_out, 1)

                finish(it)

            for order in range(ORDERS):
                groups(dve, order, lambda m, it, i: body(m, it, order))

        @block.scalar
        def _(act):
            for i, (dst, src) in enumerate(((wfc[0], fc_hi), (wfc[1], fc_lo), (wproj, proj_t))):
                act.dma_start(dst[:, :, :].bitcast(F32), src).then_inc(w_in[i], 16)
            act.sem_inc(relu_done, 2)
            with act.Fori(0, NCH) as it:
                for m in range(HT):
                    uu, j = it * HT + m, m % 2
                    act.wait_ge(fc_mm, uu + HT + 1)
                    act.wait_ge(r_split, uu + 1)
                    act.activation(r[j][:, :], pf[j][:, :], ACT.Relu).then_inc(relu_done, 1)
                    act.wait_ge(sq_done, uu + 1)
                    act.wait_ge(proj_mm, uu + 1)
                    act.activation(r_hi[j][:, :], r[j][:, :], ACT.Copy).then_inc(r_hi_done, 1)

        @block.tensor
        def _(pe):
            pe.sem_inc(fc_mm, HT)
            pe.sem_inc(proj_mm, 2)
            pe.sem_inc(xf_ready, 1)
            tail = pe.value_load(flag[0:1, 0:1], min_val=0, max_val=1)

            def fc(it, m, i):
                if m == 0:
                    pe.wait_ge(w_in[0], 16)
                    pe.wait_ge(w_in[1], 16)
                    pe.wait_ge(xn_loaded[i], (it - i) * 16 + 32)
                pe.wait_ge(relu_done, it * HT + (m + 1))
                ws = slice(m * P, (m + 1) * P)
                for k in range(KT):
                    last = split_mm(pe, pf[m % 2][:, :], (wfc[0][:, k, ws], wfc[1][:, k, ws]),
                                    (xn[i][0][:, k, :], xn[i][1][:, k, :]), k == 0, k == KT - 1)
                last.then_inc(fc_mm, 1)

            def proj(it, m):
                pe.wait_ge(r_split, it * HT + (m + 3))
                if m == 0:
                    pe.wait_ge(w_in[2], 16)
                    pe.wait_ge(xf_ready, it + 1)
                for i in range(TT):
                    for n, part in enumerate((r_hi, r_lo)):
                        last = pe.matmul(pp[:, i, :], part[m % 2][:, i * P:(i + 1) * P], wproj[:, m, :],
                                         start=(m == 0 and n == 0 and i % 2 == 0), stop=(m == HT - 1 and n == 1),
                                         skip_group_check=True)
                last.then_inc(proj_mm, 1)

            for order in range(ORDERS):
                def body(m, it, i):
                    for g in range(GPI):
                        G = it * GPI + g
                        y = py[g % 2]

                        def conv(tile, c, A0, count):
                            for A in range(A0, A0 + count):
                                j = A - A0 if order else A0 + count - 1 - A
                                last = pe.matmul(y[:, c, :, A:NA], tile[:, j * P:(j + 1) * P],
                                                 V[:, bass.ds(m * (GPI * GC) + (g * GC + c), 1), :, 0:NA - A]
                                                 .rearrange("p c n a -> p (c n) a"),
                                                 start=(c == 0 and A == 0), stop=True, skip_group_check=True)
                            return last

                        def near(q):
                            pe.wait_ge(T_loaded[q], G * 16 + 16)
                            for c in range(TC):
                                last = conv(T[:, q, c, :], q * TC + c, 0, NEAR)
                            last.then_inc(tile_mm, 1)

                        pe.wait_ge(y_out, G + 1)
                        near(0)
                        middle = pe.value_load(flag[0:1, bass.ds(G + 1, 1)], min_val=0, max_val=2 ** TILES - 1)
                        with pe.If(middle > 0):
                            pe.wait_ge(mid_loaded, G * 16 + 32)
                            for q in range(TILES):
                                with pe.If(middle // 2 ** q % 2 > 0):
                                    for c in range(q * TC, q * TC + TC):
                                        conv(Tmid[:, c, :], c, NEAR, 1)
                        with pe.If(tail > 0):
                            for j in range(FAR):
                                pe.wait_ge(far_loaded, G * (16 * FAR) + 16 * (j + 1))
                                for c in range(TC):
                                    last = conv(T[:, 1, c, :], (j % TILES) * TC + c, NEAR + 1 + NEAR * (j // TILES), NEAR)
                                last.then_inc(far_used, 1)
                        fc(it, 2 * g, i)
                        near(1)
                        if g > 0:
                            proj(it, 2 * g - 1)
                        fc(it, 2 * g + 1, i)
                        near(2)
                        near(3)
                        proj(it, 2 * g)
                    proj(it, HT - 1)
                groups(pe, order, body)


def output_stage(nc, out, load_gates, load_sum, xf_saved, ident, V, gc2, xf, wo, gc2_loaded, xf_loaded, wo_in):
    with ExitStack() as ctx:
        def sb(name, shape, dt=F32):
            return ctx.enter_context(nc.sbuf_tensor(name, shape, dt))

        def sem(name):
            return ctx.enter_context(nc.semaphore(name))

        ys = [sb(f"ys{i}", [P, TT, D]) for i in range(2)]
        yg = [sb(f"yg{i}", [P, KT, CH]) for i in range(2)]
        ygs = [[sb(f"yg_{part}{i}", [P, KT, CH], F32R) for part in ("hi", "lo")] for i in range(2)]
        wos = [sb("wo_hi", [P, KT, D], F32R), sb("wo_lo", [P, KT, D], F32R)]
        pT = [ctx.enter_context(nc.psum_tensor(f"pyT{i}", [P, KT, CH], F32)) for i in range(2)]
        po = [ctx.enter_context(nc.psum_tensor(f"po{i}", [P, TT, D], F32)) for i in range(2)]

        sp_passed, pool_passed = sem("sp_passed"), sem("pool_passed")
        wo_hi_ready, wo_split = sem("wo_hi_ready"), sem("wo_split")
        ys_ready = sem("ys_ready")
        yT_mm = sem("yT_mm")
        yg_ready = sem("yg_ready")
        yg_hi_done, yg_split = sem("yg_hi_done"), sem("yg_split")
        out_mm = sem("out_mm")
        out_ready = sem("out_ready")
        out_saved = [sem(f"out_saved{i}") for i in range(SLOTS)]
        block = ctx.enter_context(nc.Block())

        def chunks(eng, body, lead):
            for c in range(lead):
                body(c, c)
            with eng.Fori(0, NCH // SLOTS - 1) as m:
                for j in range(SLOTS):
                    body(m * SLOTS + (lead + j), (lead + j) % SLOTS)
            for c in range(NCH - SLOTS + lead, NCH):
                body(c, c % SLOTS)

        out_tiles = out.rearrange("n (q i p) d -> (n q) p i d", i=TT, p=P)

        @block.sync
        def _(sp):
            sp.wait_ge(xf_saved, 16 * NCH)

            def gates(c, j):
                wait_alone(sp, yg_ready, c - SLOTS + 3, sp_passed)
                load_gates(sp, c, j)

            def sums(c, j):
                wait_alone(sp, out_saved[j], (c - j) * (16 // SLOTS), sp_passed)
                load_sum(sp, c, j)

            for c in (SLOTS, SLOTS + 1):
                gates(c, c % SLOTS)
            with sp.Fori(1, NCH // SLOTS - 1) as m:
                for j in range(SLOTS):
                    gates(m * SLOTS + (j + 2), (j + 2) % SLOTS)
                    sums(m * SLOTS + j, j)
            for c in range(NCH - SLOTS, NCH):
                if c + 2 < NCH:
                    gates(c + 2, (c + 2) % SLOTS)
                sums(c, c % SLOTS)

        @block.gpsimd
        def _(pool):
            with pool.Fori(0, NCH // SLOTS) as m:
                for j in range(SLOTS):
                    c = m * SLOTS + j
                    wait_alone(pool, out_ready, c + 3, pool_passed)
                    pool.dma_start(out_tiles[bass.ds(c, 1)].rearrange("c p i d -> (c p) i d"), xf[j]).then_inc(out_saved[j], 16)
            for j in range(SLOTS):
                pool.wait_ge(out_saved[j], 16 * NCH // SLOTS)

        @block.scalar
        def _(act):
            def stage(n, k):
                act.activation(ys[k % 2][:, :, :].rearrange("p i c -> p c i"),
                               V[:, :, bass.ds(n, 1), TT * k:TT * k + TT].rearrange("p c n a -> p c (n a)"),
                               ACT.Copy).then_inc(ys_ready, 1)

            def high(c, i):
                act.wait_ge(yg_ready, c + 3)
                act.wait_ge(out_mm, c + 1)
                act.activation(ygs[i][0][:, :, :], yg[i][:, :, :], ACT.Copy).then_inc(yg_hi_done, 1)

            stage(0, 0)
            stage(0, 1)
            act.wait_ge(wo_in, 16)
            act.activation(wos[0][:, :, :], wo, ACT.Copy).then_inc(wo_hi_ready, 1)
            with act.Fori(0, B - 1) as n:
                for k in range(CPB):
                    c = n * CPB + k
                    act.wait_ge(yT_mm, c + 1)
                    stage(n + (k + 2) // CPB, (k + 2) % CPB)
                    high(c, k % 2)
            for k in range(CPB):
                c = NCH - CPB + k
                if c + 2 < NCH:
                    act.wait_ge(yT_mm, c + 1)
                    stage(B - 1, k + 2)
                high(c, k % 2)

        @block.vector
        def _(dve):
            dve.sem_inc(yg_ready, 2)
            dve.sem_inc(out_ready, 2)
            dve.sem_inc(out_mm, 2)

            def gated(c, j):
                dve.wait_ge(yT_mm, c + 1)
                dve.wait_ge(gc2_loaded[j], (c - j) * (16 // SLOTS) + 16)
                dve.tensor_tensor(yg[j % 2][:, :, :], pT[j % 2][:, :, :], gc2[j], ALU.mult).then_inc(yg_ready, 1)

            def low(c, j):
                i = j % 2
                dve.wait_ge(yg_hi_done, c + 1)
                dve.tensor_tensor(ygs[i][1][:, :, :], yg[i][:, :, :], ygs[i][0][:, :, :].bitcast(F32), ALU.subtract).then_inc(yg_split, 1)

            def summed(c, j):
                dve.wait_ge(out_mm, c + 3)
                dve.wait_ge(xf_loaded[j], (c - j) * (16 // SLOTS) + 16)
                dve.tensor_tensor(xf[j], po[j % 2][:, :, :], xf[j], ALU.add).then_inc(out_ready, 1)

            def body(c, j):
                gated(c, j)
                if not isinstance(c, int) or c >= 2:
                    summed(c - 2, (j + 2) % SLOTS)
                low(c, j)
                if isinstance(c, int) and c == 0:
                    dve.wait_ge(wo_hi_ready, 1)
                    dve.tensor_tensor(wos[1][:, :, :], wo, wos[0][:, :, :].bitcast(F32), ALU.subtract).then_inc(wo_split, 1)

            chunks(dve, body, 2)
            for c in (NCH - 2, NCH - 1):
                summed(c, c % SLOTS)

        @block.tensor
        def _(pe):
            def transposed(c, j):
                i = j % 2
                pe.wait_ge(ys_ready, c + 1)
                pe.wait_ge(yg_ready, c + 1)
                for k in range(KT):
                    for t in range(TT):
                        last = pe.transpose(pT[i][:, k, t * P:(t + 1) * P], ys[i][:, t, k * P:(k + 1) * P], ident[:, :])
                last.then_inc(yT_mm, 1)

            def projected(c, j):
                i = j % 2
                pe.wait_ge(yg_split, c + 1)
                pe.wait_ge(out_ready, c + 1)
                for t in range(TT):
                    ts = slice(t * P, (t + 1) * P)
                    for k in range(KT):
                        last = split_mm(pe, po[i][:, t, :], (ygs[i][0][:, k, ts], ygs[i][1][:, k, ts]),
                                        (wos[0][:, k, :], wos[1][:, k, :]), k == 0, k == KT - 1)
                last.then_inc(out_mm, 1)

            def body(c, j):
                transposed(c, j)
                if not isinstance(c, int) or c >= 1:
                    projected(c - 1, (j + SLOTS - 1) % SLOTS)

            transposed(0, 0)
            pe.wait_ge(wo_split, 1)
            transposed(1, 1)
            projected(0, 0)
            with pe.Fori(0, NCH // SLOTS - 1) as m:
                for j in range(SLOTS):
                    body(m * SLOTS + (2 + j), (2 + j) % SLOTS)
            for c in (NCH - 2, NCH - 1):
                body(c, c % SLOTS)
            projected(NCH - 1, (NCH - 1) % SLOTS)


def conv_ffn_kernel(nc, x, in_w, in_b, out_w, out_b, freqs, w1, b1, w2, b2, w3, b3, decay, conv_w, conv_b,
                    gate_w, gate_b, fast_b, w_fc, w_proj, u, v, gate, out):
    filters = nc.dram_tensor("filters", [ORDERS * D, PADDED], F32).ap()
    fc_hi = nc.dram_tensor("fc_hi", [P, KT, HID], F32).ap()
    fc_lo = nc.dram_tensor("fc_lo", [P, KT, HID], F32).ap()
    proj_t = nc.dram_tensor("proj_t", [P, HT, D], F32).ap()
    xnT_hbm = nc.dram_tensor("xnT_hbm", [2, NCH, P, KT, CH], F32).ap()
    gc2_hbm = nc.dram_tensor("gc2_hbm", [NCH, P, KT, CH], F32).ap()
    xf_hbm = nc.dram_tensor("xf_hbm", [NCH, P, TT, D], F32).ap()

    with ExitStack() as ctx:
        def sb(name, shape, dt=F32):
            return ctx.enter_context(nc.sbuf_tensor(name, shape, dt))

        ident = sb("ident", [P, P])
        bv_row, srow = sb("bv_row", [P, D]), sb("srow", [P, D])
        flag = sb("flag", [1, 1 + GROUPS], I32)
        eps, half = sb("eps", [P, TT]), sb("half", [P, TT])
        V = sb("V", [P, D, B, NA])
        GC1 = sb("GC1", [P, D, B, NA])
        gc2_saved = ctx.enter_context(nc.semaphore("gc2_saved"))
        with ExitStack() as weights:
            Win = [weights.enter_context(nc.sbuf_tensor(f"win_{part}", [P, KT, 3 * D], F32R)) for part in ("hi", "lo")]
            Wgate = [weights.enter_context(nc.sbuf_tensor(f"wgate_{part}", [P, ORDERS * KT, D], F32R)) for part in ("hi", "lo")]
            hbm = (in_w, in_b, out_b, freqs, w1, b1, w2, b2, w3, b3, decay, gate_w, fast_b, w_fc, w_proj, u, v, gate,
                   filters, fc_hi, fc_lo, proj_t)
            xt = [weights.enter_context(nc.sbuf_tensor(f"xt{i}", [P, TT, D], F32)) for i in range(2)]
            taps = weights.enter_context(nc.sbuf_tensor("taps", [P, 4, 6], F32))
            norms = weights.enter_context(nc.sbuf_tensor("norms", [P, TT, 11], F32))
            x_loaded = [weights.enter_context(nc.semaphore(f"x_loaded{i}")) for i in range(2)]
            stat_done, aggr_done, rstd_step, xn_ready = (weights.enter_context(nc.semaphore(n)) for n in ("stat_done", "aggr_done", "rstd_step", "xn_ready"))
            dve_passed, pool_passed = (weights.enter_context(nc.semaphore(n)) for n in ("dve_norm_passed", "pool_norm_passed"))
            norm = norm_steps(xt, norms, eps, half, x_loaded, stat_done, aggr_done, rstd_step, xn_ready, dve_passed, pool_passed)
            bias_in = weights.enter_context(nc.semaphore("bias_in"))

            def load_first(sp):
                for i in range(2):
                    sp.dma_start(xt[i][:, :, :], x_tile(x, i)).then_inc(x_loaded[i], 16)
                sp.dma_start(taps[:, :, 3], in_b[D:3 * D].rearrange("(c p) -> p c", p=P)).then_inc(bias_in, 16)
                for o in range(ORDERS):
                    cs = slice(KT * o, KT * o + KT)
                    for k in range(3):
                        sp.dma_start(taps[:, cs, k], conv_w[o, k, 0, :].rearrange("(c p) -> p c", p=P)).then_inc(bias_in, 16)
                    sp.dma_start(taps[:, cs, 4], conv_b[o, :].rearrange("(c p) -> p c", p=P)).then_inc(bias_in, 16)
                    sp.dma_start(taps[:, cs, 5], gate_b[o, :].rearrange("(c p) -> p c", p=P)).then_inc(bias_in, 16)

            setup_stage(nc, hbm, ident, bv_row, srow, flag, V, GC1, Win, Wgate, eps, half, load_first, norm)
            project_stage(nc, x, xnT_hbm, gc2_hbm, ident, bv_row, V, GC1, Win, Wgate, eps, xt, x_loaded, xn_ready, norm, taps, bias_in, gc2_saved)
        Gf = GC1[:, :, :, :].rearrange("p c n a -> p (c n a)")
        slot = KT * CH
        gc2 = [Gf[:, j * slot:(j + 1) * slot].rearrange("p (k t) -> p k t", k=KT) for j in range(SLOTS)]
        xf = [Gf[:, (SLOTS + j) * slot:(SLOTS + j + 1) * slot].rearrange("p (i d) -> p i d", i=TT) for j in range(SLOTS)]
        wo = Gf[:, 2 * SLOTS * slot:2 * SLOTS * slot + KT * D].rearrange("p (k c) -> p k c", k=KT)
        gc2_loaded, xf_loaded = ([ctx.enter_context(nc.semaphore(f"{n}{j}")) for j in range(SLOTS)] for n in ("gc2_loaded", "xf_loaded"))
        wo_in = ctx.enter_context(nc.semaphore("wo_in"))
        xf_saved = ctx.enter_context(nc.semaphore("xf_saved"))

        def load_gates(sp, c, j):
            sp.dma_start(gc2[j], gc2_hbm[bass.ds(c, 1)].rearrange("c p k t -> (c p) k t")).then_inc(gc2_loaded[j], 16)

        def load_sum(sp, c, j):
            sp.dma_start(xf[j], xf_hbm[bass.ds(c, 1)].rearrange("c p i d -> (c p) i d")).then_inc(xf_loaded[j], 16)

        def load_output(sp):
            sp.wait_ge(gc2_saved, 16 * NCH + 16)
            sp.dma_start(wo, out_w.rearrange("(k p) c -> p k c", p=P)).then_inc(wo_in, 16)
            for j in range(SLOTS):
                load_gates(sp, j, j)
                load_sum(sp, j, j)

        mix_stage(nc, load_output, xf_saved, gc2_saved, x, filters, fc_hi, fc_lo, proj_t, xnT_hbm, xf_hbm, out_b, srow, flag, V, GC1)
        output_stage(nc, out, load_gates, load_sum, xf_saved, ident, V, gc2, xf, wo, gc2_loaded, xf_loaded, wo_in)


_INS = ["attn_x", "attn_in_proj_w", "attn_in_proj_b", "attn_out_proj_w", "attn_out_proj_b", "attn_freqs",
        "attn_mlp_w1", "attn_mlp_b1", "attn_mlp_w2", "attn_mlp_b2", "attn_mlp_w3", "attn_mlp_b3", "attn_decay",
        "attn_conv_w", "attn_conv_b", "attn_gate_w", "attn_gate_b", "ffn_fast_b", "ffn_w_fc", "ffn_w_proj",
        "ffn_u", "ffn_v", "ffn_gate"]


def kernel(**inputs):
    import numpy as _np
    import concourse.bacc as _bacc
    from concourse import mybir as _mybir
    from concourse.bass_utils import run_bass_kernel_spmd as _run

    nc = _bacc.Bacc("TRN2", target_bir_lowering=False, num_devices=1)
    arrays, args = {}, []
    for name in _INS:
        a = _np.ascontiguousarray(inputs["L0_" + name])
        arrays[f"in_{name}"] = a
        args.append(nc.dram_tensor(f"in_{name}", a.shape, _mybir.dt.from_np(a.dtype), kind="ExternalInput").ap())
    args.append(nc.dram_tensor("out_0", (B, L, D), F32, kind="ExternalOutput").ap())
    conv_ffn_kernel(nc, *args)
    r = _run(nc, [arrays], core_ids=[0])
    return r.results[0]["out_0"]
```
